# Optimizing a Trainium2 kernel written in Bass

```python
import numpy as np
import jax
import jax.numpy as jnp

def _softmax(x, axis=-1):
    return jax.nn.softmax(x, axis=axis)

def _gelu(x):
    return jax.nn.gelu(x, approximate=True)

def _silu(x):
    return jax.nn.silu(x)

def _sigmoid(x):
    return jax.nn.sigmoid(x)

def _layernorm(x, axis=-1, eps=1e-05):
    m = jnp.mean(x, axis=axis, keepdims=True)
    v = jnp.var(x, axis=axis, keepdims=True)
    return (x - m) / jnp.sqrt(v + eps)

def _scatter_add(tgt, idx, src, axis=0):
    return tgt.at[idx].add(src)

def _segment_sum(src, seg, n):
    return jax.ops.segment_sum(src, seg, n)
kernel_name = 'mk_adj_ffn_d2_adj_r2_eb9c73'

def setup_inputs(seed: int=0):
    np.random.seed(seed)
    _w = jnp.asarray

    def _rec_inputs():
        import jax
        import jax.numpy as jnp
        _gk = jax.random.key(seed)
        x = -0.0005207 + 1.001 * jax.random.normal(jax.random.fold_in(_gk, 1), (4096, 128), jnp.float32)
        _a = jax.random.bernoulli(jax.random.fold_in(_gk, 2), 0.000976562, (4096, 4096))
        _a = jnp.logical_or(_a, jnp.eye(4096, dtype=bool))
        _af = _a.astype(jnp.float32)
        _af = _af * jax.random.uniform(jax.random.fold_in(_gk, 3), (4096, 4096), jnp.float32, 0.05, 1)
        adj = _af
        return (x, adj)
    x, adj = _rec_inputs()

    def _L0_gnn_setup():
        import jax, jax.numpy as jnp
        import numpy as np
        key = jax.random.key(seed)
        k1, k2, k3, k4 = jax.random.split(key, 4)
        N, F_in, F_out = (4096, 128, 128)
        x = jax.random.normal(k1, (N, F_in), dtype=jnp.float32)
        adj = jax.random.uniform(k2, (N, N), dtype=jnp.float32)
        lim = 1.0 / np.sqrt(F_in)
        W = jax.random.uniform(k3, (F_out, F_in), dtype=jnp.float32, minval=-lim, maxval=lim)
        b = jax.random.uniform(k4, (F_out,), dtype=jnp.float32, minval=-lim, maxval=lim)
        return {'x': x, 'adj': adj, 'W': W, 'b': b}
    _L0_gnn_all = _L0_gnn_setup()
    _L0_gnn_in = {k: v for k, v in _L0_gnn_all.items() if k in ('W', 'b')}
    del _L0_gnn_all

    def _L0_ffn_setup():
        import jax, jax.numpy as jnp
        import numpy as np
        D_MODEL = 128
        D_STATE = 64
        D_CONV = 4
        EXPAND = 2
        HEADDIM = 64
        D_INNER = EXPAND * D_MODEL
        NHEADS = D_INNER // HEADDIM
        CONV_DIM = D_INNER + 2 * D_STATE
        D_IN_PROJ = 2 * D_INNER + 2 * D_STATE + NHEADS
        CHUNK = 128
        EPS = 1e-05

        def segsum(a):
            T = a.shape[-1]
            cs = jnp.cumsum(a, axis=-1)
            ss = cs[..., :, None] - cs[..., None, :]
            mask = jnp.tril(jnp.ones((T, T), dtype=bool))
            return jnp.where(mask, ss, -jnp.inf)

        def mamba2_block(x, W_in, conv_w, conv_b, dt_bias, A_log, D, norm_w, W_out, W_lin, b_lin):
            Bsz, L, _ = x.shape
            zxbcdt = x @ W_in
            z, xBC, dt = jnp.split(zxbcdt, [D_INNER, D_INNER + CONV_DIM], axis=-1)
            xp = jnp.pad(xBC, ((0, 0), (D_CONV - 1, 0), (0, 0)))
            conv = conv_b + sum((xp[:, k:k + L, :] * conv_w[:, k] for k in range(D_CONV)))
            xBC = jax.nn.silu(conv)
            xh, Bmat, Cmat = jnp.split(xBC, [D_INNER, D_INNER + D_STATE], axis=-1)
            dt = jax.nn.softplus(dt + dt_bias)
            A = -jnp.exp(A_log)
            nc = L // CHUNK
            xh = xh.reshape(Bsz, nc, CHUNK, NHEADS, HEADDIM)
            Bc = Bmat.reshape(Bsz, nc, CHUNK, D_STATE)
            Cc = Cmat.reshape(Bsz, nc, CHUNK, D_STATE)
            dtc = dt.reshape(Bsz, nc, CHUNK, NHEADS)
            dA = jnp.einsum('bclh,h->bhcl', dtc, A)
            A_cum = jnp.cumsum(dA, axis=-1)
            Lmat = jnp.exp(segsum(dA))
            xdt = xh * dtc[..., None]
            Y_diag = jnp.einsum('bcln,bcsn,bhcls,bcshp->bclhp', Cc, Bc, Lmat, xdt)
            decay_states = jnp.exp(A_cum[..., -1:] - A_cum)
            states = jnp.einsum('bcln,bhcl,bclhp->bchpn', Bc, decay_states, xdt)
            chunk_decay = jnp.exp(A_cum[..., -1])

            def step(h, inp):
                s, d = inp
                return (h * d[..., None, None] + s, h)
            _, prevs = jax.lax.scan(step, jnp.zeros_like(states[:, 0]), (jnp.moveaxis(states, 1, 0), jnp.moveaxis(chunk_decay, 2, 0)))
            prevs = jnp.moveaxis(prevs, 0, 1)
            Y_off = jnp.einsum('bcln,bchpn,bhcl->bclhp', Cc, prevs, jnp.exp(A_cum))
            Y = (Y_diag + Y_off + xh * D[:, None]).reshape(Bsz, L, D_INNER)
            Y = Y * jax.nn.silu(z)
            Y = Y * jax.lax.rsqrt(jnp.mean(Y * Y, axis=-1, keepdims=True) + EPS) * norm_w
            out = Y @ W_out
            return out @ W_lin + b_lin
        key = jax.random.key(seed)
        ks = jax.random.split(key, 12)
        B, L = (8, 2048)

        def gauss(k, shape, scale):
            return jax.random.normal(k, shape, dtype=jnp.float32) * scale
        return {'x': gauss(ks[0], (B, L, D_MODEL), 1.0), 'W_in': gauss(ks[1], (D_MODEL, D_IN_PROJ), D_MODEL ** (-0.5)), 'conv_w': gauss(ks[2], (CONV_DIM, D_CONV), 0.3), 'conv_b': gauss(ks[3], (CONV_DIM,), 0.1), 'dt_bias': jax.random.uniform(ks[4], (NHEADS,), minval=-4.0, maxval=-1.0), 'A_log': jnp.log(jax.random.uniform(ks[5], (NHEADS,), minval=1.0, maxval=16.0)), 'D': jnp.ones((NHEADS,), jnp.float32), 'norm_w': jnp.ones((D_INNER,), jnp.float32), 'W_out': gauss(ks[6], (D_INNER, D_MODEL), D_INNER ** (-0.5)), 'W_lin': gauss(ks[7], (D_MODEL, D_MODEL), D_MODEL ** (-0.5)), 'b_lin': jnp.zeros((D_MODEL,), jnp.float32)}
    _L0_ffn_all = _L0_ffn_setup()
    _L0_ffn_in = {k: v for k, v in _L0_ffn_all.items() if k in ('W_in', 'conv_w', 'conv_b', 'dt_bias', 'A_log', 'D', 'norm_w', 'W_out', 'W_lin', 'b_lin')}
    del _L0_ffn_all

    def _L1_gnn_setup():
        import jax, jax.numpy as jnp
        import numpy as np
        N = 4096
        D = 128
        L = 3

        def _cxin_conv(x, a, eps, W, b):
            ax = a @ x
            h = ax + (1.0 + eps[0]) * ax
            for i in range(L):
                h = jax.nn.relu(h @ W[i].T + b[i])
            return h
        key = jax.random.key(seed)
        ks = jax.random.split(key, 8)
        s = 1.0 / np.sqrt(D)
        return {'x1': jax.random.normal(ks[0], (N, D), jnp.float32), 'x2': jax.random.normal(ks[1], (N, D), jnp.float32), 'G1': jax.random.uniform(ks[2], (N, N), jnp.float32), 'G2': jax.random.uniform(ks[3], (N, N), jnp.float32), 'eps1': jnp.zeros((1,), jnp.float32), 'eps2': jnp.zeros((1,), jnp.float32), 'W1': jax.random.normal(ks[4], (L, D, D), jnp.float32) * s, 'b1': jnp.zeros((L, D), jnp.float32), 'W2': jax.random.normal(ks[5], (L, D, D), jnp.float32) * s, 'b2': jnp.zeros((L, D), jnp.float32), 'Wm': jax.random.normal(ks[6], (D, 2 * D), jnp.float32) * (1.0 / np.sqrt(2 * D)), 'bm': jnp.zeros((D,), jnp.float32)}
    _L1_gnn_all = _L1_gnn_setup()
    _L1_gnn_in = {k: v for k, v in _L1_gnn_all.items() if k in ('x2', 'eps1', 'eps2', 'W1', 'b1', 'W2', 'b2', 'Wm', 'bm')}
    del _L1_gnn_all

    def _L1_ffn_setup():
        import jax, jax.numpy as jnp
        import numpy as np
        BN_EPS = 0.001

        def _bn(h, g, b, m, v):
            return g * (h - m) * jax.lax.rsqrt(v + BN_EPS) + b
        key = jax.random.key(seed)
        ks = jax.random.split(key, 8)
        B, F, Df = (128, 64, 128)
        E, H, D = (8, 128, 128)
        s1 = 1.0 / np.sqrt(Df)
        s2 = 1.0 / np.sqrt(H)
        return {'x': jax.random.normal(ks[0], (B, F, Df), jnp.float32), 'Wr': jax.random.normal(ks[1], (Df, E), jnp.float32) * s1, 'br': jnp.zeros((E,), jnp.float32), 'W1': jax.random.normal(ks[2], (E, Df, H), jnp.float32) * s1, 'b1': jnp.zeros((E, H), jnp.float32), 'g1': jnp.ones((E, H), jnp.float32), 'be1': jnp.zeros((E, H), jnp.float32), 'm1': jnp.zeros((E, H), jnp.float32), 'v1': jnp.ones((E, H), jnp.float32), 'W2': jax.random.normal(ks[3], (E, H, H), jnp.float32) * s2, 'b2': jnp.zeros((E, H), jnp.float32), 'g2': jnp.ones((E, H), jnp.float32), 'be2': jnp.zeros((E, H), jnp.float32), 'm2': jnp.zeros((E, H), jnp.float32), 'v2': jnp.ones((E, H), jnp.float32), 'Wo': jax.random.normal(ks[4], (E, H, D), jnp.float32) * s2, 'bo': jnp.zeros((E, D), jnp.float32)}
    _L1_ffn_all = _L1_ffn_setup()
    _L1_ffn_in = {k: v for k, v in _L1_ffn_all.items() if k in ('Wr', 'br', 'W1', 'b1', 'g1', 'be1', 'm1', 'v1', 'W2', 'b2', 'g2', 'be2', 'm2', 'v2', 'Wo', 'bo')}
    del _L1_ffn_all
    return {'x': x, 'adj': adj, 'L0_gnn_W': _L0_gnn_in['W'], 'L0_gnn_b': _L0_gnn_in['b'], 'L0_ffn_W_in': _L0_ffn_in['W_in'], 'L0_ffn_conv_w': _L0_ffn_in['conv_w'], 'L0_ffn_conv_b': _L0_ffn_in['conv_b'], 'L0_ffn_dt_bias': _L0_ffn_in['dt_bias'], 'L0_ffn_A_log': _L0_ffn_in['A_log'], 'L0_ffn_D': _L0_ffn_in['D'], 'L0_ffn_norm_w': _L0_ffn_in['norm_w'], 'L0_ffn_W_out': _L0_ffn_in['W_out'], 'L0_ffn_W_lin': _L0_ffn_in['W_lin'], 'L0_ffn_b_lin': _L0_ffn_in['b_lin'], 'L1_gnn_x2': _L1_gnn_in['x2'], 'L1_gnn_eps1': _L1_gnn_in['eps1'], 'L1_gnn_eps2': _L1_gnn_in['eps2'], 'L1_gnn_W1': _L1_gnn_in['W1'], 'L1_gnn_b1': _L1_gnn_in['b1'], 'L1_gnn_W2': _L1_gnn_in['W2'], 'L1_gnn_b2': _L1_gnn_in['b2'], 'L1_gnn_Wm': _L1_gnn_in['Wm'], 'L1_gnn_bm': _L1_gnn_in['bm'], 'L1_ffn_Wr': _L1_ffn_in['Wr'], 'L1_ffn_br': _L1_ffn_in['br'], 'L1_ffn_W1': _L1_ffn_in['W1'], 'L1_ffn_b1': _L1_ffn_in['b1'], 'L1_ffn_g1': _L1_ffn_in['g1'], 'L1_ffn_be1': _L1_ffn_in['be1'], 'L1_ffn_m1': _L1_ffn_in['m1'], 'L1_ffn_v1': _L1_ffn_in['v1'], 'L1_ffn_W2': _L1_ffn_in['W2'], 'L1_ffn_b2': _L1_ffn_in['b2'], 'L1_ffn_g2': _L1_ffn_in['g2'], 'L1_ffn_be2': _L1_ffn_in['be2'], 'L1_ffn_m2': _L1_ffn_in['m2'], 'L1_ffn_v2': _L1_ffn_in['v2'], 'L1_ffn_Wo': _L1_ffn_in['Wo'], 'L1_ffn_bo': _L1_ffn_in['bo']}

def reference(x, adj, L0_gnn_W, L0_gnn_b, L0_ffn_W_in, L0_ffn_conv_w, L0_ffn_conv_b, L0_ffn_dt_bias, L0_ffn_A_log, L0_ffn_D, L0_ffn_norm_w, L0_ffn_W_out, L0_ffn_W_lin, L0_ffn_b_lin, L1_gnn_x2, L1_gnn_eps1, L1_gnn_eps2, L1_gnn_W1, L1_gnn_b1, L1_gnn_W2, L1_gnn_b2, L1_gnn_Wm, L1_gnn_bm, L1_ffn_Wr, L1_ffn_br, L1_ffn_W1, L1_ffn_b1, L1_ffn_g1, L1_ffn_be1, L1_ffn_m1, L1_ffn_v1, L1_ffn_W2, L1_ffn_b2, L1_ffn_g2, L1_ffn_be2, L1_ffn_m2, L1_ffn_v2, L1_ffn_Wo, L1_ffn_bo):
    import jax
    import jax.numpy as jnp

    def _L0_gnn_ref(x, adj, W, b):
        import jax, jax.numpy as jnp
        import numpy as np
        N = adj.shape[0]
        adj = adj + jnp.eye(N, dtype=adj.dtype)
        deg = adj.sum(axis=1)
        deg_inv_sqrt = deg ** (-0.5)
        deg_inv_sqrt = jnp.where(jnp.isinf(deg_inv_sqrt), 0.0, deg_inv_sqrt)
        adj_normalized = deg_inv_sqrt[:, None] * adj * deg_inv_sqrt[None, :]
        support = x @ W.T + b
        return adj_normalized @ support

    def _L0_ffn_ref(x, W_in, conv_w, conv_b, dt_bias, A_log, D, norm_w, W_out, W_lin, b_lin):
        import jax, jax.numpy as jnp
        import numpy as np
        D_MODEL = 128
        D_STATE = 64
        D_CONV = 4
        EXPAND = 2
        HEADDIM = 64
        D_INNER = EXPAND * D_MODEL
        NHEADS = D_INNER // HEADDIM
        CONV_DIM = D_INNER + 2 * D_STATE
        D_IN_PROJ = 2 * D_INNER + 2 * D_STATE + NHEADS
        CHUNK = 128
        EPS = 1e-05

        def segsum(a):
            T = a.shape[-1]
            cs = jnp.cumsum(a, axis=-1)
            ss = cs[..., :, None] - cs[..., None, :]
            mask = jnp.tril(jnp.ones((T, T), dtype=bool))
            return jnp.where(mask, ss, -jnp.inf)

        def mamba2_block(x, W_in, conv_w, conv_b, dt_bias, A_log, D, norm_w, W_out, W_lin, b_lin):
            Bsz, L, _ = x.shape
            zxbcdt = x @ W_in
            z, xBC, dt = jnp.split(zxbcdt, [D_INNER, D_INNER + CONV_DIM], axis=-1)
            xp = jnp.pad(xBC, ((0, 0), (D_CONV - 1, 0), (0, 0)))
            conv = conv_b + sum((xp[:, k:k + L, :] * conv_w[:, k] for k in range(D_CONV)))
            xBC = jax.nn.silu(conv)
            xh, Bmat, Cmat = jnp.split(xBC, [D_INNER, D_INNER + D_STATE], axis=-1)
            dt = jax.nn.softplus(dt + dt_bias)
            A = -jnp.exp(A_log)
            nc = L // CHUNK
            xh = xh.reshape(Bsz, nc, CHUNK, NHEADS, HEADDIM)
            Bc = Bmat.reshape(Bsz, nc, CHUNK, D_STATE)
            Cc = Cmat.reshape(Bsz, nc, CHUNK, D_STATE)
            dtc = dt.reshape(Bsz, nc, CHUNK, NHEADS)
            dA = jnp.einsum('bclh,h->bhcl', dtc, A)
            A_cum = jnp.cumsum(dA, axis=-1)
            Lmat = jnp.exp(segsum(dA))
            xdt = xh * dtc[..., None]
            Y_diag = jnp.einsum('bcln,bcsn,bhcls,bcshp->bclhp', Cc, Bc, Lmat, xdt)
            decay_states = jnp.exp(A_cum[..., -1:] - A_cum)
            states = jnp.einsum('bcln,bhcl,bclhp->bchpn', Bc, decay_states, xdt)
            chunk_decay = jnp.exp(A_cum[..., -1])

            def step(h, inp):
                s, d = inp
                return (h * d[..., None, None] + s, h)
            _, prevs = jax.lax.scan(step, jnp.zeros_like(states[:, 0]), (jnp.moveaxis(states, 1, 0), jnp.moveaxis(chunk_decay, 2, 0)))
            prevs = jnp.moveaxis(prevs, 0, 1)
            Y_off = jnp.einsum('bcln,bchpn,bhcl->bclhp', Cc, prevs, jnp.exp(A_cum))
            Y = (Y_diag + Y_off + xh * D[:, None]).reshape(Bsz, L, D_INNER)
            Y = Y * jax.nn.silu(z)
            Y = Y * jax.lax.rsqrt(jnp.mean(Y * Y, axis=-1, keepdims=True) + EPS) * norm_w
            out = Y @ W_out
            return out @ W_lin + b_lin
        return mamba2_block(x, W_in, conv_w, conv_b, dt_bias, A_log, D, norm_w, W_out, W_lin, b_lin)

    def _L1_gnn_ref(x1, x2, G1, G2, eps1, eps2, W1, b1, W2, b2, Wm, bm):
        import jax, jax.numpy as jnp
        import numpy as np
        N = 4096
        D = 128
        L = 3

        def _cxin_conv(x, a, eps, W, b):
            ax = a @ x
            h = ax + (1.0 + eps[0]) * ax
            for i in range(L):
                h = jax.nn.relu(h @ W[i].T + b[i])
            return h
        out1 = _cxin_conv(x1, G1, eps1, W1, b1)
        out2 = _cxin_conv(x2, G2, eps2, W2, b2)
        merged = jnp.concatenate((out1, out2), axis=1)
        return merged @ Wm.T + bm

    def _L1_ffn_ref(x, Wr, br, W1, b1, g1, be1, m1, v1, W2, b2, g2, be2, m2, v2, Wo, bo):
        import jax, jax.numpy as jnp
        import numpy as np
        BN_EPS = 0.001

        def _bn(h, g, b, m, v):
            return g * (h - m) * jax.lax.rsqrt(v + BN_EPS) + b
        feat = jnp.mean(x, axis=0)
        w = jax.nn.softmax(feat @ Wr + br, axis=-1)
        h = jnp.einsum('bfd,edh->bfeh', x, W1) + b1
        h = jax.nn.relu(_bn(h, g1, be1, m1, v1))
        h = jnp.einsum('bfeh,ehk->bfek', h, W2) + b2
        h = jax.nn.relu(_bn(h, g2, be2, m2, v2))
        y = jnp.einsum('bfeh,ehd->bfed', h, Wo) + bo
        return jnp.einsum('bfed,fe->bfd', y, w)
    x = x + _L0_gnn_ref(_layernorm(x, axis=-1), adj, L0_gnn_W, L0_gnn_b)
    x = x + _L0_ffn_ref(_layernorm(x, axis=-1)[None], L0_ffn_W_in, L0_ffn_conv_w, L0_ffn_conv_b, L0_ffn_dt_bias, L0_ffn_A_log, L0_ffn_D, L0_ffn_norm_w, L0_ffn_W_out, L0_ffn_W_lin, L0_ffn_b_lin)[0]
    x = x + _L1_gnn_ref(_layernorm(x, axis=-1), L1_gnn_x2, adj, adj, L1_gnn_eps1, L1_gnn_eps2, L1_gnn_W1, L1_gnn_b1, L1_gnn_W2, L1_gnn_b2, L1_gnn_Wm, L1_gnn_bm)
    x = x + _L1_ffn_ref(_layernorm(x, axis=-1)[None], L1_ffn_Wr, L1_ffn_br, L1_ffn_W1, L1_ffn_b1, L1_ffn_g1, L1_ffn_be1, L1_ffn_m1, L1_ffn_v1, L1_ffn_W2, L1_ffn_b2, L1_ffn_g2, L1_ffn_be2, L1_ffn_m2, L1_ffn_v2, L1_ffn_Wo, L1_ffn_bo)[0]
    return x

_drawn_inputs = setup_inputs


def setup_inputs(seed=0):
    import zlib

    import numpy as np

    out = dict(_drawn_inputs(seed))
    spreads = {'L0_ffn_D': (1.0, 0.2),
     'L0_ffn_norm_w': (1.0, 0.2),
     'L0_ffn_b_lin': (0.0, 0.1),
     'L1_gnn_b1': (0.0, 0.1),
     'L1_gnn_b2': (0.0, 0.1),
     'L1_gnn_bm': (0.0, 0.1),
     'L1_ffn_br': (0.0, 0.8),
     'L1_ffn_b1': (0.0, 0.568),
     'L1_ffn_g1': (1.0, 0.584),
     'L1_ffn_be1': (0.0, 0.592),
     'L1_ffn_m1': (0.0, 0.564),
     'L1_ffn_v1': (1.0, 0.6),
     'L1_ffn_b2': (0.0, 0.407),
     'L1_ffn_g2': (1.0, 0.2),
     'L1_ffn_be2': (0.0, 0.452),
     'L1_ffn_m2': (0.0, 0.423),
     'L1_ffn_v2': (1.0, 0.6),
     'L1_ffn_bo': (0.0, 0.301)}
    factors = {'L0_ffn_A_log': 6.641}
    for name, (base, spread) in spreads.items():
        noise = np.random.default_rng([zlib.crc32(name.encode()), seed]).standard_normal(out[name].shape)
        drawn = base * np.exp(spread * noise) if base else spread * noise
        out[name] = jnp.asarray(drawn.astype(out[name].dtype))
    for name, factor in factors.items():
        out[name] = (out[name] * factor).astype(out[name].dtype)
    return out
```

```python
from contextlib import ExitStack

import concourse.bass as bass
from concourse import mybir

ALU = mybir.AluOpType
ACT = mybir.ActivationFunctionType
AX_X = mybir.AxisListType.X
F32 = mybir.dt.float32

T = 4096
D = 128
P = 128
NT = T // P
BT = 512
NB = T // BT
C = BT // P
G = 8
SLOTS = 4
GJ = NT // G
DI, DS, NH, HD = 256, 64, 4, 64
TAPS = 4
E = 8
LN_EPS, RMS_EPS, BN_EPS = 1e-5, 1e-5, 1e-3

_WIDTHS = [
    ("ident", P), ("upper", P), ("last", P), ("ones", P),
    ("g0_b", D), ("bm", D), ("b_lin", D), ("br", E),
    ("conv_w", 3 * TAPS), ("conv_b", 3), ("skip", 2), ("norm_w", 2), ("eps1", 1), ("eps2", 1),
    ("mlp1_b", 3), ("mlp2_b", 3),
    ("g1", E), ("be1", E), ("m1", E), ("v1", E), ("b1", E),
    ("g2", E), ("be2", E), ("m2", E), ("v2", E), ("b2", E),
    ("a_log", 1), ("dt_bias", 1), ("pick", NH * P), ("restart", BT), ("bo", D),
    ("g0_w", D), ("w_in", 2 * DI + 2 * DS + NH), ("w_out_t", DI), ("w_lin", D),
    ("mlp1_w", 3 * D), ("mlp2_w", 3 * D), ("wm", 2 * D), ("wr", E),
    ("ew1", E * D), ("ew2", E * D), ("ewo", E * D),
]
COL, _at = {}, 0
for _name, _w in _WIDTHS:
    COL[_name] = (_at, _at + _w)
    _at += _w
PARAMS = _at


def ts(i, n):
    return bass.ts(i, n)


def wait(eng, sem, value):
    if isinstance(value, int) and value <= 0:
        return
    eng.wait_ge(sem, value)


def build(nc, x_in, x2_in, adj_in, par_in, out):
    with ExitStack() as ctx:
        def sb(name, shape):
            return ctx.enter_context(nc.sbuf_tensor(name, shape, F32))

        def bank(name):
            return ctx.enter_context(nc.psum_tensor(name, [P, BT], F32))

        def sem(name):
            return ctx.enter_context(nc.semaphore(name))

        par = sb("par", [P, PARAMS])
        ring = sb("ring", [P, SLOTS, GJ, BT])
        x = sb("x", [P, NT, D])
        sup = sb("sup", [P, NT, D])
        feat = sb("feat", [P, NT, D])
        side = sb("side", [P, NT, D])
        dis = sb("dis", [P, NT])
        stats = sb("stats", [P, C, 6])
        mv = sb("mv", [P, C, 2])
        var = sb("var", [P, C])
        rstd = sb("rstd", [P, C])
        spare = sb("spare", [P, 64])
        neg_half = sb("neg_half", [P, 2 * E])
        xhat = sb("xhat", [P, C, D])
        xhat_t = sb("xhat_t", [P, BT])
        z_t = sb("z_t", [P, BT])
        work = sb("work", [P, 7, BT])
        part, pair, colsum = work[:, 0:4], work[:, 4:6], work[:, 6]
        wide = sb("wide", [P, 7, BT])
        deg = sb("deg", [P, C])
        dg = sb("dg", [P, 4, C])
        gain = sb("gain", [P, 2])
        hid = [wide[:, i] for i in range(3)]
        w_ol = sb("w_ol", [P, 2, D])
        skip_d = sb("skip_d", [P, 2, P])
        a_neg = sb("a_neg", [NH, 2])
        bn_s = sb("bn_s", [P, 2 * E])
        bn_f = sb("bn_f", [P, 2 * E])
        bn_t = sb("bn_t", [P, 3, 2 * E])
        xbc = [sb(f"xbc{k}", [P, TAPS - 1 + BT]) for k in range(3)]
        conv = [work[:, 2 * k:2 * k + 2] for k in range(3)]
        zs = wide[:, 0:2].rearrange("p a (b d) -> p (a b) d", b=2)
        xs = [wide[:, 2 + k] for k in range(2)]
        bs = wide[0:DS, 4]
        cs = wide[0:DS, 5]
        dtr = sb("dtr", [NH, 2, BT])
        acum = sb("acum", [NH, BT])
        cols = sb("cols", [P, 2, C, NH])
        dec = sb("dec", [P, 3, C * NH])
        dece = sb("dece", [P, 3, C * NH])
        decay = [sb(f"decay{i}", [P, NH, P]) for i in range(2)]
        g_m = [sb(f"g_m{i}", [P, P]) for i in range(2)]
        xt = [sb(f"xt{i}", [P, DI + DS]) for i in range(2)]
        xdt = [sb(f"xdt{i}", [P, DI]) for i in range(2)]
        xdd = [sb(f"xdd{i}", [P, DI]) for i in range(2)]
        y0 = [sb(f"y0{i}", [P, DI]) for i in range(2)]
        y = [sb(f"y{i}", [P, DI]) for i in range(2)]
        y2 = [sb(f"y2{i}", [P, DI]) for i in range(2)]
        ysq = sb("ysq", [P, DI])
        y_t = [sb(f"y_t{i}", [P, DI]) for i in range(2)]
        ssq = sb("ssq", [P, C])
        msq = sb("msq", [P, C])
        rms = sb("rms", [P, C])
        state = sb("state", [DS, DI])
        lg = sb("lg", [P, 3, C, E])
        red = sb("red", [P, 3, C])
        gate = sb("gate", [P, C, E])
        gate_t = sb("gate_t", [E, BT])
        h1 = [wide[:, 3 + i] for i in range(2)]
        h2 = [wide[:, 5 + i] for i in range(2)]

        acc_ps = bank("acc_ps")
        tr_ps = bank("tr_ps")
        b2, b3, b4, b5, b6, b7 = (bank(f"b{i}_ps") for i in range(2, 8))

        def pc(name, lo=0, hi=None, rows=P):
            a, b = COL[name]
            return par[0:rows, a + lo:(a + hi if hi is not None else b)]

        ident = pc("ident")

        par_loaded = sem("par_loaded")
        x_loaded = sem("x_loaded")
        x2_loaded = sem("x2_loaded")
        adj_loaded = [sem(f"adj_loaded{q}") for q in range(SLOTS)]
        adj_used = sem("adj_used")
        adj_summed = sem("adj_summed")
        out_stored = sem("out_stored")
        consts_set = sem("consts_set")
        prep_pe = sem("prep_pe")
        prep_dve = sem("prep_dve")
        prep_act = sem("prep_act")
        prep_pool = sem("prep_pool")
        ln_stats, ln_aggr, ln_var, ln_rstd, ln_norm = (sem(n) for n in ("ln_stats", "ln_aggr", "ln_var", "ln_rstd", "ln_norm"))
        names0 = "xt_ps deg_ps sup_ps mlp_ps mg_ps z_sb xt_sb h part colsum sup deg mg dis scaled".split()
        p0 = {n: sem("p0_" + n) for n in names0}
        names1 = ("z_sb zt_ps x1 xt_ps xt_sb proj_ps zp_ps xbc dtact dtexp dtln dtrow scan zs conv carry act cols_ps cols "
                  "end_ps dec dece xT_ps xT rb_ps esub earg ee gt_ps gm m xdt xdd y_ps y0 y y2 ssq rv rms yT_ps yT o_ps "
                  "x2 x1b st_ps stmul st").split()
        p1 = {n: sem("p1_" + n) for n in names1}
        names2 = ("z_sb mlp_ps h mg_ps xm x3 xt_ps xt_sb gl_ps lg mx sub ex sum rcp gate gt_ps gt_sb gb_ps gb "
                  "w1_ps h1 w2_ps h2 wo_ps acc").split()
        p2 = {n: sem("p2_" + n) for n in names2}

        holds = []

        def hold(engine):
            at = len(holds)
            holds.append(at)
            o = spare[:, at:at + 1]
            if engine is nc.gpsimd:
                engine.tensor_tensor(o, neg_half[:, 0:1], neg_half[:, 1:2], ALU.add)
            else:
                engine.tensor_copy(o, neg_half[:, 0:1])

        def strips_used(ph, b, q):
            return ((ph * NB) + b) * G + q + 1

        def strip_loaded(ph, b, q):
            return 16 * ((ph * NB + b) * (G // SLOTS) + q // SLOTS + 1)

        block = ctx.enter_context(nc.Block())

        @block.sync
        def _(sp):
            sp.dma_start(feat[:], x2_in.rearrange("(t p) d -> p t d", p=P)).then_inc(x2_loaded, 16)

            def load(ph, b):
                for q in range(G):
                    wait(sp, adj_used, strips_used(ph, b, q) - SLOTS)
                    if ph == 0:
                        wait(sp, adj_summed, G * b + q + 1 - SLOTS)
                    elif ph == 1 and isinstance(b, int):
                        wait(sp, adj_summed, min(G * NB + q + 1 - SLOTS, G * NB))
                    sp.dma_start(ring[:, q % SLOTS], adj_in[b, q]).then_inc(adj_loaded[q % SLOTS], 16)

            for ph in range(3):
                load(ph, 0)
                with sp.Fori(1, NB) as b:
                    load(ph, b)

        @block.tensor
        def _(pe):
            def mm(o, l, r, start=True, stop=True, **k):
                return nc.tensor.matmul(o, l, r, start=start, stop=stop, **k)

            def adjacency(ph, b, lo, hi, stationary, free_sem):
                for i in range(lo, hi):
                    q, j = divmod(i, GJ)
                    if i == 0:
                        wait(pe, free_sem, b)
                    if j == 0:
                        wait(pe, adj_loaded[q % SLOTS], strip_loaded(ph, b, q))
                    ins = mm(acc_ps[:], stationary[:, i, :], ring[:, q % SLOTS, j, :], start=(i == 0), stop=(i == NT - 1))
                    if j == GJ - 1:
                        ins.then_inc(adj_used, 1)

            def transposes(src, dst, n, done):
                for c in range(n):
                    ins = nc.tensor.transpose(dst[:, c * P:(c + 1) * P], src(c), ident)
                ins.then_inc(done, 1)

            pe.wait_ge(par_loaded, 16)
            for k in range(2):
                ins = mm(b2[:, k * P:(k + 1) * P], pc("w_out_t", k * P, (k + 1) * P), pc("w_lin"))
            ins.then_inc(prep_pe, 1)

            def iter0(b, here, before):
                if here:
                    wait(pe, ln_norm, 4 * (b + 1))
                    transposes(lambda c: xhat[:, c, :], tr_ps, C, p0["xt_ps"])
                if before:
                    wait(pe, p0["colsum"], 7 * b)
                    wait(pe, p0["deg"], b - 1)
                    for c in range(C):
                        ins = mm(b5[:, c:c + 1], colsum[:, c * P:(c + 1) * P], pc("ones", 0, 1))
                    ins.then_inc(p0["deg_ps"], 1)
                if here:
                    adjacency(0, b, 0, 8, feat, p0["z_sb"])
                    wait(pe, p0["xt_sb"], b + 1)
                    wait(pe, p0["sup"], b)
                    for c in range(C):
                        ins = mm(b3[:, c * D:(c + 1) * D], xhat_t[:, c * P:(c + 1) * P], pc("g0_w"))
                    ins.then_inc(p0["sup_ps"], 1)
                for l in range(3):
                    if before:
                        if l == 0:
                            wait(pe, p0["z_sb"], b)
                            wait(pe, p0["h"], 3 * (b - 1))
                        else:
                            wait(pe, p0["h"], 3 * (b - 1) + l)
                        mm(b2[:], pc("mlp2_w", l * D, (l + 1) * D), z_t[:] if l == 0 else hid[l - 1][:]).then_inc(p0["mlp_ps"], 1)
                    if here:
                        adjacency(0, b, 8 * l + 8, 8 * l + (16 if l < 2 else 12), feat, None)
                if before:
                    wait(pe, p0["h"], 3 * b)
                    wait(pe, p0["mg"], b - 1)
                    for c in range(C):
                        ins = mm(b4[:, c * D:(c + 1) * D], hid[2][:, c * P:(c + 1) * P], pc("wm", D, 2 * D))
                    ins.then_inc(p0["mg_ps"], 1)
                if here:
                    adjacency(0, b, 28, 32, feat, None)

            pe.wait_ge(x2_loaded, 16)
            iter0(0, True, False)
            iter0(1, True, True)
            with pe.Fori(2, NB) as b:
                iter0(b, True, True)
            iter0(NB, False, True)

            pe.wait_ge(p0["scaled"], 3 * NB)
            pe.wait_ge(p0["mg"], NB)
            pe.wait_ge(prep_dve, 7)
            pe.wait_ge(prep_pool, 8)

            def chunk_scores(a, c):
                n = C * a + c
                wait(pe, p1["act"], 4 * a + 4)
                wait(pe, p1["xT"], n)
                if c == 0:
                    wait(pe, p1["xbc"], 3 * a + 3)
                cc = slice(c * P, (c + 1) * P)
                for k in range(2):
                    nc.tensor.transpose(b4[:, k * P:(k + 1) * P], xs[k][:, cc], ident)
                nc.tensor.transpose(b4[:, DI:DI + DS], bs[:, cc], pc("ident", 0, DS, rows=DS)).then_inc(p1["xT_ps"], 1)
                wait(pe, p1["esub"], n)
                wait(pe, p1["dec"], 3 * a + 3)
                for h in range(NH):
                    ins = mm(b5[:, h * P:(h + 1) * P], pc("pick", h * P, (h + 1) * P, rows=NH), acum[:, cc])
                ins.then_inc(p1["rb_ps"], 1)
                wait(pe, p1["gm"], n)
                mm(b2[:, 0:P], bs[:, cc], cs[:, cc]).then_inc(p1["gt_ps"], 1)

            def chunk_outputs(a, c):
                n = C * a + c
                i = c % 2
                cc = slice(c * P, (c + 1) * P)
                wait(pe, p1["xdd"], n + 1)
                wait(pe, p1["st"], n)
                mm(b3[0:DS, 0:DI], xt[i][:, DI:DI + DS], xdd[i][:]).then_inc(p1["st_ps"], 1)
                wait(pe, p1["y"], n)
                wait(pe, p1["zs"], 2 * a + 2)
                mm(b6[:, DI:2 * DI], cs[:, cc], state[:], skip_group_check=True)
                for k in range(2):
                    mm(b6[:, k * P:(k + 1) * P], xs[k][:, cc], skip_d[:, k, :], start=False, stop=False,
                       skip_group_check=True)
                wait(pe, p1["m"], n + 1)
                wait(pe, p1["xdt"], n + 1)
                for h in range(NH):
                    ins = mm(b6[:, h * HD:(h + 1) * HD], decay[i][:, h, :], xdt[i][:, h * HD:(h + 1) * HD],
                             start=False, stop=(h == NH - 1), skip_group_check=True)
                ins.then_inc(p1["y_ps"], 1)

            def chunk_turn(a, c):
                n = C * a + c
                wait(pe, p1["y2"], n + 1)
                wait(pe, p1["yT"], n)
                for k in range(2):
                    ins = nc.tensor.transpose(b7[:, k * P:(k + 1) * P], y2[c % 2][:, k * P:(k + 1) * P], ident)
                ins.then_inc(p1["yT_ps"], 1)

            def chunk_project(a, c):
                n = C * a + c
                wait(pe, p1["yT"], n + 1)
                wait(pe, p1["x2"], n)
                for k in range(2):
                    ins = mm(tr_ps[:, 0:D], y_t[c % 2][:, k * P:(k + 1) * P], w_ol[:, k, :], start=(k == 0), stop=(k == 1))
                ins.then_inc(p1["o_ps"], 1)

            def iter1(b, here, before):
                a = b - 1
                if before:
                    wait(pe, p1["z_sb"], b)
                    wait(pe, p1["x2"], C * a)
                    transposes(lambda c: z_t[:, c * P:(c + 1) * P], tr_ps, C, p1["zt_ps"])
                if here:
                    adjacency(1, b, 0, 4, sup, p1["z_sb"])
                if before:
                    wait(pe, ln_norm, 4 * (NB + 2 * a + 1))
                    transposes(lambda c: xhat[:, c, :], tr_ps, C, p1["xt_ps"])
                if here:
                    adjacency(1, b, 4, 6, sup, None)
                if before:
                    wait(pe, p1["xt_sb"], b)
                    wait(pe, p1["esub"], C * a)
                    mm(b5[0:NH, :], pc("w_in", 2 * DI + 2 * DS, 2 * DI + 2 * DS + NH), xhat_t[:]).then_inc(p1["proj_ps"], 1)
                    wait(pe, p1["gm"], C * a)
                    wait(pe, p1["st"], C * a)
                    wait(pe, p1["xT"], C * a)
                    for k, bk in enumerate((b2, b3, b4)):
                        mm(bk[:], pc("w_in", DI + k * P, DI + (k + 1) * P), xhat_t[:]).then_inc(p1["proj_ps"], 1)
                    wait(pe, p1["y"], C * a)
                    wait(pe, p1["yT"], C * a)
                    for c in range(C):
                        bk = (b6, b7)[c // 2]
                        ins = mm(bk[:, c % 2 * DI:(c % 2 + 1) * DI], xhat_t[:, c * P:(c + 1) * P], pc("w_in", 0, DI))
                        if c % 2:
                            ins.then_inc(p1["zp_ps"], 1)
                if here:
                    adjacency(1, b, 6, 12, sup, None)
                if before:
                    wait(pe, p1["scan"], b)
                    wait(pe, p1["dtact"], 2 * b)
                    mm(b5[:, BT - 1:BT], ident, pc("ones", 0, 1))
                    for k, src in enumerate((acum, dtr[:, 0, :])):
                        for c in range(C):
                            ins = nc.tensor.transpose(b5[:, (k * C + c) * NH:(k * C + c + 1) * NH],
                                                      src[:, c * P:(c + 1) * P], pc("ident", 0, NH, rows=NH))
                    ins.then_inc(p1["cols_ps"], 1)
                if here:
                    adjacency(1, b, 12, 14, sup, None)
                if before:
                    wait(pe, p1["cols"], b)
                    mm(b5[:, 0:C * NH], pc("last"), cols[:, 0, :, :].rearrange("p c h -> p (c h)")).then_inc(p1["end_ps"], 1)
                if here:
                    adjacency(1, b, 14, 16, sup, None)
                fill = 16
                for step in range(C + 3):
                    if before:
                        if step >= 3:
                            chunk_project(a, step - 3)
                        if 0 <= step - 2 < C:
                            chunk_turn(a, step - 2)
                        if 0 <= step - 1 < C:
                            chunk_outputs(a, step - 1)
                        if step < C:
                            chunk_scores(a, step)
                    if here:
                        n = (3, 3, 3, 3, 2, 2, 0)[step]
                        adjacency(1, b, fill, fill + n, sup, None)
                        fill += n

            iter1(0, True, False)
            iter1(1, True, True)
            with pe.Fori(2, NB) as b:
                iter1(b, True, True)
            iter1(NB, False, True)

            pe.wait_ge(ln_norm, 4 * 3 * NB)
            pe.wait_ge(p1["x2"], C * NB)

            def expert_in(a, e):
                n = E * a + e
                wait(pe, p2["h1"], n - 1 if e else n)
                mm((b4, b5)[e % 2][:], pc("ew1", e * D, (e + 1) * D), xhat_t[:]).then_inc(p2["w1_ps"], 1)

            def expert_mid(a, e):
                n = E * a + e
                wait(pe, p2["h1"], n + 1)
                wait(pe, p2["h2"], n)
                mm(b6[:], pc("ew2", e * D, (e + 1) * D), h1[e % 2][:]).then_inc(p2["w2_ps"], 1)

            def expert_out(a, e):
                n = E * a + e
                wait(pe, p2["h2"], n + 1)
                wait(pe, p2["acc"], C * n)
                for c in range(C):
                    ins = mm(b7[:, c * D:(c + 1) * D], h2[e % 2][:, c * P:(c + 1) * P], pc("ewo", e * D, (e + 1) * D))
                ins.then_inc(p2["wo_ps"], 1)

            def iter2(b, here, before):
                a = b - 1
                at = 0

                def fill(n):
                    nonlocal at
                    if here:
                        adjacency(2, b, at, at + n, feat, p2["z_sb"])
                        at += n

                fill(2)
                if before:
                    for l in range(3):
                        wait(pe, p2["z_sb"], b) if l == 0 else wait(pe, p2["h"], 3 * a + l)
                        wait(pe, p2["h"], 3 * a + l)
                        mm(b2[:], pc("mlp1_w", l * D, (l + 1) * D), z_t[:] if l == 0 else hid[l - 1][:]).then_inc(p2["mlp_ps"], 1)
                        fill(2)
                    wait(pe, p2["h"], 3 * b)
                    wait(pe, p2["gb"], a)
                    for c in range(C):
                        ins = mm(b3[:, c * D:(c + 1) * D], hid[2][:, c * P:(c + 1) * P], pc("wm", 0, D))
                    ins.then_inc(p2["mg_ps"], 1)
                    fill(5)
                    wait(pe, ln_norm, 4 * (3 * NB + b))
                    transposes(lambda c: xhat[:, c, :], tr_ps, C, p2["xt_ps"])
                    fill(1)
                    wait(pe, p2["xt_sb"], b)
                    for c in range(C):
                        ins = mm(b3[:, c * E:(c + 1) * E], xhat_t[:, c * P:(c + 1) * P], pc("wr"))
                    ins.then_inc(p2["gl_ps"], 1)
                    for e in range(E + 2):
                        if e < E:
                            expert_in(a, e)
                        if 0 <= e - 1 < E:
                            expert_mid(a, e - 1)
                        if e == 1:
                            wait(pe, p2["gate"], b)
                            for c in range(C):
                                ins = nc.tensor.transpose(b3[0:E, c * P:(c + 1) * P], gate[:, c, :], ident)
                            ins.then_inc(p2["gt_ps"], 1)
                        if e == 2:
                            wait(pe, p2["gt_sb"], b)
                            for c in range(C):
                                ins = mm(b3[:, c * D:(c + 1) * D], gate_t[:, c * P:(c + 1) * P], pc("bo", rows=E))
                            ins.then_inc(p2["gb_ps"], 1)
                        if e >= 2:
                            expert_out(a, e - 2)
                        fill(2 if e < 8 else 1)
                else:
                    fill(NT - at)
                if here:
                    assert at == NT, at

            iter2(0, True, False)
            iter2(1, True, True)
            with pe.Fori(2, NB) as b:
                iter2(b, True, True)
            iter2(NB, False, True)

        @block.scalar
        def _(act):
            A = nc.scalar.activation
            act.dma_start(par[:], par_in).then_inc(par_loaded, 16)
            act.dma_start(x[:], x_in.rearrange("(t p) d -> p t d", p=P)).then_inc(x_loaded, 16)
            act.wait_ge(par_loaded, 16)
            A(a_neg[:, 0:1], pc("a_log", rows=NH), ACT.Exp).then_inc(prep_act, 1)
            act.wait_ge(prep_dve, 2)

            def iter0(b, here, before):
                if before:
                    wait(act, adj_used, strips_used(0, b - 1, G - 1))
                    wait(act, p0["mlp_ps"], 3 * (b - 1))
                    A(z_t[:], acc_ps[:], ACT.Identity, scale=gain[:, 1:2]).then_inc(p0["z_sb"], 1)
                if here:
                    wait(act, p0["xt_ps"], b + 1)
                    wait(act, p0["sup_ps"], b)
                    A(xhat_t[:], tr_ps[:], ACT.Copy).then_inc(p0["xt_sb"], 1)
                if before:
                    for l in range(3):
                        wait(act, p0["mlp_ps"], 3 * (b - 1) + l + 1)
                        if l == 2:
                            wait(act, p0["mg_ps"], b - 1)
                        A(hid[l][:], b2[:], ACT.Relu, bias=pc("mlp2_b", l, l + 1)).then_inc(p0["h"], 1)

            iter0(0, True, False)
            iter0(1, True, True)
            with act.Fori(2, NB) as b:
                iter0(b, True, True)
            iter0(NB, False, True)

            def iter1(b):
                a = b - 1
                wait(act, adj_used, strips_used(1, a, G - 1))
                wait(act, p1["zt_ps"], a)
                if isinstance(b, int) and b == 1:
                    wait(act, p0["mlp_ps"], 3 * NB)
                A(z_t[:], acc_ps[:], ACT.Copy).then_inc(p1["z_sb"], 1)
                wait(act, p1["xt_ps"], b)
                wait(act, p1["zp_ps"], 2 * a)
                if isinstance(b, int) and b == 1:
                    wait(act, p0["sup_ps"], NB)
                A(xhat_t[:], tr_ps[:], ACT.Copy).then_inc(p1["xt_sb"], 1)
                dtb = pc("dt_bias", rows=NH)
                wait(act, p1["proj_ps"], 4 * a + 1)
                wait(act, p1["cols_ps"], a)
                A(dtr[:, 0, :], b5[0:NH, :], ACT.Relu, bias=dtb).then_inc(p1["dtact"], 1)
                A(dtr[:, 1, :], b5[0:NH, :], ACT.Abs, bias=dtb).then_inc(p1["dtact"], 1)
                for k, bk in enumerate((b2, b3, b4)):
                    wait(act, p1["proj_ps"], 4 * a + k + 2)
                    wait(act, p1["carry"], 3 * (a + 1))
                    A(xbc[k][:, TAPS - 1:], bk[:], ACT.Copy).then_inc(p1["xbc"], 1)
                wait(act, p1["dtact"], 2 * b)
                A(dtr[:, 1, :], dtr[:, 1, :], ACT.Exp, scale=-1.0).then_inc(p1["dtexp"], 1)
                wait(act, p1["dtexp"], b)
                A(dtr[:, 1, :], dtr[:, 1, :], ACT.Ln, bias=1.0).then_inc(p1["dtln"], 1)
                for k, bk in enumerate((b6, b7)):
                    wait(act, p1["zp_ps"], 2 * a + k + 1)
                    wait(act, p1["y2"], C * a)
                    A(zs[:, 2 * k:2 * k + 2, :].rearrange("p c d -> p (c d)"), bk[:], ACT.Silu).then_inc(p1["zs"], 1)
                wait(act, p1["y_ps"], C * a)
                wait(act, p1["st_ps"], C * a)
                for k in range(2):
                    wait(act, p1["conv"], 12 * a + 9 + k + 1)
                    A(xs[k][:], conv[k][:, 1, :], ACT.Silu, bias=pc("conv_b", k, k + 1)).then_inc(p1["act"], 1)
                wait(act, p1["conv"], 12 * a + 12)
                cb = pc("conv_b", 2, 3)
                A(bs[:], conv[2][0:DS, 1, :], ACT.Silu, bias=cb[0:DS, :]).then_inc(p1["act"], 1)
                A(cs[:], conv[2][DS:2 * DS, 1, :], ACT.Silu, bias=cb[DS:2 * DS, :]).then_inc(p1["act"], 1)
                wait(act, p1["dec"], 3 * b)
                A(dece[:], dec[:], ACT.Exp).then_inc(p1["dece"], 1)
                for step in range(C + 2):
                    if step < C:
                        c, n, i = step, C * a + step, step % 2
                        wait(act, p1["xT_ps"], n + 1)
                        wait(act, p1["st_ps"], n - 1)
                        A(xt[i][:], b4[:, 0:DI + DS], ACT.Copy).then_inc(p1["xT"], 1)
                        wait(act, p1["earg"], n + 1)
                        A(decay[i][:], decay[i][:], ACT.Exp, scale=1.0).then_inc(p1["ee"], 1)
                    if step >= 2:
                        c, n, i = step - 2, C * a + step - 2, step % 2
                        wait(act, p1["y2"], n + 1)
                        wait(act, p1["ssq"], n)
                        A(ysq[:], y2[i][:], ACT.Square, accum_out=ssq[:, c:c + 1]).then_inc(p1["ssq"], 1)
                        wait(act, p1["yT_ps"], n + 1)
                        wait(act, p1["o_ps"], n - 1)
                        A(y_t[i][:], b7[:, 0:DI], ACT.Copy).then_inc(p1["yT"], 1)

            act.wait_ge(p1["carry"], 3)
            iter1(1)
            with act.Fori(2, NB + 1) as b:
                iter1(b)

            def iter2(b):
                a = b - 1
                wait(act, adj_used, strips_used(2, a, G - 1))
                wait(act, p2["mlp_ps"], 3 * a)
                A(z_t[:], acc_ps[:], ACT.Identity, scale=gain[:, 0:1]).then_inc(p2["z_sb"], 1)
                for l in range(3):
                    wait(act, p2["mlp_ps"], 3 * a + l + 1)
                    if l == 2:
                        wait(act, p2["mg_ps"], a)
                    A(hid[l][:], b2[:], ACT.Relu, bias=pc("mlp1_b", l, l + 1)).then_inc(p2["h"], 1)
                wait(act, p2["xt_ps"], b)
                wait(act, p2["w1_ps"], E * a)
                A(xhat_t[:], tr_ps[:], ACT.Copy).then_inc(p2["xt_sb"], 1)
                wait(act, p2["sub"], b)
                A(lg[:, 2], lg[:, 1], ACT.Exp).then_inc(p2["ex"], 1)
                for e in range(E + 1):
                    if e < E:
                        n = E * a + e
                        wait(act, p2["w1_ps"], n + 1)
                        wait(act, p2["w2_ps"], n - 1)
                        A(h1[e % 2][:], (b4, b5)[e % 2][:], ACT.Relu, scale=bn_s[:, e:e + 1], bias=bn_f[:, e:e + 1]).then_inc(p2["h1"], 1)
                    if e >= 1:
                        n = E * a + e - 1
                        wait(act, p2["w2_ps"], n + 1)
                        wait(act, p2["wo_ps"], n - 1)
                        A(h2[(e - 1) % 2][:], b6[:], ACT.Relu, scale=bn_s[:, E + e - 1:E + e], bias=bn_f[:, E + e - 1:E + e]).then_inc(p2["h2"], 1)

            act.wait_ge(prep_pool, 8)
            iter2(1)
            with act.Fori(2, NB + 1) as b:
                iter2(b)

        @block.vector
        def _(dve):
            V = nc.vector

            def norm_stats(n, tile):
                wait(dve, ln_aggr, 4 * n)
                hold(V)
                for c in range(C):
                    V.bn_stats(stats[:, c, :], tile(c)).then_inc(ln_stats, 1)
                wait(dve, ln_norm, 4 * n)
                wait(dve, ln_stats, 4 * n + 4)
                hold(V)
                for c in range(C):
                    V.bn_aggr(mv[:, c, :], stats[:, c, :]).then_inc(ln_aggr, 1)

            def norm_apply(n, tile, dst):
                wait(dve, ln_rstd, n + 1)
                for c in range(C):
                    V.tensor_scalar(dst(c), tile(c), mv[:, c, 0:1], rstd[:, c:c + 1], ALU.subtract, ALU.mult).then_inc(ln_norm, 1)

            V.memset(neg_half[:], -0.5).then_inc(consts_set, 1)
            V.memset(state[:], 0.0).then_inc(consts_set, 1)
            dve.wait_ge(consts_set, 2)
            dve.wait_ge(par_loaded, 16)
            V.tensor_scalar(gain[:, 0:1], pc("eps1"), 1.0, 1.0, ALU.add, ALU.add).then_inc(prep_dve, 1)
            V.tensor_scalar(gain[:, 1:2], pc("eps2"), 1.0, 1.0, ALU.add, ALU.add).then_inc(prep_dve, 1)
            dve.wait_ge(x_loaded, 16)
            norm_stats(0, lambda c: x[:, c, :])
            norm_apply(0, lambda c: x[:, c, :], lambda c: xhat[:, c, :])
            dve.wait_ge(prep_act, 1)
            V.tensor_scalar(a_neg[:, 1:2], a_neg[:, 0:1], -1.0, None, ALU.mult).then_inc(prep_dve, 1)
            for k in range(2):
                V.tensor_scalar(skip_d[:, k, :], ident, pc("skip", k, k + 1), None, ALU.mult).then_inc(prep_dve, 1)
            dve.wait_ge(prep_pe, 1)
            for k in range(2):
                V.tensor_scalar(w_ol[:, k, :], b2[:, k * P:(k + 1) * P], pc("norm_w", k, k + 1), None, ALU.mult).then_inc(prep_dve, 1)

            def rows4(ap):
                return ap[:].rearrange("p (c d) -> p c d", c=C)

            def bias4(name):
                return pc(name).unsqueeze(1).broadcast_to([P, C, D])

            def iter0(b, here, before, follows):
                if before:
                    wait(dve, p0["deg_ps"], b)
                    wait(dve, p0["dis"], 5 * (b - 1))
                    V.tensor_scalar(deg[:], b5[:, 0:C], 1.0, None, ALU.add).then_inc(p0["deg"], 1)
                if here:
                    for q in range(G):
                        wait(dve, adj_loaded[q % SLOTS], strip_loaded(0, b, q))
                        if q < 4:
                            wait(dve, p0["colsum"], 7 * b)
                        else:
                            wait(dve, p0["colsum"], 7 * b + (q - 4) // 2 + 1)
                        V.tensor_reduce(part[:, q % 4, :], ring[:, q % SLOTS].rearrange("p j n -> p n j"), AX_X, ALU.add).then_inc(adj_summed, 1)
                        if q % 2:
                            k = q // 2
                            wait(dve, adj_summed, G * b + q + 1)
                            dst = pair[:, k, :] if k < 2 else part[:, 2 * k - 4, :]
                            V.tensor_tensor(dst, part[:, 2 * k % 4, :], part[:, 2 * k % 4 + 1, :], ALU.add).then_inc(p0["colsum"], 1)
                        if q == 2 and follows:
                            norm_stats(b + 1, lambda c: x[:, 4 * (b + 1) + c, :])
                        if q == 3:
                            wait(dve, p0["sup_ps"], b + 1)
                            V.tensor_tensor(sup[:, ts(b, C), :], rows4(b3), bias4("g0_b"), ALU.add).then_inc(p0["sup"], 1)
                        if q == 3 and follows:
                            wait(dve, p0["xt_ps"], b + 1)
                            norm_apply(b + 1, lambda c: x[:, 4 * (b + 1) + c, :], lambda c: xhat[:, c, :])
                    wait(dve, p0["colsum"], 7 * b + 4)
                    for k in range(2):
                        V.tensor_tensor(pair[:, k, :], pair[:, k, :], part[:, 2 * k, :], ALU.add).then_inc(p0["colsum"], 1)
                    wait(dve, p0["colsum"], 7 * b + 6)
                    wait(dve, p0["deg_ps"], b)
                    V.tensor_tensor(colsum[:], pair[:, 0, :], pair[:, 1, :], ALU.add).then_inc(p0["colsum"], 1)
                if before:
                    wait(dve, p0["mg_ps"], b)
                    V.tensor_tensor(side[:, ts(b - 1, C), :], rows4(b4), bias4("bm"), ALU.add).then_inc(p0["mg"], 1)

            iter0(0, True, False, True)
            iter0(1, True, True, True)
            with dve.Fori(2, NB - 1) as b:
                iter0(b, True, True, True)
            iter0(NB - 1, True, True, False)
            iter0(NB, False, True, False)

            for k in range(3):
                V.memset(xbc[k][:, 0:TAPS - 1], 0.0).then_inc(p1["carry"], 1)

            def iter1(a):
                t0 = 4 * a
                wait(dve, p1["zt_ps"], a + 1)
                if isinstance(a, int) and a == 0:
                    dve.wait_ge(p0["scaled"], 3 * NB)
                for c in range(C):
                    V.scalar_tensor_tensor(out=x[:, t0 + c, :], in0=tr_ps[:, c * P:(c + 1) * P], scalar=dis[:, ts(t0 + c, 1)],
                                           in1=x[:, t0 + c, :], op0=ALU.mult, op1=ALU.add).then_inc(p1["x1"], 1)
                wait(dve, p1["x1"], 4 * a + 4)
                n = NB + 2 * a
                norm_stats(n, lambda c: x[:, t0 + c, :])
                norm_apply(n, lambda c: x[:, t0 + c, :], lambda c: xhat[:, c, :])
                for j in range(TAPS):
                    for k in range(3):
                        wait(dve, p1["xbc"], 3 * a + k + 1)
                        w = pc("conv_w", k * TAPS + j, k * TAPS + j + 1)
                        src = xbc[k][:, j:j + BT]
                        if j == 0:
                            wait(dve, p1["conv"], 12 * a)
                            wait(dve, p1["act"], 4 * a)
                            V.tensor_scalar(conv[k][:, 0, :], src, w, None, ALU.mult).then_inc(p1["conv"], 1)
                        else:
                            wait(dve, p1["conv"], 12 * a + 3 * (j - 1) + k + 1)
                            V.scalar_tensor_tensor(out=conv[k][:, j % 2, :], in0=src, scalar=w, in1=conv[k][:, (j - 1) % 2, :],
                                                   op0=ALU.mult, op1=ALU.add).then_inc(p1["conv"], 1)
                    if j == 1:
                        wait(dve, p1["dtln"], a + 1)
                        wait(dve, p1["cols_ps"], a)
                        V.tensor_tensor(dtr[:, 0, :], dtr[:, 0, :], dtr[:, 1, :], ALU.add).then_inc(p1["dtrow"], 1)
                        wait(dve, p1["dtrow"], 2 * a + 1)
                        V.tensor_scalar(dtr[:, 1, :], dtr[:, 0, :], a_neg[:, 1:2], None, ALU.mult).then_inc(p1["dtrow"], 1)
                        wait(dve, p1["dtrow"], 2 * a + 2)
                        wait(dve, p1["rb_ps"], C * a)
                        V.tensor_tensor_scan(acum[:], pc("restart", rows=NH), dtr[:, 1, :], 0.0, ALU.mult, ALU.add).then_inc(p1["scan"], 1)
                wait(dve, p1["conv"], 12 * a + 12)
                for k in range(3):
                    V.tensor_copy(xbc[k][:, 0:TAPS - 1], xbc[k][:, BT:BT + TAPS - 1]).then_inc(p1["carry"], 1)
                wait(dve, p1["cols_ps"], a + 1)
                wait(dve, p1["xdt"], C * a)
                wait(dve, p1["earg"], C * a)
                V.tensor_copy(cols[:].rearrange("p k c h -> p (k c h)"), b5[:, 0:2 * C * NH]).then_inc(p1["cols"], 1)
                wait(dve, p1["end_ps"], a + 1)
                wait(dve, p1["cols"], a + 1)
                wait(dve, p1["dece"], a)
                ac = cols[:, 0].rearrange("p c h -> p (c h)")
                V.tensor_tensor(dec[:, 0, :], b5[:, 0:C * NH], ac, ALU.subtract).then_inc(p1["dec"], 1)
                V.tensor_copy(dec[:, 1, :], ac).then_inc(p1["dec"], 1)
                V.tensor_copy(dec[:, 2, :], b5[:, 0:C * NH]).then_inc(p1["dec"], 1)

                def heads(ap, n):
                    return ap.unsqueeze(2).broadcast_to([ap.shape[0], NH, n])

                for step in range(C + 3):
                    if step < C:
                        c, n, i = step, C * a + step, step % 2
                        wait(dve, p1["rb_ps"], n + 1)
                        wait(dve, p1["y_ps"], n - 1)
                        V.tensor_tensor(decay[i][:], b5[:].rearrange("p (h l) -> p h l", h=NH), heads(cols[:, 0, c, :], P),
                                        ALU.subtract).then_inc(p1["esub"], 1)
                        wait(dve, p1["gt_ps"], n + 1)
                        wait(dve, p1["m"], n - 1)
                        V.tensor_tensor(g_m[i][:], b2[:, 0:P], pc("upper"), ALU.mult).then_inc(p1["gm"], 1)
                        wait(dve, p1["esub"], n + 1)
                        V.tensor_scalar(decay[i][:], decay[i][:], 0.0, None, ALU.min).then_inc(p1["earg"], 1)
                    if 1 <= step <= C:
                        c, n, i = step - 1, C * a + step - 1, (step - 1) % 2
                        wait(dve, p1["y_ps"], n + 1)
                        wait(dve, p1["dece"], a + 1)
                        wait(dve, p1["y"], n)
                        V.tensor_tensor(y0[i][:].rearrange("p (h d) -> p h d", h=NH), b6[:, DI:2 * DI].rearrange("p (h d) -> p h d", h=NH),
                                        heads(dece[:, 1, c * NH:(c + 1) * NH], HD), ALU.mult).then_inc(p1["y0"], 1)
                        wait(dve, p1["st"], n)
                        st = state[:].rearrange("p (h d) -> p h d", h=NH)
                        V.tensor_tensor(st, st, heads(dece[0:DS, 2, c * NH:(c + 1) * NH], HD), ALU.mult).then_inc(p1["stmul"], 1)
                        wait(dve, p1["y0"], n + 1)
                        wait(dve, p1["y2"], n - 1)
                        V.tensor_tensor(y[i][:], b6[:, 0:DI], y0[i][:], ALU.add).then_inc(p1["y"], 1)
                        wait(dve, p1["stmul"], n + 1)
                        wait(dve, p1["st_ps"], n + 1)
                        V.tensor_tensor(state[:], state[:], b3[0:DS, 0:DI], ALU.add).then_inc(p1["st"], 1)
                    if step < C:
                        c, n, i = step, C * a + step, step % 2
                        wait(dve, p1["ee"], n + 1)
                        wait(dve, p1["gm"], n + 1)
                        V.tensor_tensor(decay[i][:], decay[i][:], g_m[i][:].unsqueeze(1).broadcast_to([P, NH, P]), ALU.mult).then_inc(p1["m"], 1)
                    if step >= 3:
                        c, n = step - 3, C * a + step - 3
                        wait(dve, p1["o_ps"], n + 1)
                        wait(dve, p1["rms"], n + 1)
                        wait(dve, p1["x1b"], a + 1)
                        V.scalar_tensor_tensor(out=x[:, t0 + c, :], in0=tr_ps[:, 0:D], scalar=rms[:, c:c + 1], in1=x[:, t0 + c, :],
                                               op0=ALU.mult, op1=ALU.add).then_inc(p1["x2"], 1)
                wait(dve, p1["x2"], C * a + C)
                norm_stats(NB + 2 * a + 1, lambda c: x[:, t0 + c, :])
                norm_apply(NB + 2 * a + 1, lambda c: x[:, t0 + c, :], lambda c: feat[:, t0 + c, :])

            iter1(0)
            with dve.Fori(1, NB) as a:
                iter1(a)

            def iter2(a):
                t0 = 4 * a
                b = a + 1
                xb = x[:, ts(a, C), :]
                wait(dve, p2["mg_ps"], b)
                wait(dve, p2["xm"], b)
                V.tensor_tensor(xb, rows4(b3), xb, ALU.add).then_inc(p2["x3"], 1)
                wait(dve, p2["x3"], b)
                n = 3 * NB + a
                norm_stats(n, lambda c: x[:, t0 + c, :])
                norm_apply(n, lambda c: x[:, t0 + c, :], lambda c: xhat[:, c, :])
                wait(dve, p2["gl_ps"], b)
                wait(dve, p2["gt_ps"], a)
                V.tensor_tensor(lg[:, 0], b3[:, 0:C * E].rearrange("p (c e) -> p c e", c=C),
                                pc("br").unsqueeze(1).broadcast_to([P, C, E]), ALU.add).then_inc(p2["lg"], 1)
                wait(dve, p2["lg"], b)
                V.tensor_reduce(red[:, 0, :], lg[:, 0], AX_X, ALU.max).then_inc(p2["mx"], 1)
                wait(dve, p2["mx"], b)
                V.tensor_tensor(lg[:, 1], lg[:, 0], red[:, 0, :].unsqueeze(2).broadcast_to([P, C, E]), ALU.subtract).then_inc(p2["sub"], 1)
                wait(dve, p2["ex"], b)
                V.tensor_reduce(red[:, 1, :], lg[:, 2], AX_X, ALU.add).then_inc(p2["sum"], 1)
                wait(dve, p2["sum"], b)
                V.reciprocal(red[:, 2, :], red[:, 1, :]).then_inc(p2["rcp"], 1)
                wait(dve, p2["rcp"], b)
                wait(dve, p2["acc"], C * E * a)
                V.tensor_tensor(gate[:], lg[:, 2], red[:, 2, :].unsqueeze(2).broadcast_to([P, C, E]), ALU.mult).then_inc(p2["gate"], 1)
                wait(dve, p2["gt_ps"], b)
                V.tensor_copy(gate_t[:], b3[0:E, :]).then_inc(p2["gt_sb"], 1)
                wait(dve, p2["gb_ps"], b)
                V.tensor_tensor(xb, rows4(b3), xb, ALU.add).then_inc(p2["gb"], 1)
                wait(dve, p2["gate"], b)
                wait(dve, p2["gb"], b)
                for e in range(E):
                    wait(dve, p2["wo_ps"], E * a + e + 1)
                    for c in range(C):
                        if e:
                            wait(dve, p2["acc"], C * (E * a + e - 1) + c + 1)
                        V.scalar_tensor_tensor(out=x[:, t0 + c, :], in0=b7[:, c * D:(c + 1) * D], scalar=gate[:, c, e:e + 1],
                                               in1=x[:, t0 + c, :], op0=ALU.mult, op1=ALU.add).then_inc(p2["acc"], 1)

            iter2(0)
            with dve.Fori(1, NB) as a:
                iter2(a)

        @block.gpsimd
        def _(pool):
            Q = nc.gpsimd

            def norm_rstd(n):
                wait(pool, ln_aggr, 4 * n + 4)
                wait(pool, ln_rstd, n)
                hold(Q)
                Q.tensor_scalar(var[:], mv[:, :, 1], LN_EPS, None, ALU.add).then_inc(ln_var, 1)
                wait(pool, ln_var, n + 1)
                Q.tensor_tensor(rstd[:], var[:], neg_half[:, 0:C], ALU.pow).then_inc(ln_rstd, 1)

            pool.wait_ge(consts_set, 1)
            norm_rstd(0)
            pool.wait_ge(par_loaded, 16)
            for k, (v, g, m, bb, be) in enumerate((("v1", "g1", "m1", "b1", "be1"), ("v2", "g2", "m2", "b2", "be2"))):
                s = slice(k * E, (k + 1) * E)
                base = 5 * k
                Q.tensor_scalar(bn_t[:, 0, s], pc(v), BN_EPS, None, ALU.add).then_inc(prep_pool, 1)
                pool.wait_ge(prep_pool, base + 1)
                Q.tensor_tensor(bn_t[:, 1, s], bn_t[:, 0, s], neg_half[:, s], ALU.pow).then_inc(prep_pool, 1)
                Q.tensor_tensor(bn_t[:, 2, s], pc(bb), pc(m), ALU.subtract).then_inc(prep_pool, 1)
                pool.wait_ge(prep_pool, base + 3)
                Q.tensor_tensor(bn_s[:, s], pc(g), bn_t[:, 1, s], ALU.mult).then_inc(prep_pool, 1)
                pool.wait_ge(prep_pool, base + 4)
                Q.tensor_tensor(bn_f[:, s], bn_t[:, 2, s], bn_s[:, s], ALU.mult).then_inc(prep_pool, 1)
            pool.wait_ge(prep_pool, 10)
            for k, be in enumerate(("be1", "be2")):
                s = slice(k * E, (k + 1) * E)
                Q.tensor_tensor(bn_f[:, s], bn_f[:, s], pc(be), ALU.add).then_inc(prep_pool, 1)

            def degrees(a):
                wait(pool, p0["deg"], a + 1)
                d = p0["dis"]
                hold(Q)
                Q.tensor_scalar(dg[:, 0, :], deg[:], 0.0, None, ALU.is_equal).then_inc(d, 1)
                wait(pool, d, 5 * a + 1)
                Q.tensor_tensor(dg[:, 1, :], deg[:], dg[:, 0, :], ALU.add).then_inc(d, 1)
                Q.tensor_scalar(dg[:, 3, :], dg[:, 0, :], -1.0, 1.0, ALU.mult, ALU.add).then_inc(d, 1)
                wait(pool, d, 5 * a + 3)
                Q.tensor_tensor(dg[:, 2, :], dg[:, 1, :], neg_half[:, 0:C], ALU.pow).then_inc(d, 1)
                wait(pool, d, 5 * a + 4)
                Q.tensor_tensor(dis[:, ts(a, C)], dg[:, 2, :], dg[:, 3, :], ALU.mult).then_inc(d, 1)
                wait(pool, d, 5 * a + 5)
                wait(pool, p0["sup"], a + 1)
                s, tb = p0["scaled"], ts(a, C)
                hold(Q)
                by = dis[:, tb].unsqueeze(2).broadcast_to([P, C, D])
                Q.tensor_tensor(sup[:, tb, :], sup[:, tb, :], by, ALU.mult).then_inc(s, 1)
                wait(pool, s, 3 * a + 1)
                hold(Q)
                Q.tensor_tensor(decay[0][:], sup[:, tb, :], by, ALU.mult).then_inc(s, 1)
                wait(pool, s, 3 * a + 2)
                hold(Q)
                Q.tensor_tensor(x[:, tb, :], x[:, tb, :], decay[0][:], ALU.add).then_inc(s, 1)

            norm_rstd(1)
            with pool.Fori(1, NB - 1) as b:
                degrees(b - 1)
                norm_rstd(b + 1)
            degrees(NB - 2)
            degrees(NB - 1)

            def iter1(a):
                norm_rstd(NB + 2 * a)
                tb = ts(a, C)
                wait(pool, ln_norm, 4 * (NB + 2 * a + 1))
                hold(Q)
                Q.tensor_tensor(x[:, tb, :], x[:, tb, :], pc("b_lin").unsqueeze(1).broadcast_to([P, C, D]), ALU.add).then_inc(p1["x1b"], 1)
                for step in range(C + 2):
                    if step < C:
                        c, n, i = step, C * a + step, step % 2
                        wait(pool, p1["xT"], n + 1)
                        wait(pool, p1["cols"], a + 1)
                        wait(pool, p1["y_ps"], n - 1)
                        h3 = lambda ap: ap.rearrange("p (h d) -> p h d", h=NH)
                        Q.tensor_tensor(h3(xdt[i][:]), h3(xt[i][:, 0:DI]), cols[:, 1, c, :].unsqueeze(2).broadcast_to([P, NH, HD]),
                                        ALU.mult).then_inc(p1["xdt"], 1)
                        wait(pool, p1["xdt"], n + 1)
                        wait(pool, p1["dece"], a + 1)
                        wait(pool, p1["st_ps"], n - 1)
                        Q.tensor_tensor(h3(xdd[i][:]), h3(xdt[i][:]), dece[:, 0, c * NH:(c + 1) * NH].unsqueeze(2).broadcast_to([P, NH, HD]),
                                        ALU.mult).then_inc(p1["xdd"], 1)
                    if 1 <= step <= C:
                        c, n, i = step - 1, C * a + step - 1, (step - 1) % 2
                        wait(pool, p1["y"], n + 1)
                        wait(pool, p1["zs"], 2 * a + 2)
                        wait(pool, p1["yT_ps"], n - 1)
                        wait(pool, p1["ssq"], n - 1)
                        Q.tensor_tensor(y2[i][:], y[i][:], zs[:, c, :], ALU.mult).then_inc(p1["y2"], 1)
                    if step >= 2:
                        c, n = step - 2, C * a + step - 2
                        wait(pool, p1["ssq"], n + 1)
                        wait(pool, p1["rms"], n)
                        hold(Q)
                        Q.tensor_scalar(msq[:, c:c + 1], ssq[:, c:c + 1], 1.0 / DI, RMS_EPS, ALU.mult, ALU.add).then_inc(p1["rv"], 1)
                        wait(pool, p1["rv"], n + 1)
                        wait(pool, p1["x2"], C * a)
                        Q.tensor_tensor(rms[:, c:c + 1], msq[:, c:c + 1], neg_half[:, 0:1], ALU.pow).then_inc(p1["rms"], 1)
                norm_rstd(NB + 2 * a + 1)

            pool.wait_ge(p0["scaled"], 3 * NB)
            iter1(0)
            with pool.Fori(1, NB) as a:
                iter1(a)

            def iter2(a):
                tb = ts(a, C)
                hold(Q)
                Q.tensor_tensor(x[:, tb, :], x[:, tb, :], side[:, tb, :], ALU.add).then_inc(p2["xm"], 1)
                norm_rstd(3 * NB + a)
                wait(pool, p2["acc"], C * E * (a + 1))
                pool.dma_start(out[a], x[:, tb, :]).then_inc(out_stored, 16)

            pool.wait_ge(p0["mg"], NB)
            pool.wait_ge(ln_norm, 4 * 3 * NB)
            iter2(0)
            with pool.Fori(1, NB) as a:
                iter2(a)
            pool.wait_ge(out_stored, 16 * NB)


def kernel(**inputs):
    import numpy as np
    import concourse.bacc as bacc
    from concourse.bass_utils import run_bass_kernel_spmd

    v = {k: np.asarray(a) for k, a in inputs.items()}
    adj = np.ascontiguousarray(v["adj"].reshape(NB, BT, G, GJ, P).transpose(0, 2, 4, 3, 1))

    par = np.zeros((P, PARAMS), np.float32)

    def put(name, a, rows=P):
        lo, hi = COL[name]
        par[0:rows, lo:hi] = a

    idx = np.arange(P)
    put("ident", np.eye(P))
    put("upper", idx[None, :] >= idx[:, None])
    put("last", np.broadcast_to((idx == P - 1)[:, None], (P, P)))
    put("ones", np.ones((P, P)))
    put("pick", np.repeat(np.eye(NH), P, axis=1), NH)
    put("restart", np.broadcast_to(np.arange(BT) % P != 0, (NH, BT)), NH)
    put("g0_b", np.broadcast_to(v["L0_gnn_b"], (P, D)))
    put("bm", np.broadcast_to(v["L1_gnn_bm"], (P, D)))
    put("b_lin", np.broadcast_to(v["L0_ffn_b_lin"], (P, D)))
    put("br", np.broadcast_to(v["L1_ffn_br"], (P, E)))
    put("conv_w", v["L0_ffn_conv_w"].reshape(3, P, TAPS).transpose(1, 0, 2).reshape(P, 3 * TAPS))
    put("conv_b", v["L0_ffn_conv_b"].reshape(3, P).T)
    put("skip", np.repeat(v["L0_ffn_D"], HD).reshape(2, P).T)
    put("norm_w", v["L0_ffn_norm_w"].reshape(2, P).T)
    put("eps1", np.broadcast_to(v["L1_gnn_eps1"], (P, 1)))
    put("eps2", np.broadcast_to(v["L1_gnn_eps2"], (P, 1)))
    put("mlp1_b", v["L1_gnn_b1"].T)
    put("mlp2_b", v["L1_gnn_b2"].T)
    for name in ("g1", "be1", "m1", "v1", "b1", "g2", "be2", "m2", "v2", "b2"):
        put(name, v["L1_ffn_" + name].T)
    put("a_log", v["L0_ffn_A_log"][:, None], NH)
    put("dt_bias", v["L0_ffn_dt_bias"][:, None], NH)
    put("bo", v["L1_ffn_bo"], E)
    put("g0_w", v["L0_gnn_W"].T)
    put("w_in", v["L0_ffn_W_in"])
    put("w_out_t", v["L0_ffn_W_out"].T)
    put("w_lin", v["L0_ffn_W_lin"])
    put("mlp1_w", v["L1_gnn_W1"].transpose(2, 0, 1).reshape(D, 3 * D))
    put("mlp2_w", v["L1_gnn_W2"].transpose(2, 0, 1).reshape(D, 3 * D))
    put("wm", v["L1_gnn_Wm"].reshape(D, 2, D).transpose(2, 1, 0).reshape(D, 2 * D))
    put("wr", v["L1_ffn_Wr"])
    put("ew1", v["L1_ffn_W1"].transpose(1, 0, 2).reshape(D, E * D))
    put("ew2", v["L1_ffn_W2"].transpose(1, 0, 2).reshape(D, E * D))
    put("ewo", v["L1_ffn_Wo"].transpose(1, 0, 2).reshape(D, E * D))

    arrays = {"x_dram": np.ascontiguousarray(v["x"]), "x2_dram": np.ascontiguousarray(v["L1_gnn_x2"]),
              "adj_dram": adj, "par_dram": par}
    nc = bacc.Bacc("TRN2", target_bir_lowering=False, num_devices=1)
    args = [nc.dram_tensor(n, a.shape, mybir.dt.from_np(a.dtype), kind="ExternalInput").ap() for n, a in arrays.items()]
    res = nc.dram_tensor("out_dram", (NB, P, C, D), F32, kind="ExternalOutput").ap()
    build(nc, *args, res)
    r = run_bass_kernel_spmd(nc, [arrays], core_ids=[0])
    return np.ascontiguousarray(r.results[0]["out_dram"].transpose(0, 2, 1, 3).reshape(T, D))
```

```python
from contextlib import ExitStack

import concourse.bass as bass
from concourse import mybir

ALU = mybir.AluOpType
ACT = mybir.ActivationFunctionType
AX_X = mybir.AxisListType.X
F32 = mybir.dt.float32
F16 = mybir.dt.float16
BF16 = mybir.dt.bfloat16

T = 4096
D = 128
P = 128
NT = T // P
BT = 512
NB = T // BT
C = BT // P
GJ = 2
G = NT // GJ
SLOTS = 8
NBUF = 4
DI, DS, NH, HD = 256, 64, 4, 64
TAPS = 4
E = 8
LN_EPS, RMS_EPS, BN_EPS = 1e-5, 1e-5, 1e-3

KINDS = ["FQ" * 8, "FVFV" * 3 + "FQFV", "VVQV" * 4]
CHUNK_FILL = (2, 1, 2, 1, 1, 1, 0)
SUMS = G // 2
LEAD = 4
SPLITS = [sum(k != "F" for k in kinds) for kinds in KINDS]
assert all(n % NBUF == 0 for n in SPLITS) and all(k[-1] != "F" for k in KINDS)

_WIDTHS = [
    ("ident", P), ("barred", P), ("last", P), ("ones", P),
    ("g0_b", D), ("bm", D), ("b_lin", D), ("br", E),
    ("conv_w", 3 * TAPS), ("conv_b", 3), ("skip", 2), ("norm_w", 2), ("eps1", 1), ("eps2", 1),
    ("mlp1_b", 3), ("mlp2_b", 3),
    ("g1", E), ("be1", E), ("m1", E), ("v1", E), ("b1", E),
    ("g2", E), ("be2", E), ("m2", E), ("v2", E), ("b2", E),
    ("a_log", 1), ("dt_bias", 1), ("pick", NH), ("bo", D),
    ("g0_w", D), ("w_in", 2 * DI + 2 * DS + NH), ("w_out_t", DI), ("w_lin", D),
    ("mlp1_w", 3 * D), ("mlp2_w", 3 * D), ("wm", 2 * D), ("wr", E),
    ("ew1", E * D), ("ew2", E * D), ("ewo", E * D),
]
COL, _at = {}, 0
for _name, _w in _WIDTHS:
    COL[_name] = (_at, _at + _w)
    _at += _w
PARAMS = _at


def ts(i, n):
    return bass.ts(i, n)


def wait(eng, sem, value):
    if isinstance(value, int) and value <= 0:
        return
    eng.wait_ge(sem, value)


def build(nc, x_in, x2_in, adj_in, par_in, out):
    with ExitStack() as ctx:
        def sb(name, shape):
            return ctx.enter_context(nc.sbuf_tensor(name, shape, F32))

        def sbt(name, shape, dtype):
            return ctx.enter_context(nc.sbuf_tensor(name, shape, dtype))

        def bank(name):
            return ctx.enter_context(nc.psum_tensor(name, [P, BT], F32))

        def sem(name):
            return ctx.enter_context(nc.semaphore(name))

        par = sb("par", [P, PARAMS])
        ring = sb("ring", [P, SLOTS, GJ, BT])
        x = sb("x", [P, NT, D])
        halves = sbt("halves", [P, NBUF, 2, GJ, BT], F16)
        sup = sb("sup", [P, NT, D])
        feat = sb("feat", [P, NT, D])
        side = sb("side", [P, NT, D])
        dis = sb("dis", [P, NT])
        stats = sb("stats", [P, C, 6])
        mv = sb("mv", [P, C, 2])
        var = sb("var", [P, C])
        rstd = sb("rstd", [P, C])
        spare = sb("spare", [P, 128])
        neg_half = sb("neg_half", [P, 2 * E])
        xhat = sb("xhat", [P, C, D])
        xhat_t = sb("xhat_t", [P, BT])
        z_t = sb("z_t", [P, BT])
        work = sb("work", [P, 7, BT])
        part, pair, colsum = [work[:, 2 * k:2 * k + 2] for k in range(2)], work[:, 4:6], work[:, 6]
        wide = sb("wide", [P, 7, BT])
        deg = sb("deg", [P, C])
        dg = sb("dg", [P, 4, C])
        gain = sb("gain", [P, 2])
        hid = [wide[:, i] for i in range(3)]
        w_ol = sb("w_ol", [P, 2, D])
        skip_d = sb("skip_d", [P, 2, P])
        a_neg = sb("a_neg", [NH, 2])
        bn_s = sb("bn_s", [P, 2 * E])
        bn_f = sb("bn_f", [P, 2 * E])
        bn_t = sb("bn_t", [P, 3, 2 * E])
        xbc = [sb(f"xbc{k}", [P, TAPS - 1 + BT]) for k in range(3)]
        conv = [work[:, 2 * k:2 * k + 2] for k in range(3)]
        zs = wide[:, 0:2].rearrange("p a (b d) -> p (a b) d", b=2)
        xs = [wide[:, 2 + k] for k in range(2)]
        bs = wide[0:DS, 4]
        cs = wide[0:DS, 5]
        dt_row = wide[0:NH, 6]
        da_row = sb("da_row", [NH, BT])
        mid = sbt("mid", [NH, BT], BF16)
        rows = sbt("rows", [P, BT], BF16)
        pick = sbt("pick", [P, NH, P], BF16)
        unpick = sbt("unpick", [P, NH, P], BF16)
        ident16 = sbt("ident16", [P, P], BF16)
        barred = sbt("barred", [P, P], BF16)
        acum = work[0:NH, 6]
        cols = sb("cols", [P, 2, C, NH])
        dec = sb("dec", [P, 3, C * NH])
        dece = sb("dece", [P, 3, C * NH])
        decay = [sb(f"decay{i}", [P, NH, P]) for i in range(2)]
        xt = [sb(f"xt{i}", [P, DI + DS]) for i in range(2)]
        xdt = [sb(f"xdt{i}", [P, DI]) for i in range(2)]
        xdd = [sb(f"xdd{i}", [P, DI]) for i in range(2)]
        y = [sb(f"y{i}", [P, DI]) for i in range(2)]
        y2 = [sb(f"y2{i}", [P, DI]) for i in range(2)]
        y_t = [sb(f"y_t{i}", [P, DI]) for i in range(2)]
        ssq = sb("ssq", [P, C])
        msq = sb("msq", [P, C])
        rms = sb("rms", [P, C])
        state = sb("state", [DS, DI])
        lg = sb("lg", [P, 3, C, E])
        red = sb("red", [P, 3, C])
        gate = sb("gate", [P, C, E])
        gate_t = work[0:E, 6]
        h1 = [wide[:, 3 + i] for i in range(2)]
        h2 = [wide[:, 5 + i] for i in range(2)]

        def as_halves(t):
            return t[:].bitcast(F16).rearrange("p t (k d) -> p t k d", k=2)

        sup16, feat16 = as_halves(sup), as_halves(feat)
        x2_stage = wide[:, 0:4].rearrange("p a (b j d) -> p (a b) j d", b=2, j=GJ)
        fresh = decay[0]

        acc_ps = bank("acc_ps")
        tr_ps = bank("tr_ps")
        b2, b3, b4, b5, b6, b7 = (bank(f"b{i}_ps") for i in range(2, 8))

        def pc(name, lo=0, hi=None, rows=P):
            a, b = COL[name]
            return par[0:rows, a + lo:(a + hi if hi is not None else b)]

        ident = pc("ident")

        par_loaded = sem("par_loaded")
        x_loaded = sem("x_loaded")
        x2_loaded = sem("x2_loaded")
        x2_split = sem("x2_split")
        rows_set = sem("rows_set")
        adj_loaded = [sem(f"adj_loaded{q}") for q in range(SLOTS)]
        adj_used = sem("adj_used")
        split_used = sem("split_used")
        hi_done = sem("hi_done")
        lo_done = {"V": sem("lo_done_v"), "Q": sem("lo_done_q")}
        adj_summed = sem("adj_summed")
        out_stored = sem("out_stored")
        consts_set = sem("consts_set")
        prep_pe = sem("prep_pe")
        prep_dve = sem("prep_dve")
        prep_act = sem("prep_act")
        prep_pool = sem("prep_pool")
        ln_stats, ln_aggr, ln_var, ln_rstd, ln_norm = (sem(n) for n in ("ln_stats", "ln_aggr", "ln_var", "ln_rstd", "ln_norm"))
        names0 = "xt_ps deg_ps sup_ps mlp_ps mg_ps z_sb xt_sb h part colsum sup deg mg dis s32 shi slo sx sf".split()
        p0 = {n: sem("p0_" + n) for n in names0}
        names1 = ("z_sb zt_ps x1 xt_ps xt_sb proj_ps zp_ps xbc dtact dtexp dtln dtrow scan zs conv carry act cols_ps cols "
                  "end_ps dec dece xT_ps xT rb_ps ee gt_ps m rest mid rows xdt xdd y_ps y0 y y2 ssq rv rms yT_ps yT o_ps "
                  "x2 x1b st_ps stmul st fhi flo").split()
        p1 = {n: sem("p1_" + n) for n in names1}
        names2 = ("z_sb mlp_ps h mg_ps xm x3 xt_ps xt_sb gl_ps lg mx sub ex sum rcp gate gt_ps gt_sb gb_ps gb "
                  "w1_ps h1 w2_ps h2 wo_ps acc").split()
        p2 = {n: sem("p2_" + n) for n in names2}

        holds = []

        def hold(engine):
            at = len(holds)
            holds.append(at)
            o = spare[:, at:at + 1]
            if engine is nc.gpsimd:
                engine.tensor_tensor(o, neg_half[:, 0:1], neg_half[:, 1:2], ALU.add)
            else:
                engine.tensor_copy(o, neg_half[:, 0:1])

        def counted(ph, b, q, kinds):
            before = sum(NB * sum(k in kinds for k in KINDS[i]) for i in range(ph))
            return before + b * sum(k in kinds for k in KINDS[ph]) + sum(k in kinds for k in KINDS[ph][:q + 1])

        def strip_loaded(ph, b, q):
            return 16 * ((ph * NB + b) * (G // SLOTS) + q // SLOTS + 1)

        def wait_strip_freed(eng, ph, b, q):
            kind = KINDS[ph][q]
            if kind == "F":
                wait(eng, adj_used, counted(ph, b, q, "F"))
            else:
                wait(eng, lo_done[kind], counted(ph, b, q, kind))
            if ph == 0:
                wait(eng, adj_summed, G // 2 * b + q // 2 + 1)

        def block_done(ph, b):
            return counted(ph, b, G - 1, "VQ")

        def buffer(ph, q):
            return (counted(ph, 0, q, "VQ") - 1) % NBUF

        def make_hi(act, ph, b, lo, hi):
            for q in range(lo, hi):
                if KINDS[ph][q] == "F":
                    continue
                wait(act, adj_loaded[q % SLOTS], strip_loaded(ph, b, q))
                wait(act, split_used, counted(ph, b, q, "VQ") - NBUF)
                nc.scalar.activation(halves[:, buffer(ph, q), 0], ring[:, q % SLOTS], ACT.Copy).then_inc(hi_done, 1)

        def make_lo(eng, kind, ph, b, lo, hi):
            for q in range(lo, hi):
                if KINDS[ph][q] != kind:
                    continue
                wait(eng, adj_loaded[q % SLOTS], strip_loaded(ph, b, q))
                wait(eng, hi_done, counted(ph, b, q, "VQ"))
                eng.tensor_tensor(halves[:, buffer(ph, q), 1], ring[:, q % SLOTS], halves[:, buffer(ph, q), 0],
                                  ALU.subtract).then_inc(lo_done[kind], 1)

        block = ctx.enter_context(nc.Block())

        @block.sync
        def _(sp):
            x2v = x2_in.rearrange("(s e j p) d -> p s e j d", p=P, j=GJ, e=2)
            featv = feat[:].rearrange("p (s e j) d -> p s e j d", e=2, j=GJ)
            stagev = x2_stage

            def load(ph, b):
                for q in range(G):
                    if q >= SLOTS:
                        wait_strip_freed(sp, ph, b, q - SLOTS)
                    elif not isinstance(b, int) or b > 0:
                        wait_strip_freed(sp, ph, b - 1, q + G - SLOTS)
                    elif ph > 0:
                        wait_strip_freed(sp, ph - 1, NB - 1, q + G - SLOTS)
                    sp.dma_start(ring[:, q % SLOTS], adj_in[b, q]).then_inc(adj_loaded[q % SLOTS], 16)
                    if ph == 0 and isinstance(b, int) and q == 0:
                        for j in range(GJ):
                            sp.dma_start(featv[:, :, 0, j], x2v[:, :, 0, j]).then_inc(x2_loaded, 16)
                            sp.dma_start(stagev[:, :, j], x2v[:, :, 1, j]).then_inc(x2_loaded, 16)

            for ph in range(3):
                load(ph, 0)
                with sp.Fori(1, NB) as b:
                    load(ph, b)

        @block.tensor
        def _(pe):
            def mm(o, l, r, start=True, stop=True, **k):
                return nc.tensor.matmul(o, l, r, start=start, stop=stop, **k)

            def adjacency(ph, b, lo, hi, stationary, halved, free_sem):
                for q in range(lo, hi):
                    if q == 0:
                        wait(pe, free_sem, b)
                    split = KINDS[ph][q] != "F"
                    if split:
                        wait(pe, lo_done[KINDS[ph][q]], counted(ph, b, q, KINDS[ph][q]))
                    else:
                        wait(pe, adj_loaded[q % SLOTS], strip_loaded(ph, b, q))
                    for j in range(GJ):
                        i = q * GJ + j
                        first, last = i == 0, i == NT - 1
                        if not split:
                            ins = mm(acc_ps[:], stationary[:, i, :], ring[:, q % SLOTS, j, :], start=first, stop=last)
                            continue
                        hi_lo = halves[:, buffer(ph, q)]
                        mm(acc_ps[:], halved[:, i, 0, :], hi_lo[:, 0, j, :], start=first, stop=False)
                        mm(acc_ps[:], halved[:, i, 0, :], hi_lo[:, 1, j, :], start=False, stop=False)
                        ins = mm(acc_ps[:], halved[:, i, 1, :], hi_lo[:, 0, j, :], start=False, stop=last)
                    ins.then_inc(split_used if split else adj_used, 1)

            def transposes(src, dst, n, done):
                for c in range(n):
                    ins = nc.tensor.transpose(dst[:, c * P:(c + 1) * P], src(c), ident)
                ins.then_inc(done, 1)

            pe.wait_ge(par_loaded, 16)
            for k in range(2):
                ins = mm(b2[:, k * P:(k + 1) * P], pc("w_out_t", k * P, (k + 1) * P), pc("w_lin"))
            ins.then_inc(prep_pe, 1)

            def iter0(b, here, before):
                if here:
                    wait(pe, ln_norm, 4 * (b + 1))
                    transposes(lambda c: xhat[:, c, :], tr_ps, C, p0["xt_ps"])
                if before:
                    wait(pe, p0["colsum"], SUMS * b)
                    wait(pe, p0["deg"], b - 1)
                    for c in range(C):
                        ins = mm(b5[:, c:c + 1], colsum[:, c * P:(c + 1) * P], pc("ones", 0, 1))
                    ins.then_inc(p0["deg_ps"], 1)
                if here:
                    adjacency(0, b, 0, 4, feat, feat16, p0["z_sb"])
                    wait(pe, p0["xt_sb"], b + 1)
                    wait(pe, p0["sup"], b)
                    for c in range(C):
                        ins = mm(b3[:, c * D:(c + 1) * D], xhat_t[:, c * P:(c + 1) * P], pc("g0_w"))
                    ins.then_inc(p0["sup_ps"], 1)
                for l in range(3):
                    if before:
                        if l == 0:
                            wait(pe, p0["z_sb"], b)
                            wait(pe, p0["h"], 3 * (b - 1))
                        else:
                            wait(pe, p0["h"], 3 * (b - 1) + l)
                        mm(b2[:], pc("mlp2_w", l * D, (l + 1) * D), z_t[:] if l == 0 else hid[l - 1][:]).then_inc(p0["mlp_ps"], 1)
                    if here:
                        adjacency(0, b, 4 * l + 4, 4 * l + (8 if l < 2 else 6), feat, feat16, None)
                if before:
                    wait(pe, p0["h"], 3 * b)
                    wait(pe, p0["mg"], b - 1)
                    for c in range(C):
                        ins = mm(b4[:, c * D:(c + 1) * D], hid[2][:, c * P:(c + 1) * P], pc("wm", D, 2 * D))
                    ins.then_inc(p0["mg_ps"], 1)
                if here:
                    adjacency(0, b, 14, 16, feat, feat16, None)

            pe.wait_ge(x2_loaded, 64)
            pe.wait_ge(x2_split, 4)
            iter0(0, True, False)
            iter0(1, True, True)
            with pe.Fori(2, NB) as b:
                iter0(b, True, True)
            iter0(NB, False, True)

            pe.wait_ge(p0["sf"], NB)
            pe.wait_ge(p0["slo"], NB)
            pe.wait_ge(p0["mg"], NB)
            pe.wait_ge(rows_set, 5)
            pe.wait_ge(prep_dve, 7)
            pe.wait_ge(prep_pool, 8)

            def chunk_scores(a, c):
                n = C * a + c
                wait(pe, p1["act"], 4 * a + 4)
                wait(pe, p1["xT"], n)
                if c == 0:
                    wait(pe, p1["xbc"], 3 * a + 3)
                cc = slice(c * P, (c + 1) * P)
                for k in range(2):
                    nc.tensor.transpose(b4[:, k * P:(k + 1) * P], xs[k][:, cc], ident)
                nc.tensor.transpose(b4[:, DI:DI + DS], bs[:, cc], pc("ident", 0, DS, rows=DS)).then_inc(p1["xT_ps"], 1)
                wait(pe, p1["ee"], n)
                wait(pe, p1["dec"], 3 * a + 3)
                wait(pe, p1["rows"], 3 * a + 3)
                mm(b5[:].rearrange("p (h l) -> p h l", h=NH), ident16[:], barred[:].unsqueeze(1).broadcast_to([P, NH, P]),
                   skip_group_check=True)
                for h in range(NH):
                    mm(b5[:, h * P:(h + 1) * P], pick[:, h, :], rows[:, cc], start=False, stop=False, skip_group_check=True)
                    ins = mm(b5[:, h * P:(h + 1) * P], rows[:, cc], unpick[:, h, :], start=False, stop=(h == NH - 1),
                             skip_group_check=True)
                ins.then_inc(p1["rb_ps"], 1)
                wait(pe, p1["m"], n)
                mm(b2[:, 0:P], bs[:, cc], cs[:, cc]).then_inc(p1["gt_ps"], 1)

            def chunk_outputs(a, c):
                n = C * a + c
                i = c % 2
                cc = slice(c * P, (c + 1) * P)
                wait(pe, p1["xdd"], n + 1)
                wait(pe, p1["st"], n)
                mm(b3[0:DS, 0:DI], xt[i][:, DI:DI + DS], xdd[i][:]).then_inc(p1["st_ps"], 1)
                wait(pe, p1["y"], n)
                wait(pe, p1["zs"], 2 * a + 2)
                mm(b6[:, DI:2 * DI], cs[:, cc], state[:], skip_group_check=True)
                for k in range(2):
                    mm(b6[:, k * P:(k + 1) * P], xs[k][:, cc], skip_d[:, k, :], start=False, stop=False,
                       skip_group_check=True)
                wait(pe, p1["m"], n + 1)
                wait(pe, p1["xdt"], n + 1)
                for h in range(NH):
                    ins = mm(b6[:, h * HD:(h + 1) * HD], decay[i][:, h, :], xdt[i][:, h * HD:(h + 1) * HD],
                             start=False, stop=(h == NH - 1), skip_group_check=True)
                ins.then_inc(p1["y_ps"], 1)

            def chunk_turn(a, c):
                n = C * a + c
                wait(pe, p1["y2"], n + 1)
                wait(pe, p1["yT"], n)
                for k in range(2):
                    ins = nc.tensor.transpose(b7[:, k * P:(k + 1) * P], y2[c % 2][:, k * P:(k + 1) * P], ident)
                ins.then_inc(p1["yT_ps"], 1)

            def chunk_project(a, c):
                n = C * a + c
                wait(pe, p1["yT"], n + 1)
                wait(pe, p1["x2"], n)
                for k in range(2):
                    ins = mm(tr_ps[:, 0:D], y_t[c % 2][:, k * P:(k + 1) * P], w_ol[:, k, :], start=(k == 0), stop=(k == 1))
                ins.then_inc(p1["o_ps"], 1)

            def iter1(b, here, before):
                a = b - 1
                if before:
                    wait(pe, p1["z_sb"], b)
                    wait(pe, p1["x2"], C * a)
                    transposes(lambda c: z_t[:, c * P:(c + 1) * P], tr_ps, C, p1["zt_ps"])
                if here:
                    adjacency(1, b, 0, 2, sup, sup16, p1["z_sb"])
                if before:
                    wait(pe, ln_norm, 4 * (NB + 2 * a + 1))
                    transposes(lambda c: xhat[:, c, :], tr_ps, C, p1["xt_ps"])
                if here:
                    adjacency(1, b, 2, 3, sup, sup16, None)
                if before:
                    wait(pe, p1["xt_sb"], b)
                    wait(pe, p1["ee"], C * a)
                    mm(b5[0:NH, :], pc("w_in", 2 * DI + 2 * DS, 2 * DI + 2 * DS + NH), xhat_t[:]).then_inc(p1["proj_ps"], 1)
                    wait(pe, p1["m"], C * a)
                    wait(pe, p1["st"], C * a)
                    wait(pe, p1["xT"], C * a)
                    for k, bk in enumerate((b2, b3, b4)):
                        mm(bk[:], pc("w_in", DI + k * P, DI + (k + 1) * P), xhat_t[:]).then_inc(p1["proj_ps"], 1)
                    wait(pe, p1["y"], C * a)
                    wait(pe, p1["yT"], C * a)
                    for c in range(C):
                        bk = (b6, b7)[c // 2]
                        ins = mm(bk[:, c % 2 * DI:(c % 2 + 1) * DI], xhat_t[:, c * P:(c + 1) * P], pc("w_in", 0, DI))
                        if c % 2:
                            ins.then_inc(p1["zp_ps"], 1)
                if here:
                    adjacency(1, b, 3, 6, sup, sup16, None)
                if before:
                    wait(pe, p1["scan"], C * b)
                    wait(pe, p1["dtact"], 2 * b)
                    mm(b5[:, BT - 1:BT], ident, pc("ones", 0, 1))
                    for k, src in enumerate((acum, dt_row[:])):
                        for c in range(C):
                            ins = nc.tensor.transpose(b5[:, (k * C + c) * NH:(k * C + c + 1) * NH],
                                                      src[:, c * P:(c + 1) * P], pc("ident", 0, NH, rows=NH))
                    ins.then_inc(p1["cols_ps"], 1)
                if here:
                    adjacency(1, b, 6, 7, sup, sup16, None)
                if before:
                    wait(pe, p1["cols"], b)
                    mm(b5[:, 0:C * NH], pc("last"), cols[:, 0, :, :].rearrange("p c h -> p (c h)")).then_inc(p1["end_ps"], 1)
                if here:
                    adjacency(1, b, 7, 8, sup, sup16, None)
                fill = 8
                for step in range(C + 3):
                    if before:
                        if step >= 3:
                            chunk_project(a, step - 3)
                        if 0 <= step - 2 < C:
                            chunk_turn(a, step - 2)
                        if 0 <= step - 1 < C:
                            chunk_outputs(a, step - 1)
                        if step < C:
                            chunk_scores(a, step)
                    if here:
                        n = CHUNK_FILL[step]
                        adjacency(1, b, fill, fill + n, sup, sup16, None)
                        fill += n

            iter1(0, True, False)
            iter1(1, True, True)
            with pe.Fori(2, NB) as b:
                iter1(b, True, True)
            iter1(NB, False, True)

            pe.wait_ge(p1["flo"], NB)
            pe.wait_ge(p1["x2"], C * NB)

            def expert_in(a, e):
                n = E * a + e
                wait(pe, p2["h1"], n - 1 if e else n)
                mm((b4, b5)[e % 2][:], pc("ew1", e * D, (e + 1) * D), xhat_t[:]).then_inc(p2["w1_ps"], 1)

            def expert_mid(a, e):
                n = E * a + e
                wait(pe, p2["h1"], n + 1)
                wait(pe, p2["h2"], n)
                mm(b6[:], pc("ew2", e * D, (e + 1) * D), h1[e % 2][:]).then_inc(p2["w2_ps"], 1)

            def expert_out(a, e):
                n = E * a + e
                wait(pe, p2["h2"], n + 1)
                wait(pe, p2["acc"], C * n)
                for c in range(C):
                    ins = mm(b7[:, c * D:(c + 1) * D], h2[e % 2][:, c * P:(c + 1) * P], pc("ewo", e * D, (e + 1) * D))
                ins.then_inc(p2["wo_ps"], 1)

            def iter2(b, here, before):
                a = b - 1
                at = 0

                def fill(n):
                    nonlocal at
                    if here:
                        adjacency(2, b, at, at + n, feat, feat16, p2["z_sb"])
                        at += n

                fill(1)
                if before:
                    for l in range(3):
                        wait(pe, p2["z_sb"], b) if l == 0 else wait(pe, p2["h"], 3 * a + l)
                        wait(pe, p2["h"], 3 * a + l)
                        mm(b2[:], pc("mlp1_w", l * D, (l + 1) * D), z_t[:] if l == 0 else hid[l - 1][:]).then_inc(p2["mlp_ps"], 1)
                        fill(1)
                    wait(pe, p2["h"], 3 * b)
                    wait(pe, p2["gb"], a)
                    for c in range(C):
                        ins = mm(b3[:, c * D:(c + 1) * D], hid[2][:, c * P:(c + 1) * P], pc("wm", 0, D))
                    ins.then_inc(p2["mg_ps"], 1)
                    fill(2)
                    wait(pe, ln_norm, 4 * (3 * NB + b))
                    transposes(lambda c: xhat[:, c, :], tr_ps, C, p2["xt_ps"])
                    fill(1)
                    wait(pe, p2["xt_sb"], b)
                    for c in range(C):
                        ins = mm(b3[:, c * E:(c + 1) * E], xhat_t[:, c * P:(c + 1) * P], pc("wr"))
                    ins.then_inc(p2["gl_ps"], 1)
                    for e in range(E + 2):
                        if e < E:
                            expert_in(a, e)
                        if 0 <= e - 1 < E:
                            expert_mid(a, e - 1)
                        if e == 1:
                            wait(pe, p2["gate"], b)
                            for c in range(C):
                                ins = nc.tensor.transpose(b3[0:E, c * P:(c + 1) * P], gate[:, c, :], ident)
                            ins.then_inc(p2["gt_ps"], 1)
                        if e == 2:
                            wait(pe, p2["gt_sb"], b)
                            for c in range(C):
                                ins = mm(b3[:, c * D:(c + 1) * D], gate_t[:, c * P:(c + 1) * P], pc("bo", rows=E))
                            ins.then_inc(p2["gb_ps"], 1)
                        if e >= 2:
                            expert_out(a, e - 2)
                        fill(1 if e < 9 else 0)
                else:
                    fill(G - at)
                if here:
                    assert at == G, at

            iter2(0, True, False)
            iter2(1, True, True)
            with pe.Fori(2, NB) as b:
                iter2(b, True, True)
            iter2(NB, False, True)

        @block.scalar
        def _(act):
            A = nc.scalar.activation
            act.dma_start(x[:], x_in.rearrange("(t p) d -> p t d", p=P)).then_inc(x_loaded, 16)
            act.dma_start(par[:], par_in).then_inc(par_loaded, 16)
            act.wait_ge(par_loaded, 16)
            A(a_neg[:, 0:1], pc("a_log", rows=NH), ACT.Exp).then_inc(prep_act, 1)
            act.wait_ge(prep_dve, 2)

            def iter0(b, here, before, upcoming):
                if before:
                    wait(act, split_used, block_done(0, b - 1))
                    wait(act, p0["mlp_ps"], 3 * (b - 1))
                    A(z_t[:], acc_ps[:], ACT.Identity, scale=gain[:, 1:2]).then_inc(p0["z_sb"], 1)
                if here:
                    wait(act, p0["xt_ps"], b + 1)
                    wait(act, p0["sup_ps"], b)
                    A(xhat_t[:], tr_ps[:], ACT.Copy).then_inc(p0["xt_sb"], 1)
                    make_hi(act, 0, b, LEAD, 4 + LEAD)
                for l in range(3):
                    if before:
                        wait(act, p0["mlp_ps"], 3 * (b - 1) + l + 1)
                        if l == 2:
                            wait(act, p0["mg_ps"], b - 1)
                        A(hid[l][:], b2[:], ACT.Relu, bias=pc("mlp2_b", l, l + 1)).then_inc(p0["h"], 1)
                    if here and l < 2:
                        make_hi(act, 0, b, 4 * l + 4 + LEAD, 4 * l + 8 + LEAD)
                if before:
                    a = b - 1
                    wait(act, p0["dis"], 5 * a + 5)
                    wait(act, p0["sx"], 2 * a)
                    wait(act, p0["slo"], a)
                    for c in range(C):
                        A(fresh[:, c, :], sup[:, 4 * a + c, :], ACT.Copy, scale=dis[:, ts(4 * a + c, 1)]).then_inc(p0["s32"], 1)
                    wait(act, p0["s32"], 4 * a + 4)
                    A(sup[:, ts(2 * a, GJ), :], fresh[:, 0:GJ, :], ACT.Copy).then_inc(p0["sf"], 1)
                    A(sup16[:, ts(2 * a + 1, GJ), 0, :], fresh[:, GJ:, :], ACT.Copy).then_inc(p0["shi"], 1)
                if upcoming:
                    make_hi(act, *upcoming, 0, LEAD)

            make_hi(act, 0, 0, 0, LEAD)
            iter0(0, True, False, (0, 1))
            iter0(1, True, True, (0, 2))
            with act.Fori(2, NB - 1) as b:
                iter0(b, True, True, (0, b + 1))
            iter0(NB - 1, True, True, (1, 0))
            iter0(NB, False, True, None)

            at = [sum(CHUNK_FILL[:k]) + 8 for k in range(C + 3)]

            def iter1(b, here, upcoming):
                a = b - 1

                def hi(lo, hi):
                    if here:
                        make_hi(act, 1, b, lo, hi)

                wait(act, split_used, block_done(1, a))
                wait(act, p1["zt_ps"], a)
                if isinstance(b, int) and b == 1:
                    wait(act, p0["mlp_ps"], 3 * NB)
                A(z_t[:], acc_ps[:], ACT.Copy).then_inc(p1["z_sb"], 1)
                wait(act, p1["xt_ps"], b)
                wait(act, p1["zp_ps"], 2 * a)
                if isinstance(b, int) and b == 1:
                    wait(act, p0["sup_ps"], NB)
                A(xhat_t[:], tr_ps[:], ACT.Copy).then_inc(p1["xt_sb"], 1)
                hi(LEAD, 6)
                dtb = pc("dt_bias", rows=NH)
                wait(act, p1["proj_ps"], 4 * a + 1)
                wait(act, p1["cols_ps"], a)
                A(dt_row[:], b5[0:NH, :], ACT.Relu, bias=dtb).then_inc(p1["dtact"], 1)
                A(da_row[:], b5[0:NH, :], ACT.Abs, bias=dtb).then_inc(p1["dtact"], 1)
                for k, bk in enumerate((b2, b3, b4)):
                    wait(act, p1["proj_ps"], 4 * a + k + 2)
                    wait(act, p1["carry"], 3 * (a + 1))
                    A(xbc[k][:, TAPS - 1:], bk[:], ACT.Copy).then_inc(p1["xbc"], 1)
                hi(6, 7)
                wait(act, p1["dtact"], 2 * b)
                A(da_row[:], da_row[:], ACT.Exp, scale=-1.0).then_inc(p1["dtexp"], 1)
                wait(act, p1["dtexp"], b)
                A(da_row[:], da_row[:], ACT.Ln, bias=1.0).then_inc(p1["dtln"], 1)
                for k, bk in enumerate((b6, b7)):
                    wait(act, p1["zp_ps"], 2 * a + k + 1)
                    wait(act, p1["y2"], C * a)
                    A(zs[:, 2 * k:2 * k + 2, :].rearrange("p c d -> p (c d)"), bk[:], ACT.Silu).then_inc(p1["zs"], 1)
                hi(7, 9)
                wait(act, p1["mid"], b)
                A(rows[32:32 + NH, :], mid[:], ACT.Copy).then_inc(p1["rows"], 1)
                wait(act, p1["y_ps"], C * a)
                wait(act, p1["st_ps"], C * a)
                for k in range(2):
                    wait(act, p1["conv"], 12 * a + 9 + k + 1)
                    A(xs[k][:], conv[k][:, 1, :], ACT.Silu, bias=pc("conv_b", k, k + 1)).then_inc(p1["act"], 1)
                wait(act, p1["conv"], 12 * a + 12)
                cb = pc("conv_b", 2, 3)
                A(bs[:], conv[2][0:DS, 1, :], ACT.Silu, bias=cb[0:DS, :]).then_inc(p1["act"], 1)
                A(cs[:], conv[2][DS:2 * DS, 1, :], ACT.Silu, bias=cb[DS:2 * DS, :]).then_inc(p1["act"], 1)
                hi(9, at[0] + 2)
                wait(act, p1["dec"], 3 * b)
                A(dece[:], dec[:], ACT.Exp).then_inc(p1["dece"], 1)
                for step in range(C + 2):
                    if step < C:
                        c, n, i = step, C * a + step, step % 2
                        wait(act, p1["xT_ps"], n + 1)
                        wait(act, p1["st_ps"], n - 1)
                        A(xt[i][:], b4[:, 0:DI + DS], ACT.Copy).then_inc(p1["xT"], 1)
                        wait(act, p1["rb_ps"], n + 1)
                        wait(act, p1["y_ps"], n - 1)
                        if c == 0:
                            wait(act, p1["flo"], a)
                            wait(act, p1["fhi"], a)
                        A(decay[i][:].rearrange("p h l -> p (h l)"), b5[:], ACT.Exp).then_inc(p1["ee"], 1)
                    if step >= 2:
                        c, n, i = step - 2, C * a + step - 2, step % 2
                        wait(act, p1["y2"], n + 1)
                        wait(act, p1["ssq"], n)
                        wait(act, p1["o_ps"], n - 1)
                        A(y_t[i][:], y2[i][:], ACT.Square, accum_out=ssq[:, c:c + 1]).then_inc(p1["ssq"], 1)
                        wait(act, p1["yT_ps"], n + 1)
                        wait(act, p1["ssq"], n + 1)
                        A(y_t[i][:], b7[:, 0:DI], ACT.Copy).then_inc(p1["yT"], 1)
                    hi(min(at[step] + 2, G), min(at[step + 1] + 2, G))
                if upcoming:
                    make_hi(act, *upcoming, 0, LEAD)
                wait(act, ln_norm, 4 * (NB + 2 * a + 2))
                A(feat16[:, ts(a, C), 0, :], fresh[:], ACT.Copy).then_inc(p1["fhi"], 1)

            make_hi(act, 1, 0, LEAD, G)
            make_hi(act, 1, 1, 0, LEAD)
            act.wait_ge(p1["carry"], 3)
            iter1(1, True, (1, 2))
            with act.Fori(2, NB - 1) as b:
                iter1(b, True, (1, b + 1))
            iter1(NB - 1, True, (2, 0))
            iter1(NB, False, None)

            def iter2(b, here, upcoming):
                a = b - 1

                def hi(lo, hi):
                    if here:
                        make_hi(act, 2, b, lo, hi)

                wait(act, split_used, block_done(2, a))
                wait(act, p2["mlp_ps"], 3 * a)
                A(z_t[:], acc_ps[:], ACT.Identity, scale=gain[:, 0:1]).then_inc(p2["z_sb"], 1)
                for l in range(3):
                    wait(act, p2["mlp_ps"], 3 * a + l + 1)
                    if l == 2:
                        wait(act, p2["mg_ps"], a)
                    A(hid[l][:], b2[:], ACT.Relu, bias=pc("mlp1_b", l, l + 1)).then_inc(p2["h"], 1)
                    hi(LEAD + l, LEAD + l + 1)
                hi(LEAD + 3, 9)
                wait(act, p2["xt_ps"], b)
                wait(act, p2["w1_ps"], E * a)
                A(xhat_t[:], tr_ps[:], ACT.Copy).then_inc(p2["xt_sb"], 1)
                hi(9, 10)
                wait(act, p2["sub"], b)
                A(lg[:, 2], lg[:, 1], ACT.Exp).then_inc(p2["ex"], 1)
                for e in range(E + 1):
                    if e < E:
                        n = E * a + e
                        wait(act, p2["w1_ps"], n + 1)
                        wait(act, p2["w2_ps"], n - 1)
                        A(h1[e % 2][:], (b4, b5)[e % 2][:], ACT.Relu, scale=bn_s[:, e:e + 1], bias=bn_f[:, e:e + 1]).then_inc(p2["h1"], 1)
                    hi(10 + e, min(11 + e, G))
                    if e >= 1:
                        n = E * a + e - 1
                        wait(act, p2["w2_ps"], n + 1)
                        wait(act, p2["wo_ps"], n - 1)
                        A(h2[(e - 1) % 2][:], b6[:], ACT.Relu, scale=bn_s[:, E + e - 1:E + e], bias=bn_f[:, E + e - 1:E + e]).then_inc(p2["h2"], 1)
                if upcoming:
                    make_hi(act, *upcoming, 0, LEAD)

            act.wait_ge(prep_pool, 8)
            make_hi(act, 2, 0, LEAD, G)
            make_hi(act, 2, 1, 0, LEAD)
            iter2(1, True, (2, 2))
            with act.Fori(2, NB - 1) as b:
                iter2(b, True, (2, b + 1))
            iter2(NB - 1, True, None)
            iter2(NB, False, None)

        @block.vector
        def _(dve):
            V = nc.vector

            def norm_stats(n, tile):
                wait(dve, ln_aggr, 4 * n)
                hold(V)
                for c in range(C):
                    V.bn_stats(stats[:, c, :], tile(c)).then_inc(ln_stats, 1)
                wait(dve, ln_norm, 4 * n)
                wait(dve, ln_stats, 4 * n + 4)
                hold(V)
                for c in range(C):
                    V.bn_aggr(mv[:, c, :], stats[:, c, :]).then_inc(ln_aggr, 1)

            def norm_apply(n, tile, dst):
                wait(dve, ln_rstd, n + 1)
                for c in range(C):
                    V.tensor_scalar(dst(c), tile(c), mv[:, c, 0:1], rstd[:, c:c + 1], ALU.subtract, ALU.mult).then_inc(ln_norm, 1)

            V.memset(neg_half[:], -0.5).then_inc(consts_set, 1)
            V.memset(state[:], 0.0).then_inc(consts_set, 1)
            dve.wait_ge(consts_set, 2)
            dve.wait_ge(par_loaded, 16)
            V.tensor_scalar(gain[:, 0:1], pc("eps1"), 1.0, 1.0, ALU.add, ALU.add).then_inc(prep_dve, 1)
            V.tensor_scalar(gain[:, 1:2], pc("eps2"), 1.0, 1.0, ALU.add, ALU.add).then_inc(prep_dve, 1)
            dve.wait_ge(x2_loaded, 64)
            odd = feat16.rearrange("p (s e j) k d -> p s e j k d", e=2, j=GJ)[:, :, 1]
            for j in range(GJ):
                V.tensor_copy(odd[:, :, j, 0], x2_stage[:, :, j]).then_inc(x2_split, 1)
            dve.wait_ge(x2_split, 2)
            for j in range(GJ):
                V.tensor_tensor(odd[:, :, j, 1], x2_stage[:, :, j], odd[:, :, j, 0], ALU.subtract).then_inc(x2_split, 1)
            dve.wait_ge(x_loaded, 16)
            norm_stats(0, lambda c: x[:, c, :])
            norm_apply(0, lambda c: x[:, c, :], lambda c: xhat[:, c, :])
            dve.wait_ge(prep_act, 1)
            V.tensor_scalar(a_neg[:, 1:2], a_neg[:, 0:1], -1.0, None, ALU.mult).then_inc(prep_dve, 1)
            for k in range(2):
                V.tensor_scalar(skip_d[:, k, :], ident, pc("skip", k, k + 1), None, ALU.mult).then_inc(prep_dve, 1)
            dve.wait_ge(prep_pe, 1)
            for k in range(2):
                V.tensor_scalar(w_ol[:, k, :], b2[:, k * P:(k + 1) * P], pc("norm_w", k, k + 1), None, ALU.mult).then_inc(prep_dve, 1)

            V.memset(rows[:], 0.0).then_inc(rows_set, 1)
            V.tensor_copy(pick[:], pc("pick").unsqueeze(2).broadcast_to([P, NH, P])).then_inc(rows_set, 1)
            V.tensor_scalar(unpick[:], pc("pick").unsqueeze(2).broadcast_to([P, NH, P]), -1.0, None, ALU.mult).then_inc(rows_set, 1)
            V.tensor_copy(ident16[:], ident).then_inc(rows_set, 1)
            V.tensor_copy(barred[:], pc("barred")).then_inc(rows_set, 1)

            def rows4(ap):
                return ap[:].rearrange("p (c d) -> p c d", c=C)

            def bias4(name):
                return pc(name).unsqueeze(1).broadcast_to([P, C, D])

            def iter0(b, here, before, follows):
                if before:
                    wait(dve, p0["deg_ps"], b)
                    wait(dve, p0["dis"], 5 * (b - 1))
                    V.tensor_scalar(deg[:], b5[:, 0:C], 1.0, None, ALU.add).then_inc(p0["deg"], 1)
                if here:
                    for k in range(G // 2):
                        for q in (2 * k, 2 * k + 1):
                            wait(dve, adj_loaded[q % SLOTS], strip_loaded(0, b, q))
                        dst = part[k % 2] if k else pair
                        wait(dve, p0["colsum"], SUMS * b + max(k - 2, 0))
                        s0 = 2 * k % SLOTS
                        V.tensor_tensor(dst, ring[:, s0], ring[:, s0 + 1], ALU.add).then_inc(adj_summed, 1)
                        if k:
                            wait(dve, adj_summed, G // 2 * b + k + 1)
                            wait(dve, p0["colsum"], SUMS * b + k - 1)
                            V.tensor_tensor(pair, pair, part[k % 2], ALU.add).then_inc(p0["colsum"], 1)
                        if k == 1 and follows:
                            norm_stats(b + 1, lambda c: x[:, 4 * (b + 1) + c, :])
                        if k == 2:
                            wait(dve, p0["sup_ps"], b + 1)
                            V.tensor_tensor(sup[:, ts(b, C), :], rows4(b3), bias4("g0_b"), ALU.add).then_inc(p0["sup"], 1)
                        if k == 5 and follows:
                            wait(dve, p0["xt_ps"], b + 1)
                            norm_apply(b + 1, lambda c: x[:, 4 * (b + 1) + c, :], lambda c: xhat[:, c, :])
                    wait(dve, p0["colsum"], SUMS * b + SUMS - 1)
                    wait(dve, p0["deg_ps"], b)
                    V.tensor_tensor(colsum, pair[:, 0], pair[:, 1], ALU.add).then_inc(p0["colsum"], 1)
                if before:
                    a = b - 1
                    wait(dve, p0["mg_ps"], b)
                    V.tensor_tensor(side[:, ts(a, C), :], rows4(b4), bias4("bm"), ALU.add).then_inc(p0["mg"], 1)
                    wait(dve, p0["shi"], b)
                    odd = ts(2 * a + 1, GJ)
                    V.tensor_tensor(sup16[:, odd, 1, :], fresh[:, GJ:, :], sup16[:, odd, 0, :], ALU.subtract).then_inc(p0["slo"], 1)

            iter0(0, True, False, True)
            iter0(1, True, True, True)
            with dve.Fori(2, NB - 1) as b:
                iter0(b, True, True, True)
            iter0(NB - 1, True, True, False)
            iter0(NB, False, True, False)

            for k in range(3):
                V.memset(xbc[k][:, 0:TAPS - 1], 0.0).then_inc(p1["carry"], 1)

            def iter1(b, here, upcoming):
                a = b - 1
                t0 = 4 * a

                def lo(q0, q1):
                    if here:
                        make_lo(dve, "V", 1, b, q0, q1)

                wait(dve, p1["zt_ps"], a + 1)
                if isinstance(a, int) and a == 0:
                    dve.wait_ge(p0["sx"], 2 * NB)
                for c in range(C):
                    V.scalar_tensor_tensor(out=x[:, t0 + c, :], in0=tr_ps[:, c * P:(c + 1) * P], scalar=dis[:, ts(t0 + c, 1)],
                                           in1=x[:, t0 + c, :], op0=ALU.mult, op1=ALU.add).then_inc(p1["x1"], 1)
                wait(dve, p1["x1"], 4 * a + 4)
                n = NB + 2 * a
                norm_stats(n, lambda c: x[:, t0 + c, :])
                norm_apply(n, lambda c: x[:, t0 + c, :], lambda c: xhat[:, c, :])
                lo(LEAD, 6)
                for j in range(TAPS):
                    for k in range(3):
                        wait(dve, p1["xbc"], 3 * a + k + 1)
                        w = pc("conv_w", k * TAPS + j, k * TAPS + j + 1)
                        src = xbc[k][:, j:j + BT]
                        if j == 0:
                            wait(dve, p1["conv"], 12 * a)
                            wait(dve, p1["act"], 4 * a)
                            V.tensor_scalar(conv[k][:, 0, :], src, w, None, ALU.mult).then_inc(p1["conv"], 1)
                        else:
                            wait(dve, p1["conv"], 12 * a + 3 * (j - 1) + k + 1)
                            V.scalar_tensor_tensor(out=conv[k][:, j % 2, :], in0=src, scalar=w, in1=conv[k][:, (j - 1) % 2, :],
                                                   op0=ALU.mult, op1=ALU.add).then_inc(p1["conv"], 1)
                    if j == 1:
                        wait(dve, p1["dtln"], a + 1)
                        wait(dve, p1["cols_ps"], a)
                        V.tensor_tensor(dt_row[:], dt_row[:], da_row[:], ALU.add).then_inc(p1["dtrow"], 1)
                        wait(dve, p1["dtrow"], 2 * a + 1)
                        V.tensor_scalar(da_row[:], dt_row[:], a_neg[:, 1:2], None, ALU.mult).then_inc(p1["dtrow"], 1)
                        wait(dve, p1["dtrow"], 2 * a + 2)
                        for c in range(C):
                            cc = slice(c * P, (c + 1) * P)
                            V.tensor_tensor_scan(acum[:, cc], pc("ones", rows=NH), da_row[:, cc], 0.0, ALU.mult, ALU.add).then_inc(p1["scan"], 1)
                    if j == 2:
                        wait(dve, p1["scan"], C * a + C)
                        wait(dve, p1["rb_ps"], C * a)
                        V.tensor_copy(rows[0:NH, :], acum).then_inc(p1["rows"], 1)
                        wait(dve, p1["rows"], 3 * a + 1)
                        V.tensor_tensor(da_row[:], acum, rows[0:NH, :], ALU.subtract).then_inc(p1["rest"], 1)
                        wait(dve, p1["rest"], a + 1)
                        V.tensor_copy(mid[:], da_row[:]).then_inc(p1["mid"], 1)
                        wait(dve, p1["mid"], a + 1)
                        V.tensor_tensor(rows[64:64 + NH, :], da_row[:], mid[:], ALU.subtract).then_inc(p1["rows"], 1)
                        lo(6, 8)
                wait(dve, p1["conv"], 12 * a + 12)
                for k in range(3):
                    V.tensor_copy(xbc[k][:, 0:TAPS - 1], xbc[k][:, BT:BT + TAPS - 1]).then_inc(p1["carry"], 1)
                wait(dve, p1["cols_ps"], a + 1)
                wait(dve, p1["xdt"], C * a)
                V.tensor_copy(cols[:].rearrange("p k c h -> p (k c h)"), b5[:, 0:2 * C * NH]).then_inc(p1["cols"], 1)
                wait(dve, p1["end_ps"], a + 1)
                wait(dve, p1["cols"], a + 1)
                wait(dve, p1["dece"], a)
                ac = cols[:, 0].rearrange("p c h -> p (c h)")
                V.tensor_tensor(dec[:, 0, :], b5[:, 0:C * NH], ac, ALU.subtract).then_inc(p1["dec"], 1)
                V.tensor_copy(dec[:, 1, :], ac).then_inc(p1["dec"], 1)
                V.tensor_copy(dec[:, 2, :], b5[:, 0:C * NH]).then_inc(p1["dec"], 1)
                lo(8, 10)

                def heads(ap, n):
                    return ap.unsqueeze(2).broadcast_to([ap.shape[0], NH, n])

                for step in range(C + 3):
                    if 1 <= step <= C:
                        c, n, i = step - 1, C * a + step - 1, (step - 1) % 2
                        wait(dve, p1["y_ps"], n + 1)
                        wait(dve, p1["dece"], a + 1)
                        wait(dve, p1["y2"], n - 1)
                        V.tensor_tensor(y[i][:].rearrange("p (h d) -> p h d", h=NH), b6[:, DI:2 * DI].rearrange("p (h d) -> p h d", h=NH),
                                        heads(dece[:, 1, c * NH:(c + 1) * NH], HD), ALU.mult).then_inc(p1["y0"], 1)
                        wait(dve, p1["st"], n)
                        st = state[:].rearrange("p (h d) -> p h d", h=NH)
                        V.tensor_tensor(st, st, heads(dece[0:DS, 2, c * NH:(c + 1) * NH], HD), ALU.mult).then_inc(p1["stmul"], 1)
                        wait(dve, p1["y0"], n + 1)
                        V.tensor_tensor(y[i][:], b6[:, 0:DI], y[i][:], ALU.add).then_inc(p1["y"], 1)
                        wait(dve, p1["stmul"], n + 1)
                        wait(dve, p1["st_ps"], n + 1)
                        V.tensor_tensor(state[:], state[:], b3[0:DS, 0:DI], ALU.add).then_inc(p1["st"], 1)
                    if step < C:
                        c, n, i = step, C * a + step, step % 2
                        wait(dve, p1["ee"], n + 1)
                        wait(dve, p1["gt_ps"], n + 1)
                        V.tensor_tensor(decay[i][:], decay[i][:], b2[:, 0:P].unsqueeze(1).broadcast_to([P, NH, P]), ALU.mult).then_inc(p1["m"], 1)
                    if step >= 3:
                        c, n = step - 3, C * a + step - 3
                        wait(dve, p1["o_ps"], n + 1)
                        wait(dve, p1["rms"], n + 1)
                        wait(dve, p1["x1b"], a + 1)
                        V.scalar_tensor_tensor(out=x[:, t0 + c, :], in0=tr_ps[:, 0:D], scalar=rms[:, c:c + 1], in1=x[:, t0 + c, :],
                                               op0=ALU.mult, op1=ALU.add).then_inc(p1["x2"], 1)
                    if step == 0:
                        lo(10, 12)
                    if step == 3:
                        lo(12, G)
                if upcoming:
                    make_lo(dve, "V", *upcoming, 0, LEAD)
                wait(dve, p1["x2"], C * a + C)
                n = NB + 2 * a + 1
                norm_stats(n, lambda c: x[:, t0 + c, :])
                norm_apply(n, lambda c: x[:, t0 + c, :], lambda c: fresh[:, c, :])
                wait(dve, ln_norm, 4 * n + 4)
                wait(dve, p1["fhi"], b)
                V.tensor_tensor(feat16[:, ts(a, C), 1, :], fresh[:], feat16[:, ts(a, C), 0, :], ALU.subtract).then_inc(p1["flo"], 1)

            make_lo(dve, "V", 1, 0, 0, G)
            make_lo(dve, "V", 1, 1, 0, LEAD)
            iter1(1, True, (1, 2))
            with dve.Fori(2, NB - 1) as b:
                iter1(b, True, (1, b + 1))
            iter1(NB - 1, True, (2, 0))
            iter1(NB, False, None)

            def iter2(b, here, upcoming):
                a = b - 1
                t0 = 4 * a

                def lo(q0, q1):
                    if here:
                        make_lo(dve, "V", 2, b, q0, q1)

                lo(LEAD, 6)
                xb = x[:, ts(a, C), :]
                wait(dve, p2["mg_ps"], b)
                wait(dve, p2["xm"], b)
                V.tensor_tensor(xb, rows4(b3), xb, ALU.add).then_inc(p2["x3"], 1)
                wait(dve, p2["x3"], b)
                n = 3 * NB + a
                norm_stats(n, lambda c: x[:, t0 + c, :])
                norm_apply(n, lambda c: x[:, t0 + c, :], lambda c: xhat[:, c, :])
                lo(6, 9)
                wait(dve, p2["gl_ps"], b)
                wait(dve, p2["gt_ps"], a)
                V.tensor_tensor(lg[:, 0], b3[:, 0:C * E].rearrange("p (c e) -> p c e", c=C),
                                pc("br").unsqueeze(1).broadcast_to([P, C, E]), ALU.add).then_inc(p2["lg"], 1)
                wait(dve, p2["lg"], b)
                V.tensor_reduce(red[:, 0, :], lg[:, 0], AX_X, ALU.max).then_inc(p2["mx"], 1)
                wait(dve, p2["mx"], b)
                V.tensor_tensor(lg[:, 1], lg[:, 0], red[:, 0, :].unsqueeze(2).broadcast_to([P, C, E]), ALU.subtract).then_inc(p2["sub"], 1)
                lo(9, 11)
                wait(dve, p2["ex"], b)
                V.tensor_reduce(red[:, 1, :], lg[:, 2], AX_X, ALU.add).then_inc(p2["sum"], 1)
                wait(dve, p2["sum"], b)
                V.reciprocal(red[:, 2, :], red[:, 1, :]).then_inc(p2["rcp"], 1)
                wait(dve, p2["rcp"], b)
                wait(dve, p2["acc"], C * E * a)
                V.tensor_tensor(gate[:], lg[:, 2], red[:, 2, :].unsqueeze(2).broadcast_to([P, C, E]), ALU.mult).then_inc(p2["gate"], 1)
                wait(dve, p2["gt_ps"], b)
                V.tensor_copy(gate_t[:], b3[0:E, :]).then_inc(p2["gt_sb"], 1)
                wait(dve, p2["gb_ps"], b)
                V.tensor_tensor(xb, rows4(b3), xb, ALU.add).then_inc(p2["gb"], 1)
                wait(dve, p2["gate"], b)
                wait(dve, p2["gb"], b)
                for e in range(E):
                    lo(min(11 + e, G), min(12 + e, G))
                    wait(dve, p2["wo_ps"], E * a + e + 1)
                    for c in range(C):
                        if e:
                            wait(dve, p2["acc"], C * (E * a + e - 1) + c + 1)
                        V.scalar_tensor_tensor(out=x[:, t0 + c, :], in0=b7[:, c * D:(c + 1) * D], scalar=gate[:, c, e:e + 1],
                                               in1=x[:, t0 + c, :], op0=ALU.mult, op1=ALU.add).then_inc(p2["acc"], 1)

                if upcoming:
                    make_lo(dve, "V", *upcoming, 0, LEAD)

            make_lo(dve, "V", 2, 0, LEAD, G)
            make_lo(dve, "V", 2, 1, 0, LEAD)
            iter2(1, True, (2, 2))
            with dve.Fori(2, NB - 1) as b:
                iter2(b, True, (2, b + 1))
            iter2(NB - 1, True, None)
            iter2(NB, False, None)

        @block.gpsimd
        def _(pool):
            Q = nc.gpsimd

            def norm_rstd(n):
                wait(pool, ln_aggr, 4 * n + 4)
                wait(pool, ln_rstd, n)
                hold(Q)
                Q.tensor_scalar(var[:], mv[:, :, 1], LN_EPS, None, ALU.add).then_inc(ln_var, 1)
                wait(pool, ln_var, n + 1)
                Q.tensor_tensor(rstd[:], var[:], neg_half[:, 0:C], ALU.pow).then_inc(ln_rstd, 1)

            pool.wait_ge(consts_set, 1)
            norm_rstd(0)
            pool.wait_ge(par_loaded, 16)
            for k, (v, g, m, bb, be) in enumerate((("v1", "g1", "m1", "b1", "be1"), ("v2", "g2", "m2", "b2", "be2"))):
                s = slice(k * E, (k + 1) * E)
                base = 5 * k
                Q.tensor_scalar(bn_t[:, 0, s], pc(v), BN_EPS, None, ALU.add).then_inc(prep_pool, 1)
                pool.wait_ge(prep_pool, base + 1)
                Q.tensor_tensor(bn_t[:, 1, s], bn_t[:, 0, s], neg_half[:, s], ALU.pow).then_inc(prep_pool, 1)
                Q.tensor_tensor(bn_t[:, 2, s], pc(bb), pc(m), ALU.subtract).then_inc(prep_pool, 1)
                pool.wait_ge(prep_pool, base + 3)
                Q.tensor_tensor(bn_s[:, s], pc(g), bn_t[:, 1, s], ALU.mult).then_inc(prep_pool, 1)
                pool.wait_ge(prep_pool, base + 4)
                Q.tensor_tensor(bn_f[:, s], bn_t[:, 2, s], bn_s[:, s], ALU.mult).then_inc(prep_pool, 1)
            pool.wait_ge(prep_pool, 10)
            for k, be in enumerate(("be1", "be2")):
                s = slice(k * E, (k + 1) * E)
                Q.tensor_tensor(bn_f[:, s], bn_f[:, s], pc(be), ALU.add).then_inc(prep_pool, 1)

            def degrees(a):
                wait(pool, p0["deg"], a + 1)
                d = p0["dis"]
                hold(Q)
                Q.tensor_scalar(dg[:, 0, :], deg[:], 0.0, None, ALU.is_equal).then_inc(d, 1)
                wait(pool, d, 5 * a + 1)
                Q.tensor_tensor(dg[:, 1, :], deg[:], dg[:, 0, :], ALU.add).then_inc(d, 1)
                Q.tensor_scalar(dg[:, 3, :], dg[:, 0, :], -1.0, 1.0, ALU.mult, ALU.add).then_inc(d, 1)
                wait(pool, d, 5 * a + 3)
                Q.tensor_tensor(dg[:, 2, :], dg[:, 1, :], neg_half[:, 0:C], ALU.pow).then_inc(d, 1)
                wait(pool, d, 5 * a + 4)
                Q.tensor_tensor(dis[:, ts(a, C)], dg[:, 2, :], dg[:, 3, :], ALU.mult).then_inc(d, 1)

            def own_share(a):
                tb = ts(a, C)
                wait(pool, p0["s32"], 4 * a + 4)
                wait(pool, p0["sx"], 2 * a)
                hold(Q)
                Q.tensor_tensor(decay[1][:], fresh[:], dis[:, tb].unsqueeze(2).broadcast_to([P, C, D]), ALU.mult).then_inc(p0["sx"], 1)
                wait(pool, p0["sx"], 2 * a + 1)
                hold(Q)
                Q.tensor_tensor(x[:, tb, :], x[:, tb, :], decay[1][:], ALU.add).then_inc(p0["sx"], 1)

            def iter0(b, before, upcoming, norm):
                if before:
                    degrees(b - 1)
                make_lo(pool, "Q", 0, b, LEAD, 8)
                if norm:
                    norm_rstd(b + 1)
                make_lo(pool, "Q", 0, b, 8, G)
                if before:
                    own_share(b - 1)
                if upcoming:
                    make_lo(pool, "Q", *upcoming, 0, LEAD)

            make_lo(pool, "Q", 0, 0, 0, LEAD)
            iter0(0, False, (0, 1), True)
            iter0(1, True, (0, 2), True)
            with pool.Fori(2, NB - 1) as b:
                iter0(b, True, (0, b + 1), True)
            iter0(NB - 1, True, None, False)
            degrees(NB - 1)
            own_share(NB - 1)

            def iter1(b, here):
                a = b - 1
                norm_rstd(NB + 2 * a)
                tb = ts(a, C)
                wait(pool, ln_norm, 4 * (NB + 2 * a + 1))
                hold(Q)
                Q.tensor_tensor(x[:, tb, :], x[:, tb, :], pc("b_lin").unsqueeze(1).broadcast_to([P, C, D]), ALU.add).then_inc(p1["x1b"], 1)
                for step in range(C + 2):
                    if here and step == 3:
                        make_lo(pool, "Q", 1, b, 0, G)
                    if step < C:
                        c, n, i = step, C * a + step, step % 2
                        wait(pool, p1["xT"], n + 1)
                        wait(pool, p1["cols"], a + 1)
                        wait(pool, p1["y_ps"], n - 1)
                        h3 = lambda ap: ap.rearrange("p (h d) -> p h d", h=NH)
                        Q.tensor_tensor(h3(xdt[i][:]), h3(xt[i][:, 0:DI]), cols[:, 1, c, :].unsqueeze(2).broadcast_to([P, NH, HD]),
                                        ALU.mult).then_inc(p1["xdt"], 1)
                        wait(pool, p1["xdt"], n + 1)
                        wait(pool, p1["dece"], a + 1)
                        wait(pool, p1["st_ps"], n - 1)
                        Q.tensor_tensor(h3(xdd[i][:]), h3(xdt[i][:]), dece[:, 0, c * NH:(c + 1) * NH].unsqueeze(2).broadcast_to([P, NH, HD]),
                                        ALU.mult).then_inc(p1["xdd"], 1)
                    if 1 <= step <= C:
                        c, n, i = step - 1, C * a + step - 1, (step - 1) % 2
                        wait(pool, p1["y"], n + 1)
                        wait(pool, p1["zs"], 2 * a + 2)
                        wait(pool, p1["yT_ps"], n - 1)
                        wait(pool, p1["ssq"], n - 1)
                        Q.tensor_tensor(y2[i][:], y[i][:], zs[:, c, :], ALU.mult).then_inc(p1["y2"], 1)
                    if step >= 2:
                        c, n = step - 2, C * a + step - 2
                        wait(pool, p1["ssq"], n + 1)
                        wait(pool, p1["rms"], n)
                        hold(Q)
                        Q.tensor_scalar(msq[:, c:c + 1], ssq[:, c:c + 1], 1.0 / DI, RMS_EPS, ALU.mult, ALU.add).then_inc(p1["rv"], 1)
                        wait(pool, p1["rv"], n + 1)
                        wait(pool, p1["x2"], C * a)
                        Q.tensor_tensor(rms[:, c:c + 1], msq[:, c:c + 1], neg_half[:, 0:1], ALU.pow).then_inc(p1["rms"], 1)
                norm_rstd(NB + 2 * a + 1)

            make_lo(pool, "Q", 1, 0, 0, G)
            iter1(1, True)
            with pool.Fori(2, NB) as b:
                iter1(b, True)
            iter1(NB, False)

            def iter2(b, here, upcoming):
                a = b - 1

                def lo(q0, q1):
                    if here:
                        make_lo(pool, "Q", 2, b, q0, q1)

                tb = ts(a, C)
                hold(Q)
                Q.tensor_tensor(x[:, tb, :], x[:, tb, :], side[:, tb, :], ALU.add).then_inc(p2["xm"], 1)
                lo(LEAD, 8)
                norm_rstd(3 * NB + a)
                lo(8, G)
                if upcoming:
                    make_lo(pool, "Q", *upcoming, 0, LEAD)
                wait(pool, p2["acc"], C * E * (a + 1))
                pool.dma_start(out[a], x[:, tb, :]).then_inc(out_stored, 16)

            pool.wait_ge(p0["mg"], NB)
            pool.wait_ge(ln_norm, 4 * 3 * NB)
            make_lo(pool, "Q", 2, 0, 0, G)
            make_lo(pool, "Q", 2, 1, 0, LEAD)
            iter2(1, True, (2, 2))
            with pool.Fori(2, NB - 1) as b:
                iter2(b, True, (2, b + 1))
            iter2(NB - 1, True, None)
            iter2(NB, False, None)
            pool.wait_ge(out_stored, 16 * NB)


def kernel(**inputs):
    import numpy as np
    import concourse.bacc as bacc
    from concourse.bass_utils import run_bass_kernel_spmd

    v = {k: np.asarray(a) for k, a in inputs.items()}
    adj = np.ascontiguousarray(v["adj"].reshape(NB, BT, G, GJ, P).transpose(0, 2, 4, 3, 1))

    par = np.zeros((P, PARAMS), np.float32)

    def put(name, a, rows=P):
        lo, hi = COL[name]
        par[0:rows, lo:hi] = a

    idx = np.arange(P)
    put("ident", np.eye(P))
    put("barred", np.where(idx[None, :] >= idx[:, None], 0.0, -1e30))
    put("last", np.broadcast_to((idx == P - 1)[:, None], (P, P)))
    put("ones", np.ones((P, P)))
    for part in range(3):
        par[32 * part:32 * part + NH, slice(*COL["pick"])] = np.eye(NH)
    put("g0_b", np.broadcast_to(v["L0_gnn_b"], (P, D)))
    put("bm", np.broadcast_to(v["L1_gnn_bm"], (P, D)))
    put("b_lin", np.broadcast_to(v["L0_ffn_b_lin"], (P, D)))
    put("br", np.broadcast_to(v["L1_ffn_br"], (P, E)))
    put("conv_w", v["L0_ffn_conv_w"].reshape(3, P, TAPS).transpose(1, 0, 2).reshape(P, 3 * TAPS))
    put("conv_b", v["L0_ffn_conv_b"].reshape(3, P).T)
    put("skip", np.repeat(v["L0_ffn_D"], HD).reshape(2, P).T)
    put("norm_w", v["L0_ffn_norm_w"].reshape(2, P).T)
    put("eps1", np.broadcast_to(v["L1_gnn_eps1"], (P, 1)))
    put("eps2", np.broadcast_to(v["L1_gnn_eps2"], (P, 1)))
    put("mlp1_b", v["L1_gnn_b1"].T)
    put("mlp2_b", v["L1_gnn_b2"].T)
    for name in ("g1", "be1", "m1", "v1", "b1", "g2", "be2", "m2", "v2", "b2"):
        put(name, v["L1_ffn_" + name].T)
    put("a_log", v["L0_ffn_A_log"][:, None], NH)
    put("dt_bias", v["L0_ffn_dt_bias"][:, None], NH)
    put("bo", v["L1_ffn_bo"], E)
    put("g0_w", v["L0_gnn_W"].T)
    put("w_in", v["L0_ffn_W_in"])
    put("w_out_t", v["L0_ffn_W_out"].T)
    put("w_lin", v["L0_ffn_W_lin"])
    put("mlp1_w", v["L1_gnn_W1"].transpose(2, 0, 1).reshape(D, 3 * D))
    put("mlp2_w", v["L1_gnn_W2"].transpose(2, 0, 1).reshape(D, 3 * D))
    put("wm", v["L1_gnn_Wm"].reshape(D, 2, D).transpose(2, 1, 0).reshape(D, 2 * D))
    put("wr", v["L1_ffn_Wr"])
    put("ew1", v["L1_ffn_W1"].transpose(1, 0, 2).reshape(D, E * D))
    put("ew2", v["L1_ffn_W2"].transpose(1, 0, 2).reshape(D, E * D))
    put("ewo", v["L1_ffn_Wo"].transpose(1, 0, 2).reshape(D, E * D))

    arrays = {"x_dram": np.ascontiguousarray(v["x"]), "x2_dram": np.ascontiguousarray(v["L1_gnn_x2"]),
              "adj_dram": adj, "par_dram": par}
    nc = bacc.Bacc("TRN2", target_bir_lowering=False, num_devices=1)
    args = [nc.dram_tensor(n, a.shape, mybir.dt.from_np(a.dtype), kind="ExternalInput").ap() for n, a in arrays.items()]
    res = nc.dram_tensor("out_dram", (NB, P, C, D), F32, kind="ExternalOutput").ap()
    build(nc, *args, res)
    r = run_bass_kernel_spmd(nc, [arrays], core_ids=[0])
    return np.ascontiguousarray(r.results[0]["out_dram"].transpose(0, 2, 1, 3).reshape(T, D))
```

```python
from contextlib import ExitStack

import concourse.bass as bass
from concourse import mybir

ALU = mybir.AluOpType
ACT = mybir.ActivationFunctionType
AX_X = mybir.AxisListType.X
F32 = mybir.dt.float32
F16 = mybir.dt.float16
BF16 = mybir.dt.bfloat16

T = 4096
D = 128
P = 128
NT = T // P
BT = 512
NB = T // BT
C = BT // P
GJ = 2
G = NT // GJ
SLOTS = 8
NBUF = 4
DI, DS, NH, HD = 256, 64, 4, 64
TAPS = 4
E = 8
LN_EPS, RMS_EPS, BN_EPS = 1e-5, 1e-5, 1e-3

KINDS = ["FQ" * 8, "FVFQFQFQFQFVFVFV", "VVQVVVQVQVQVVVQV"]
CHUNK_FILL = (1, 0, 1, 1, 1, 1, 0)
EXPERT_FILL = (0, 1, 1, 0, 1, 0, 1, 1, 1, 0)
SUMS = G // 2
EARLY = G - 2
LEAD = 4
SPLITS = [sum(k != "F" for k in kinds) for kinds in KINDS]
assert all(n % NBUF == 0 for n in SPLITS) and all(k[-1] != "F" for k in KINDS)

_WIDTHS = [
    ("ident", P), ("barred", P), ("last", P), ("ones", P),
    ("g0_b", D), ("bm", D), ("b_lin", D), ("br", E),
    ("conv_w", 3 * TAPS), ("conv_b", 3), ("skip", 2), ("norm_w", 2), ("eps1", 1), ("eps2", 1),
    ("mlp1_b", 3), ("mlp2_b", 3),
    ("g1", E), ("be1", E), ("m1", E), ("v1", E), ("b1", E),
    ("g2", E), ("be2", E), ("m2", E), ("v2", E), ("b2", E),
    ("a_log", 1), ("dt_bias", 1), ("pick", NH), ("bo", D),
    ("g0_w", D), ("w_in", 2 * DI + 2 * DS + NH), ("w_out_t", DI), ("w_lin", D),
    ("mlp1_w", 3 * D), ("mlp2_w", 3 * D), ("wm", 2 * D), ("wr", E),
    ("ew1", E * D), ("ew2", E * D), ("ewo", E * D),
]
COL, _at = {}, 0
for _name, _w in _WIDTHS:
    COL[_name] = (_at, _at + _w)
    _at += _w
PARAMS = _at


def ts(i, n):
    return bass.ts(i, n)


def wait(eng, sem, value):
    if isinstance(value, int) and value <= 0:
        return
    eng.wait_ge(sem, value)


def build(nc, x_in, x2_in, adj_in, par_in, out):
    with ExitStack() as ctx:
        def sb(name, shape):
            return ctx.enter_context(nc.sbuf_tensor(name, shape, F32))

        def sbt(name, shape, dtype):
            return ctx.enter_context(nc.sbuf_tensor(name, shape, dtype))

        def bank(name):
            return ctx.enter_context(nc.psum_tensor(name, [P, BT], F32))

        def sem(name):
            return ctx.enter_context(nc.semaphore(name))

        par = sb("par", [P, PARAMS])
        ring = sb("ring", [P, SLOTS, GJ, BT])
        x = sb("x", [P, NT, D])
        halves = sbt("halves", [P, NBUF, 2, GJ, BT], F16)
        sup = sb("sup", [P, NT, D])
        feat = sb("feat", [P, NT, D])
        side = sb("side", [P, NT, D])
        dis = sb("dis", [P, NT])
        stats = sb("stats", [P, C, 6])
        mv = sb("mv", [P, C, 2])
        var = sb("var", [P, C])
        rstd = sb("rstd", [P, C])
        spare = sb("spare", [P, 128])
        neg_half = sb("neg_half", [P, 2 * E])
        xhat = sb("xhat", [P, C, D])
        xhat_t = sb("xhat_t", [P, BT])
        z_t = sb("z_t", [P, BT])
        xt16 = sbt("xt16", [P, 2, BT], F16)
        work = sb("work", [P, 7, BT])
        part, pair, colsum = [work[:, 2 * k:2 * k + 2] for k in range(2)], work[:, 4:6], work[:, 6]
        wide = sb("wide", [P, 7, BT])
        deg = sb("deg", [P, C])
        dg = sb("dg", [P, 4, C])
        gain = sb("gain", [P, 2])
        hid = [wide[:, i] for i in range(3)]
        w_ol = sb("w_ol", [P, 2, D])
        skip_d = sb("skip_d", [P, 2, P])
        a_neg = sb("a_neg", [NH, 2])
        bn_s = sb("bn_s", [P, 2 * E])
        bn_f = sb("bn_f", [P, 2 * E])
        bn_t = sb("bn_t", [P, 3, 2 * E])
        xbc = [sb(f"xbc{k}", [P, TAPS - 1 + BT]) for k in range(3)]
        conv = [work[:, 2 * k:2 * k + 2] for k in range(3)]
        zs = wide[:, 0:2].rearrange("p a (b d) -> p (a b) d", b=2)
        xs = [wide[:, 2 + k] for k in range(2)]
        bs = wide[0:DS, 4]
        cs = wide[0:DS, 5]
        dt_row = wide[0:NH, 6]
        da_row = sb("da_row", [NH, BT])
        mid = sbt("mid", [NH, BT], BF16)
        rows = sbt("rows", [P, BT], BF16)
        pick = sbt("pick", [P, NH, P], BF16)
        unpick = sbt("unpick", [P, NH, P], BF16)
        ident16 = sbt("ident16", [P, P], BF16)
        barred = sbt("barred", [P, P], BF16)
        acum = work[0:NH, 6]
        cols = sb("cols", [P, 2, C, NH])
        dec = sb("dec", [P, 3, C * NH])
        dece = sb("dece", [P, 3, C * NH])
        decay = [sb(f"decay{i}", [P, NH, P]) for i in range(2)]
        xt = [sb(f"xt{i}", [P, DI + DS]) for i in range(2)]
        xdt = [sb(f"xdt{i}", [P, DI]) for i in range(2)]
        xdd = [sb(f"xdd{i}", [P, DI]) for i in range(2)]
        y = [sb(f"y{i}", [P, DI]) for i in range(2)]
        y2 = [sb(f"y2{i}", [P, DI]) for i in range(2)]
        y_t = [sb(f"y_t{i}", [P, DI]) for i in range(2)]
        ssq = sb("ssq", [P, C])
        msq = sb("msq", [P, C])
        rms = sb("rms", [P, C])
        state = sb("state", [DS, DI])
        lg = sb("lg", [P, 3, C, E])
        red = sb("red", [P, 3, C])
        gate = sb("gate", [P, C, E])
        gate_t = work[0:E, 6]
        h1 = [wide[:, 3 + i] for i in range(2)]
        h2 = [wide[:, 5 + i] for i in range(2)]

        def pc(name, lo=0, hi=None, rows=P):
            a, b = COL[name]
            return par[0:rows, a + lo:(a + hi if hi is not None else b)]

        def as_halves(t):
            return t[:].bitcast(F16).rearrange("p t (k d) -> p t k d", k=2)

        sup16, feat16 = as_halves(sup), as_halves(feat)
        ew1_stage = side[:, NT - E:, :]
        ew1_16 = pc("ew1").bitcast(F16).rearrange("p (e k d) -> p e k d", e=E, k=2)
        x2_stage = wide[:, 0:4].rearrange("p a (b j d) -> p (a b) j d", b=2, j=GJ)
        fresh = decay[0]

        acc_ps = bank("acc_ps")
        tr_ps = bank("tr_ps")
        b2, b3, b4, b5, b6, b7 = (bank(f"b{i}_ps") for i in range(2, 8))

        ident = pc("ident")

        par_loaded = sem("par_loaded")
        experts_loaded = sem("experts_loaded")
        ew1_split = sem("ew1_split")
        x_loaded = sem("x_loaded")
        x_rest_loaded = sem("x_rest_loaded")
        x2_loaded = sem("x2_loaded")
        x2_odd_loaded = sem("x2_odd_loaded")
        x2_split = sem("x2_split")
        rows_set = sem("rows_set")
        adj_loaded = [sem(f"adj_loaded{q}") for q in range(SLOTS)]
        adj_used = sem("adj_used")
        split_used = sem("split_used")
        hi_done = sem("hi_done")
        lo_done = {"V": sem("lo_done_v"), "Q": sem("lo_done_q")}
        adj_summed = sem("adj_summed")
        out_stored = sem("out_stored")
        consts_set = sem("consts_set")
        prep_pe = sem("prep_pe")
        prep_dve = sem("prep_dve")
        prep_act = sem("prep_act")
        prep_pool = sem("prep_pool")
        ln_stats, ln_aggr, ln_var, ln_rstd, ln_norm = (sem(n) for n in ("ln_stats", "ln_aggr", "ln_var", "ln_rstd", "ln_norm"))
        names0 = "xt_ps deg_ps sup_ps mlp_ps mg_ps z_sb xt_sb h part colsum sup deg mg dis s32 shi slo sx sf".split()
        p0 = {n: sem("p0_" + n) for n in names0}
        names1 = ("z_sb zt_ps x1 xt_ps xt_sb proj_ps zp_ps xbc dtact dtexp dtln dtrow scan zs conv carry act cols_ps cols "
                  "end_ps dec dece xT_ps xT rb_ps ee gt_ps m rest mid rows xdt xdd y_ps y0 y y2 ssq rv rms yT_ps yT o_ps "
                  "x2 x1b st_ps stmul st fhi flo").split()
        p1 = {n: sem("p1_" + n) for n in names1}
        names2 = ("z_sb mlp_ps h mg_ps xm x3 xt_ps xt_sb xt_hi xt_lo gl_ps lg mx sub ex sum rcp gate gt_ps gt_sb gb_ps gb "
                  "w1_ps h1 w2_ps h2 wo_ps acc").split()
        p2 = {n: sem("p2_" + n) for n in names2}

        holds = []

        def hold(engine):
            at = len(holds)
            holds.append(at)
            o = spare[:, at:at + 1]
            if engine is nc.gpsimd:
                engine.tensor_tensor(o, neg_half[:, 0:1], neg_half[:, 1:2], ALU.add)
            else:
                engine.tensor_copy(o, neg_half[:, 0:1])

        def counted(ph, b, q, kinds):
            before = sum(NB * sum(k in kinds for k in KINDS[i]) for i in range(ph))
            return before + b * sum(k in kinds for k in KINDS[ph]) + sum(k in kinds for k in KINDS[ph][:q + 1])

        def strip_loaded(ph, b, q):
            return 16 * ((ph * NB + b) * (G // SLOTS) + q // SLOTS + 1)

        def wait_strip_freed(eng, ph, b, q):
            kind = KINDS[ph][q]
            if kind == "F":
                wait(eng, adj_used, counted(ph, b, q, "F"))
            else:
                wait(eng, lo_done[kind], counted(ph, b, q, kind))
            if ph == 0:
                wait(eng, adj_summed, G // 2 * b + q // 2 + 1)

        def block_done(ph, b):
            return counted(ph, b, G - 1, "VQ")

        def buffer(ph, q):
            return (counted(ph, 0, q, "VQ") - 1) % NBUF

        def make_hi(act, ph, b, lo, hi):
            for q in range(lo, hi):
                if KINDS[ph][q] == "F":
                    continue
                wait(act, adj_loaded[q % SLOTS], strip_loaded(ph, b, q))
                wait(act, split_used, counted(ph, b, q, "VQ") - NBUF)
                nc.scalar.activation(halves[:, buffer(ph, q), 0], ring[:, q % SLOTS], ACT.Copy).then_inc(hi_done, 1)

        def make_lo(eng, kind, ph, b, lo, hi):
            for q in range(lo, hi):
                if KINDS[ph][q] != kind:
                    continue
                wait(eng, adj_loaded[q % SLOTS], strip_loaded(ph, b, q))
                wait(eng, hi_done, counted(ph, b, q, "VQ"))
                eng.tensor_tensor(halves[:, buffer(ph, q), 1], ring[:, q % SLOTS], halves[:, buffer(ph, q), 0],
                                  ALU.subtract).then_inc(lo_done[kind], 1)

        block = ctx.enter_context(nc.Block())

        @block.sync
        def _(sp):
            featv = feat[:].rearrange("p (s e j) d -> p s e j d", e=2, j=GJ)
            stagev = x2_stage

            def load(ph, b):
                for q in range(G):
                    if q >= SLOTS:
                        wait_strip_freed(sp, ph, b, q - SLOTS)
                    elif not isinstance(b, int) or b > 0:
                        wait_strip_freed(sp, ph, b - 1, q + G - SLOTS)
                    elif ph > 0:
                        wait_strip_freed(sp, ph - 1, NB - 1, q + G - SLOTS)
                    sp.dma_start(ring[:, q % SLOTS], adj_in[b, q]).then_inc(adj_loaded[q % SLOTS], 16)
                    if ph == 0 and isinstance(b, int) and q == 0:
                        for j in range(GJ):
                            sp.dma_start(featv[:, :, 0, j], x2_in[0, j]).then_inc(x2_loaded, 16)

            for j in range(GJ):
                sp.dma_start(stagev[:, :, j], x2_in[1, j]).then_inc(x2_odd_loaded, 16)
            for ph in range(3):
                load(ph, 0)
                with sp.Fori(1, NB) as b:
                    load(ph, b)

        @block.tensor
        def _(pe):
            def mm(o, l, r, start=True, stop=True, **k):
                return nc.tensor.matmul(o, l, r, start=start, stop=stop, **k)

            def adjacency(ph, b, lo, hi, stationary, halved, free_sem):
                for q in range(lo, hi):
                    if q == 0:
                        wait(pe, free_sem, b)
                    split = KINDS[ph][q] != "F"
                    if split:
                        wait(pe, lo_done[KINDS[ph][q]], counted(ph, b, q, KINDS[ph][q]))
                    else:
                        wait(pe, adj_loaded[q % SLOTS], strip_loaded(ph, b, q))
                    for j in range(GJ):
                        i = q * GJ + j
                        first, last = i == 0, i == NT - 1
                        if not split:
                            ins = mm(acc_ps[:], stationary[:, i, :], ring[:, q % SLOTS, j, :], start=first, stop=last)
                            continue
                        hi_lo = halves[:, buffer(ph, q)]
                        mm(acc_ps[:], halved[:, i, 0, :], hi_lo[:, 0, j, :], start=first, stop=False)
                        mm(acc_ps[:], halved[:, i, 0, :], hi_lo[:, 1, j, :], start=False, stop=False)
                        ins = mm(acc_ps[:], halved[:, i, 1, :], hi_lo[:, 0, j, :], start=False, stop=last)
                    ins.then_inc(split_used if split else adj_used, 1)

            def transposes(src, dst, n, done):
                for c in range(n):
                    ins = nc.tensor.transpose(dst[:, c * P:(c + 1) * P], src(c), ident)
                ins.then_inc(done, 1)

            def iter0(b, here, before):
                if before:
                    wait(pe, p0["colsum"], SUMS * b)
                    wait(pe, p0["deg"], b - 1)
                    for c in range(C):
                        ins = mm(b5[:, c:c + 1], colsum[:, c * P:(c + 1) * P], pc("ones", 0, 1))
                    ins.then_inc(p0["deg_ps"], 1)
                if here:
                    adjacency(0, b, 0, 1, feat, feat16, p0["z_sb"])
                    if isinstance(b, int) and b == 0:
                        pe.wait_ge(x2_split, 4)
                    adjacency(0, b, 1, 4, feat, feat16, None)
                    if isinstance(b, int) and b == 0:
                        pe.wait_ge(par_loaded, 16)
                    wait(pe, ln_norm, 4 * (b + 1))
                    transposes(lambda c: xhat[:, c, :], tr_ps, C, p0["xt_ps"])
                for l in range(3):
                    if before:
                        if l == 0:
                            wait(pe, p0["z_sb"], b)
                            wait(pe, p0["h"], 3 * (b - 1))
                        else:
                            wait(pe, p0["h"], 3 * (b - 1) + l)
                        mm(b2[:], pc("mlp2_w", l * D, (l + 1) * D), z_t[:] if l == 0 else hid[l - 1][:]).then_inc(p0["mlp_ps"], 1)
                    if here:
                        adjacency(0, b, 4 * l + 4, 4 * l + (8 if l < 2 else 6), feat, feat16, None)
                    if here and l == 0:
                        wait(pe, p0["xt_sb"], b + 1)
                        wait(pe, p0["sup"], b)
                        for c in range(C):
                            ins = mm(b3[:, c * D:(c + 1) * D], xhat_t[:, c * P:(c + 1) * P], pc("g0_w"))
                        ins.then_inc(p0["sup_ps"], 1)
                if before:
                    wait(pe, p0["h"], 3 * b)
                    wait(pe, p0["mg"], b - 1)
                    for c in range(C):
                        ins = mm(b4[:, c * D:(c + 1) * D], hid[2][:, c * P:(c + 1) * P], pc("wm", D, 2 * D))
                    ins.then_inc(p0["mg_ps"], 1)
                if here:
                    adjacency(0, b, 14, 16, feat, feat16, None)

            pe.wait_ge(x2_loaded, 32)
            iter0(0, True, False)
            for k in range(2):
                ins = mm(b6[:, k * P:(k + 1) * P], pc("w_out_t", k * P, (k + 1) * P), pc("w_lin"))
            ins.then_inc(prep_pe, 1)
            iter0(1, True, True)
            with pe.Fori(2, NB) as b:
                iter0(b, True, True)
            iter0(NB, False, True)

            pe.wait_ge(p0["sf"], NB)
            pe.wait_ge(p0["slo"], NB)
            pe.wait_ge(p0["mg"], NB)
            pe.wait_ge(rows_set, 5)
            pe.wait_ge(prep_dve, 7)
            pe.wait_ge(prep_pool, 8)

            def chunk_scores(a, c):
                n = C * a + c
                wait(pe, p1["act"], 4 * a + 4)
                wait(pe, p1["xT"], n)
                if c == 0:
                    wait(pe, p1["xbc"], 3 * a + 3)
                cc = slice(c * P, (c + 1) * P)
                for k in range(2):
                    nc.tensor.transpose(b4[:, k * P:(k + 1) * P], xs[k][:, cc], ident)
                nc.tensor.transpose(b4[:, DI:DI + DS], bs[:, cc], pc("ident", 0, DS, rows=DS)).then_inc(p1["xT_ps"], 1)
                wait(pe, p1["ee"], n)
                wait(pe, p1["dec"], 3 * a + 3)
                wait(pe, p1["rows"], 3 * a + 3)
                mm(b5[:].rearrange("p (h l) -> p h l", h=NH), ident16[:], barred[:].unsqueeze(1).broadcast_to([P, NH, P]),
                   skip_group_check=True)
                for h in range(NH):
                    mm(b5[:, h * P:(h + 1) * P], pick[:, h, :], rows[:, cc], start=False, stop=False, skip_group_check=True)
                    ins = mm(b5[:, h * P:(h + 1) * P], rows[:, cc], unpick[:, h, :], start=False, stop=(h == NH - 1),
                             skip_group_check=True)
                ins.then_inc(p1["rb_ps"], 1)
                wait(pe, p1["m"], n)
                mm(b2[:, 0:P], bs[:, cc], cs[:, cc]).then_inc(p1["gt_ps"], 1)

            def chunk_outputs(a, c):
                n = C * a + c
                i = c % 2
                cc = slice(c * P, (c + 1) * P)
                wait(pe, p1["xdd"], n + 1)
                wait(pe, p1["st"], n)
                mm(b3[0:DS, 0:DI], xt[i][:, DI:DI + DS], xdd[i][:]).then_inc(p1["st_ps"], 1)
                wait(pe, p1["y"], n)
                wait(pe, p1["zs"], 2 * a + 2)
                mm(b6[:, DI:2 * DI], cs[:, cc], state[:], skip_group_check=True)
                for k in range(2):
                    mm(b6[:, k * P:(k + 1) * P], xs[k][:, cc], skip_d[:, k, :], start=False, stop=False,
                       skip_group_check=True)
                wait(pe, p1["m"], n + 1)
                wait(pe, p1["xdt"], n + 1)
                for h in range(NH):
                    ins = mm(b6[:, h * HD:(h + 1) * HD], decay[i][:, h, :], xdt[i][:, h * HD:(h + 1) * HD],
                             start=False, stop=(h == NH - 1), skip_group_check=True)
                ins.then_inc(p1["y_ps"], 1)

            def chunk_turn(a, c):
                n = C * a + c
                wait(pe, p1["y2"], n + 1)
                wait(pe, p1["yT"], n)
                for k in range(2):
                    ins = nc.tensor.transpose(b7[:, k * P:(k + 1) * P], y2[c % 2][:, k * P:(k + 1) * P], ident)
                ins.then_inc(p1["yT_ps"], 1)

            def chunk_project(a, c):
                n = C * a + c
                wait(pe, p1["yT"], n + 1)
                wait(pe, p1["x2"], n)
                for k in range(2):
                    ins = mm(tr_ps[:, 0:D], y_t[c % 2][:, k * P:(k + 1) * P], w_ol[:, k, :], start=(k == 0), stop=(k == 1))
                ins.then_inc(p1["o_ps"], 1)

            def iter1(b, here, before):
                a = b - 1
                seam = isinstance(b, int) and b == NB

                def fill(lo, hi):
                    if here:
                        adjacency(1, b, lo, hi, sup, sup16, p1["z_sb"])
                    elif seam:
                        for q in range(lo, min(hi, EARLY)):
                            pe.wait_ge(p1["flo"], q // 2 + 1)
                            adjacency(2, 0, q, q + 1, feat, feat16, None)

                if before:
                    wait(pe, p1["z_sb"], b)
                    wait(pe, p1["yT"], C * a)
                    transposes(lambda c: z_t[:, c * P:(c + 1) * P], b7, C, p1["zt_ps"])
                fill(0, 5)
                if before:
                    wait(pe, ln_norm, 4 * (NB + 2 * a + 1))
                    wait(pe, p1["x2"], C * a)
                    transposes(lambda c: xhat[:, c, :], tr_ps, C, p1["xt_ps"])
                fill(5, 6)
                if before:
                    wait(pe, p1["xt_sb"], b)
                    wait(pe, p1["ee"], C * a)
                    mm(b5[0:NH, :], pc("w_in", 2 * DI + 2 * DS, 2 * DI + 2 * DS + NH), xhat_t[:]).then_inc(p1["proj_ps"], 1)
                    wait(pe, p1["m"], C * a)
                    wait(pe, p1["st"], C * a)
                    wait(pe, p1["xT"], C * a)
                    for k, bk in enumerate((b2, b3, b4)):
                        mm(bk[:], pc("w_in", DI + k * P, DI + (k + 1) * P), xhat_t[:]).then_inc(p1["proj_ps"], 1)
                    wait(pe, p1["y"], C * a)
                    wait(pe, p1["x1"], C * b)
                    for c in range(C):
                        bk = (b6, b7)[c // 2]
                        ins = mm(bk[:, c % 2 * DI:(c % 2 + 1) * DI], xhat_t[:, c * P:(c + 1) * P], pc("w_in", 0, DI))
                        if c % 2:
                            ins.then_inc(p1["zp_ps"], 1)
                fill(6, 9)
                if before:
                    wait(pe, p1["scan"], C * b)
                    wait(pe, p1["dtact"], 2 * b)
                    mm(b5[:, BT - 1:BT], ident, pc("ones", 0, 1))
                    for k, src in enumerate((acum, dt_row[:])):
                        for c in range(C):
                            ins = nc.tensor.transpose(b5[:, (k * C + c) * NH:(k * C + c + 1) * NH],
                                                      src[:, c * P:(c + 1) * P], pc("ident", 0, NH, rows=NH))
                    ins.then_inc(p1["cols_ps"], 1)
                fill(9, 10)
                if before:
                    wait(pe, p1["cols"], b)
                    mm(b5[:, 0:C * NH], pc("last"), cols[:, 0, :, :].rearrange("p c h -> p (c h)")).then_inc(p1["end_ps"], 1)
                fill(10, 11)
                at = 11
                for step in range(C + 3):
                    if before:
                        if step >= 3:
                            chunk_project(a, step - 3)
                        if 0 <= step - 1 < C:
                            chunk_outputs(a, step - 1)
                        if 0 <= step - 2 < C:
                            chunk_turn(a, step - 2)
                        if step < C:
                            chunk_scores(a, step)
                    fill(at, at + CHUNK_FILL[step])
                    at += CHUNK_FILL[step]

            iter1(0, True, False)
            iter1(1, True, True)
            with pe.Fori(2, NB) as b:
                iter1(b, True, True)
            iter1(NB, False, True)

            pe.wait_ge(p1["flo"], NB)
            pe.wait_ge(p1["x2"], C * NB)
            pe.wait_ge(experts_loaded, 32)
            pe.wait_ge(ew1_split, 2)

            def expert_in(a, e):
                n = E * a + e
                wait(pe, p2["h1"], n - 1 if e else n)
                bk = (b4, b5)[e % 2]
                if e == 0:
                    wait(pe, p2["xt_lo"], a + 1)
                mm(bk[:], ew1_16[:, e, 0], xt16[:, 0], start=True, stop=False)
                mm(bk[:], ew1_16[:, e, 1], xt16[:, 0], start=False, stop=False)
                mm(bk[:], ew1_16[:, e, 0], xt16[:, 1], start=False, stop=True).then_inc(p2["w1_ps"], 1)

            def expert_mid(a, e):
                n = E * a + e
                wait(pe, p2["h1"], n + 1)
                wait(pe, p2["h2"], n)
                mm(b6[:], pc("ew2", e * D, (e + 1) * D), h1[e % 2][:]).then_inc(p2["w2_ps"], 1)

            def expert_out(a, e):
                n = E * a + e
                wait(pe, p2["h2"], n + 1)
                wait(pe, p2["acc"], C * n)
                for c in range(C):
                    ins = mm(b7[:, c * D:(c + 1) * D], h2[e % 2][:, c * P:(c + 1) * P], pc("ewo", e * D, (e + 1) * D))
                ins.then_inc(p2["wo_ps"], 1)

            def iter2(b, here, before):
                a = b - 1
                at = 0

                def fill(n):
                    nonlocal at
                    if here:
                        adjacency(2, b, at, at + n, feat, feat16, p2["z_sb"])
                        at += n

                fill(1)
                if before:
                    for l in range(3):
                        wait(pe, p2["z_sb"], b) if l == 0 else wait(pe, p2["h"], 3 * a + l)
                        wait(pe, p2["h"], 3 * a + l)
                        mm(b2[:], pc("mlp1_w", l * D, (l + 1) * D), z_t[:] if l == 0 else hid[l - 1][:]).then_inc(p2["mlp_ps"], 1)
                        fill(1)
                    wait(pe, p2["h"], 3 * b)
                    wait(pe, p2["gb"], a)
                    for c in range(C):
                        ins = mm(b3[:, c * D:(c + 1) * D], hid[2][:, c * P:(c + 1) * P], pc("wm", 0, D))
                    ins.then_inc(p2["mg_ps"], 1)
                    fill(4)
                    wait(pe, ln_norm, 4 * (3 * NB + b))
                    wait(pe, p2["xt_hi"], a)
                    transposes(lambda c: xhat[:, c, :], tr_ps, C, p2["xt_ps"])
                    fill(1)
                    wait(pe, p2["xt_sb"], b)
                    for c in range(C):
                        ins = mm(b3[:, c * E:(c + 1) * E], xhat_t[:, c * P:(c + 1) * P], pc("wr"))
                    ins.then_inc(p2["gl_ps"], 1)
                    fill(1)
                    for e in range(E + 2):
                        if e < E:
                            expert_in(a, e)
                        if 0 <= e - 1 < E:
                            expert_mid(a, e - 1)
                        if e == 2:
                            wait(pe, p2["gate"], b)
                            for c in range(C):
                                ins = nc.tensor.transpose(b3[0:E, c * P:(c + 1) * P], gate[:, c, :], ident)
                            ins.then_inc(p2["gt_ps"], 1)
                        if e == 3:
                            wait(pe, p2["gt_sb"], b)
                            for c in range(C):
                                ins = mm(b3[:, c * D:(c + 1) * D], gate_t[:, c * P:(c + 1) * P], pc("bo", rows=E))
                            ins.then_inc(p2["gb_ps"], 1)
                        if e >= 2:
                            expert_out(a, e - 2)
                        fill(EXPERT_FILL[e])
                else:
                    fill(G - at)
                if here:
                    assert at == G, at

            adjacency(2, 0, EARLY, G, feat, feat16, None)
            iter2(1, True, True)
            with pe.Fori(2, NB) as b:
                iter2(b, True, True)
            iter2(NB, False, True)

        @block.scalar
        def _(act):
            A = nc.scalar.activation
            ew = COL["ew1"][0]
            act.dma_start(x[:, 0:C, :], x_in[:, 0:C, :]).then_inc(x_loaded, 16)
            act.wait_ge(x2_loaded, 32)
            act.dma_start(par[:, 0:ew], par_in[:, 0:ew]).then_inc(par_loaded, 16)
            act.dma_start(x[:, C:, :], x_in[:, C:, :]).then_inc(x_rest_loaded, 16)
            make_hi(act, 0, 0, 0, LEAD)
            act.wait_ge(par_loaded, 16)
            A(a_neg[:, 0:1], pc("a_log", rows=NH), ACT.Exp).then_inc(prep_act, 1)
            def iter0(b, here, before, upcoming):
                if before:
                    if isinstance(b, int) and b == 1:
                        act.wait_ge(prep_dve, 2)
                    wait(act, split_used, block_done(0, b - 1))
                    wait(act, p0["mlp_ps"], 3 * (b - 1))
                    A(z_t[:], acc_ps[:], ACT.Identity, scale=gain[:, 1:2]).then_inc(p0["z_sb"], 1)
                if here:
                    make_hi(act, 0, b, LEAD, 6)
                    wait(act, p0["xt_ps"], b + 1)
                    wait(act, p0["sup_ps"], b)
                    A(xhat_t[:], tr_ps[:], ACT.Copy).then_inc(p0["xt_sb"], 1)
                    make_hi(act, 0, b, 6, 8)
                for l in range(3):
                    if before:
                        wait(act, p0["mlp_ps"], 3 * (b - 1) + l + 1)
                        if l == 2:
                            wait(act, p0["mg_ps"], b - 1)
                        A(hid[l][:], b2[:], ACT.Relu, bias=pc("mlp2_b", l, l + 1)).then_inc(p0["h"], 1)
                    if here and l < 2:
                        make_hi(act, 0, b, 4 * l + 4 + LEAD, 4 * l + 8 + LEAD)
                if before:
                    a = b - 1
                    wait(act, p0["dis"], 5 * a + 5)
                    wait(act, p0["sx"], 2 * a)
                    wait(act, p0["slo"], a)
                    for c in range(C):
                        A(fresh[:, c, :], sup[:, 4 * a + c, :], ACT.Copy, scale=dis[:, ts(4 * a + c, 1)]).then_inc(p0["s32"], 1)
                    wait(act, p0["s32"], 4 * a + 4)
                    A(sup[:, ts(2 * a, GJ), :], fresh[:, 0:GJ, :], ACT.Copy).then_inc(p0["sf"], 1)
                    A(sup16[:, ts(2 * a + 1, GJ), 0, :], fresh[:, GJ:, :], ACT.Copy).then_inc(p0["shi"], 1)
                if upcoming:
                    make_hi(act, *upcoming, 0, LEAD)

            iter0(0, True, False, (0, 1))
            act.dma_start(ew1_stage, par_in[:, ew:ew + E * D].rearrange("p (e d) -> p e d", e=E)).then_inc(experts_loaded, 16)
            act.dma_start(par[:, ew + E * D:], par_in[:, ew + E * D:]).then_inc(experts_loaded, 16)
            iter0(1, True, True, (0, 2))
            with act.Fori(2, NB - 1) as b:
                iter0(b, True, True, (0, b + 1))
            iter0(NB - 1, True, True, (1, 0))
            iter0(NB, False, True, None)

            at = [sum(CHUNK_FILL[:k]) + 11 for k in range(C + 3)]

            def next_halves(a):
                wait(act, ln_norm, 4 * (NB + 2 * a + 2))
                A(feat16[:, ts(a, C), 0, :], fresh[:], ACT.Copy).then_inc(p1["fhi"], 1)

            def iter1(b, here, upcoming):
                a = b - 1

                def hi(lo, hi):
                    make_hi(act, *here, lo, hi)

                wait(act, split_used, block_done(1, a))
                wait(act, p1["zt_ps"], a)
                if isinstance(b, int) and b == 1:
                    wait(act, p0["mlp_ps"], 3 * NB)
                A(z_t[:], acc_ps[:], ACT.Copy).then_inc(p1["z_sb"], 1)
                hi(LEAD, 6)
                if not isinstance(b, int) or b > 1:
                    next_halves(a - 1)
                hi(6, 8)
                wait(act, p1["xt_ps"], b)
                wait(act, p1["zp_ps"], 2 * a)
                if isinstance(b, int) and b == 1:
                    wait(act, p0["sup_ps"], NB)
                A(xhat_t[:], tr_ps[:], ACT.Copy).then_inc(p1["xt_sb"], 1)
                dtb = pc("dt_bias", rows=NH)
                wait(act, p1["proj_ps"], 4 * a + 1)
                wait(act, p1["cols_ps"], a)
                A(dt_row[:], b5[0:NH, :], ACT.Relu, bias=dtb).then_inc(p1["dtact"], 1)
                A(da_row[:], b5[0:NH, :], ACT.Abs, bias=dtb).then_inc(p1["dtact"], 1)
                for k, bk in enumerate((b2, b3, b4)):
                    wait(act, p1["proj_ps"], 4 * a + k + 2)
                    wait(act, p1["carry"], 3 * (a + 1))
                    A(xbc[k][:, TAPS - 1:], bk[:], ACT.Copy).then_inc(p1["xbc"], 1)
                hi(8, 10)
                wait(act, p1["dtact"], 2 * b)
                A(da_row[:], da_row[:], ACT.Exp, scale=-1.0).then_inc(p1["dtexp"], 1)
                wait(act, p1["dtexp"], b)
                A(da_row[:], da_row[:], ACT.Ln, bias=1.0).then_inc(p1["dtln"], 1)
                for k, bk in enumerate((b6, b7)):
                    wait(act, p1["zp_ps"], 2 * a + k + 1)
                    wait(act, p1["y2"], C * a)
                    A(zs[:, 2 * k:2 * k + 2, :].rearrange("p c d -> p (c d)"), bk[:], ACT.Silu).then_inc(p1["zs"], 1)
                hi(10, 12)
                wait(act, p1["y_ps"], C * a)
                wait(act, p1["st_ps"], C * a)
                for k in range(2):
                    wait(act, p1["conv"], 12 * a + 9 + k + 1)
                    A(xs[k][:], conv[k][:, 1, :], ACT.Silu, bias=pc("conv_b", k, k + 1)).then_inc(p1["act"], 1)
                wait(act, p1["conv"], 12 * a + 12)
                cb = pc("conv_b", 2, 3)
                A(bs[:], conv[2][0:DS, 1, :], ACT.Silu, bias=cb[0:DS, :]).then_inc(p1["act"], 1)
                A(cs[:], conv[2][DS:2 * DS, 1, :], ACT.Silu, bias=cb[DS:2 * DS, :]).then_inc(p1["act"], 1)
                wait(act, p1["mid"], b)
                A(rows[32:32 + NH, :], mid[:], ACT.Copy).then_inc(p1["rows"], 1)
                hi(12, at[0] + 2)
                wait(act, p1["dec"], 3 * b)
                A(dece[:], dec[:], ACT.Exp).then_inc(p1["dece"], 1)
                for step in range(C + 2):
                    if step < C:
                        c, n, i = step, C * a + step, step % 2
                        wait(act, p1["xT_ps"], n + 1)
                        wait(act, p1["st_ps"], n - 1)
                        A(xt[i][:], b4[:, 0:DI + DS], ACT.Copy).then_inc(p1["xT"], 1)
                        wait(act, p1["rb_ps"], n + 1)
                        wait(act, p1["y_ps"], n - 1)
                        if c == 0:
                            wait(act, p1["flo"], a)
                            wait(act, p1["fhi"], a)
                        A(decay[i][:].rearrange("p h l -> p (h l)"), b5[:], ACT.Exp).then_inc(p1["ee"], 1)
                    if step >= 2:
                        c, n, i = step - 2, C * a + step - 2, step % 2
                        wait(act, p1["y2"], n + 1)
                        wait(act, p1["ssq"], n)
                        wait(act, p1["o_ps"], n - 1)
                        A(y_t[i][:], y2[i][:], ACT.Square, accum_out=ssq[:, c:c + 1]).then_inc(p1["ssq"], 1)
                        wait(act, p1["yT_ps"], n + 1)
                        wait(act, p1["ssq"], n + 1)
                        A(y_t[i][:], b7[:, 0:DI], ACT.Copy).then_inc(p1["yT"], 1)
                    hi(min(at[step] + 2, G), min(at[step + 1] + 2, G))
                    if step == C:
                        make_hi(act, *upcoming, 0, 2)
                if here != (2, 0):
                    make_hi(act, *upcoming, 2, LEAD)

            make_hi(act, 1, 0, LEAD, G)
            make_hi(act, 1, 1, 0, LEAD)
            act.wait_ge(p1["carry"], 3)
            iter1(1, (1, 1), (1, 2))
            with act.Fori(2, NB - 1) as b:
                iter1(b, (1, b), (1, b + 1))
            iter1(NB - 1, (1, NB - 1), (2, 0))
            iter1(NB, (2, 0), (2, 1))
            next_halves(NB - 1)

            def iter2(b, here, upcoming):
                a = b - 1

                def hi(lo, hi):
                    if here:
                        make_hi(act, 2, b, lo, hi)

                wait(act, split_used, block_done(2, a))
                wait(act, p2["mlp_ps"], 3 * a)
                A(z_t[:], acc_ps[:], ACT.Identity, scale=gain[:, 0:1]).then_inc(p2["z_sb"], 1)
                hi(2, 3)
                for l in range(3):
                    wait(act, p2["mlp_ps"], 3 * a + l + 1)
                    if l == 2:
                        wait(act, p2["mg_ps"], a)
                    A(hid[l][:], b2[:], ACT.Relu, bias=pc("mlp1_b", l, l + 1)).then_inc(p2["h"], 1)
                    hi(3 + l, 4 + l)
                hi(6, 9)
                wait(act, p2["xt_ps"], b)
                wait(act, p2["w1_ps"], E * a)
                A(xhat_t[:], tr_ps[:], ACT.Copy).then_inc(p2["xt_sb"], 1)
                A(xt16[:, 0], tr_ps[:], ACT.Copy).then_inc(p2["xt_hi"], 1)
                hi(9, 11)
                wait(act, p2["sub"], b)
                A(lg[:, 2], lg[:, 1], ACT.Exp).then_inc(p2["ex"], 1)
                for e in range(E + 1):
                    if e < E:
                        n = E * a + e
                        wait(act, p2["w1_ps"], n + 1)
                        wait(act, p2["w2_ps"], n - 1)
                        A(h1[e % 2][:], (b4, b5)[e % 2][:], ACT.Relu, scale=bn_s[:, e:e + 1], bias=bn_f[:, e:e + 1]).then_inc(p2["h1"], 1)
                    hi(min(11 + e, G), min(12 + e, G))
                    if e >= 1:
                        n = E * a + e - 1
                        wait(act, p2["w2_ps"], n + 1)
                        wait(act, p2["wo_ps"], n - 1)
                        A(h2[(e - 1) % 2][:], b6[:], ACT.Relu, scale=bn_s[:, E + e - 1:E + e], bias=bn_f[:, E + e - 1:E + e]).then_inc(p2["h2"], 1)
                    if upcoming and e == E - 1:
                        make_hi(act, *upcoming, 0, 2)

            act.wait_ge(prep_pool, 8)
            iter2(1, True, (2, 2))
            with act.Fori(2, NB - 1) as b:
                iter2(b, True, (2, b + 1))
            iter2(NB - 1, True, None)
            iter2(NB, False, None)

        @block.vector
        def _(dve):
            V = nc.vector

            def norm_stats(n, tile):
                norm_sums(n, tile)
                norm_aggregate(n)

            def norm_sums(n, tile):
                wait(dve, ln_aggr, 4 * n)
                hold(V)
                for c in range(C):
                    V.bn_stats(stats[:, c, :], tile(c)).then_inc(ln_stats, 1)

            def norm_aggregate(n):
                wait(dve, ln_norm, 4 * n)
                wait(dve, ln_stats, 4 * n + 4)
                hold(V)
                for c in range(C):
                    V.bn_aggr(mv[:, c, :], stats[:, c, :]).then_inc(ln_aggr, 1)

            def norm_apply(n, tile, dst):
                wait(dve, ln_rstd, n + 1)
                for c in range(C):
                    V.tensor_scalar(dst(c), tile(c), mv[:, c, 0:1], rstd[:, c:c + 1], ALU.subtract, ALU.mult).then_inc(ln_norm, 1)

            V.memset(neg_half[:], -0.5).then_inc(consts_set, 1)
            V.memset(state[:], 0.0).then_inc(consts_set, 1)
            dve.wait_ge(consts_set, 2)
            dve.wait_ge(x2_odd_loaded, 32)
            odd = feat16.rearrange("p (s e j) k d -> p s e j k d", e=2, j=GJ)[:, :, 1]
            for j in range(GJ):
                V.tensor_copy(odd[:, :, j, 0], x2_stage[:, :, j]).then_inc(x2_split, 1)
            dve.wait_ge(x2_split, 2)
            for j in range(GJ):
                V.tensor_tensor(odd[:, :, j, 1], x2_stage[:, :, j], odd[:, :, j, 0], ALU.subtract).then_inc(x2_split, 1)
            dve.wait_ge(x_loaded, 16)
            norm_stats(0, lambda c: x[:, c, :])
            norm_apply(0, lambda c: x[:, c, :], lambda c: xhat[:, c, :])
            def prepare():
                dve.wait_ge(par_loaded, 16)
                V.tensor_scalar(gain[:, 0:1], pc("eps1"), 1.0, 1.0, ALU.add, ALU.add).then_inc(prep_dve, 1)
                V.tensor_scalar(gain[:, 1:2], pc("eps2"), 1.0, 1.0, ALU.add, ALU.add).then_inc(prep_dve, 1)
                dve.wait_ge(prep_act, 1)
                V.tensor_scalar(a_neg[:, 1:2], a_neg[:, 0:1], -1.0, None, ALU.mult).then_inc(prep_dve, 1)
                for k in range(2):
                    V.tensor_scalar(skip_d[:, k, :], ident, pc("skip", k, k + 1), None, ALU.mult).then_inc(prep_dve, 1)
                dve.wait_ge(prep_pe, 1)
                for k in range(2):
                    V.tensor_scalar(w_ol[:, k, :], b6[:, k * P:(k + 1) * P], pc("norm_w", k, k + 1), None, ALU.mult).then_inc(prep_dve, 1)
                V.memset(rows[:], 0.0).then_inc(rows_set, 1)
                V.tensor_copy(pick[:], pc("pick").unsqueeze(2).broadcast_to([P, NH, P])).then_inc(rows_set, 1)
                V.tensor_scalar(unpick[:], pc("pick").unsqueeze(2).broadcast_to([P, NH, P]), -1.0, None, ALU.mult).then_inc(rows_set, 1)
                V.tensor_copy(ident16[:], ident).then_inc(rows_set, 1)
                V.tensor_copy(barred[:], pc("barred")).then_inc(rows_set, 1)

            def rows4(ap):
                return ap[:].rearrange("p (c d) -> p c d", c=C)

            def bias4(name):
                return pc(name).unsqueeze(1).broadcast_to([P, C, D])

            def iter0(b, here, before, follows):
                if before:
                    wait(dve, p0["deg_ps"], b)
                    wait(dve, p0["dis"], 5 * (b - 1))
                    V.tensor_scalar(deg[:], b5[:, 0:C], 1.0, None, ALU.add).then_inc(p0["deg"], 1)
                if here:
                    for k in range(G // 2):
                        for q in (2 * k, 2 * k + 1):
                            wait(dve, adj_loaded[q % SLOTS], strip_loaded(0, b, q))
                        dst = part[k % 2] if k else pair
                        wait(dve, p0["colsum"], SUMS * b + max(k - 2, 0))
                        s0 = 2 * k % SLOTS
                        V.tensor_tensor(dst, ring[:, s0], ring[:, s0 + 1], ALU.add).then_inc(adj_summed, 1)
                        if k:
                            wait(dve, adj_summed, G // 2 * b + k + 1)
                            wait(dve, p0["colsum"], SUMS * b + k - 1)
                            V.tensor_tensor(pair, pair, part[k % 2], ALU.add).then_inc(p0["colsum"], 1)
                        if k == 1 and follows:
                            if isinstance(b, int) and b == 0:
                                dve.wait_ge(x_rest_loaded, 16)
                            norm_stats(b + 1, lambda c: x[:, 4 * (b + 1) + c, :])
                        if k == 4:
                            wait(dve, p0["sup_ps"], b + 1)
                            V.tensor_tensor(sup[:, ts(b, C), :], rows4(b3), bias4("g0_b"), ALU.add).then_inc(p0["sup"], 1)
                        if k == 6 and follows:
                            wait(dve, p0["xt_ps"], b + 1)
                            norm_apply(b + 1, lambda c: x[:, 4 * (b + 1) + c, :], lambda c: xhat[:, c, :])
                    wait(dve, p0["colsum"], SUMS * b + SUMS - 1)
                    wait(dve, p0["deg_ps"], b)
                    V.tensor_tensor(colsum, pair[:, 0], pair[:, 1], ALU.add).then_inc(p0["colsum"], 1)
                if before:
                    a = b - 1
                    wait(dve, p0["mg_ps"], b)
                    V.tensor_tensor(side[:, ts(a, C), :], rows4(b4), bias4("bm"), ALU.add).then_inc(p0["mg"], 1)
                    wait(dve, p0["shi"], b)
                    odd = ts(2 * a + 1, GJ)
                    V.tensor_tensor(sup16[:, odd, 1, :], fresh[:, GJ:, :], sup16[:, odd, 0, :], ALU.subtract).then_inc(p0["slo"], 1)

            iter0(0, True, False, True)
            prepare()
            iter0(1, True, True, True)
            dve.wait_ge(experts_loaded, 32)
            V.tensor_copy(ew1_16[:, :, 0], ew1_stage).then_inc(ew1_split, 1)
            dve.wait_ge(ew1_split, 1)
            V.tensor_tensor(ew1_16[:, :, 1], ew1_stage, ew1_16[:, :, 0], ALU.subtract).then_inc(ew1_split, 1)
            with dve.Fori(2, NB - 1) as b:
                iter0(b, True, True, True)
            iter0(NB - 1, True, True, False)
            iter0(NB, False, True, False)

            for k in range(3):
                V.memset(xbc[k][:, 0:TAPS - 1], 0.0).then_inc(p1["carry"], 1)

            def next_halves(a):
                wait(dve, ln_norm, 4 * (NB + 2 * a + 2))
                wait(dve, p1["fhi"], a + 1)
                V.tensor_tensor(feat16[:, ts(a, C), 1, :], fresh[:], feat16[:, ts(a, C), 0, :], ALU.subtract).then_inc(p1["flo"], 1)

            def iter1(b, here, upcoming):
                a = b - 1
                t0 = 4 * a

                def lo(q0, q1):
                    make_lo(dve, "V", *here, q0, q1)

                late = not isinstance(b, int) or b > 1
                if late:
                    wait(dve, p1["x2"], C * a)
                    norm_stats(NB + 2 * a - 1, lambda c: x[:, t0 - C + c, :])
                wait(dve, p1["zt_ps"], a + 1)
                if isinstance(a, int) and a == 0:
                    dve.wait_ge(p0["sx"], 2 * NB)
                for c in range(C):
                    V.scalar_tensor_tensor(out=x[:, t0 + c, :], in0=b7[:, c * P:(c + 1) * P], scalar=dis[:, ts(t0 + c, 1)],
                                           in1=x[:, t0 + c, :], op0=ALU.mult, op1=ALU.add).then_inc(p1["x1"], 1)
                wait(dve, p1["x1"], 4 * a + 4)
                n = NB + 2 * a
                norm_sums(n, lambda c: x[:, t0 + c, :])
                if late:
                    norm_apply(n - 1, lambda c: x[:, t0 - C + c, :], lambda c: fresh[:, c, :])
                norm_aggregate(n)
                lo(2, 5)
                norm_apply(n, lambda c: x[:, t0 + c, :], lambda c: xhat[:, c, :])
                if late:
                    next_halves(a - 1)
                lo(5, 6)
                for j in range(TAPS):
                    for k in range(3):
                        wait(dve, p1["xbc"], 3 * a + k + 1)
                        w = pc("conv_w", k * TAPS + j, k * TAPS + j + 1)
                        src = xbc[k][:, j:j + BT]
                        if j == 0:
                            wait(dve, p1["conv"], 12 * a)
                            wait(dve, p1["act"], 4 * a)
                            V.tensor_scalar(conv[k][:, 0, :], src, w, None, ALU.mult).then_inc(p1["conv"], 1)
                        else:
                            wait(dve, p1["conv"], 12 * a + 3 * (j - 1) + k + 1)
                            V.scalar_tensor_tensor(out=conv[k][:, j % 2, :], in0=src, scalar=w, in1=conv[k][:, (j - 1) % 2, :],
                                                   op0=ALU.mult, op1=ALU.add).then_inc(p1["conv"], 1)
                    if j == 1:
                        wait(dve, p1["dtln"], a + 1)
                        wait(dve, p1["cols_ps"], a)
                        V.tensor_tensor(dt_row[:], dt_row[:], da_row[:], ALU.add).then_inc(p1["dtrow"], 1)
                        wait(dve, p1["dtrow"], 2 * a + 1)
                        V.tensor_scalar(da_row[:], dt_row[:], a_neg[:, 1:2], None, ALU.mult).then_inc(p1["dtrow"], 1)
                        wait(dve, p1["dtrow"], 2 * a + 2)
                        for c in range(C):
                            cc = slice(c * P, (c + 1) * P)
                            V.tensor_tensor_scan(acum[:, cc], pc("ones", rows=NH), da_row[:, cc], 0.0, ALU.mult, ALU.add).then_inc(p1["scan"], 1)
                    if j == 2:
                        lo(6, 9)
                        wait(dve, p1["cols_ps"], a + 1)
                        wait(dve, p1["xdt"], C * a)
                        V.tensor_copy(cols[:].rearrange("p k c h -> p (k c h)"), b5[:, 0:2 * C * NH]).then_inc(p1["cols"], 1)
                wait(dve, p1["conv"], 12 * a + 12)
                for k in range(3):
                    V.tensor_copy(xbc[k][:, 0:TAPS - 1], xbc[k][:, BT:BT + TAPS - 1]).then_inc(p1["carry"], 1)
                wait(dve, p1["scan"], C * a + C)
                wait(dve, p1["rb_ps"], C * a)
                V.tensor_copy(rows[0:NH, :], acum).then_inc(p1["rows"], 1)
                wait(dve, p1["rows"], 3 * a + 1)
                V.tensor_tensor(da_row[:], acum, rows[0:NH, :], ALU.subtract).then_inc(p1["rest"], 1)
                wait(dve, p1["rest"], a + 1)
                V.tensor_copy(mid[:], da_row[:]).then_inc(p1["mid"], 1)
                wait(dve, p1["mid"], a + 1)
                V.tensor_tensor(rows[64:64 + NH, :], da_row[:], mid[:], ALU.subtract).then_inc(p1["rows"], 1)
                lo(9, 10)
                wait(dve, p1["end_ps"], a + 1)
                wait(dve, p1["cols"], a + 1)
                wait(dve, p1["dece"], a)
                ac = cols[:, 0].rearrange("p c h -> p (c h)")
                V.tensor_tensor(dec[:, 0, :], b5[:, 0:C * NH], ac, ALU.subtract).then_inc(p1["dec"], 1)
                V.tensor_copy(dec[:, 1, :], ac).then_inc(p1["dec"], 1)
                V.tensor_copy(dec[:, 2, :], b5[:, 0:C * NH]).then_inc(p1["dec"], 1)

                lo(10, 12)

                def heads(ap, n):
                    return ap.unsqueeze(2).broadcast_to([ap.shape[0], NH, n])

                for step in range(C + 3):
                    if 1 <= step <= C:
                        c, n, i = step - 1, C * a + step - 1, (step - 1) % 2
                        wait(dve, p1["y_ps"], n + 1)
                        wait(dve, p1["dece"], a + 1)
                        wait(dve, p1["y2"], n - 1)
                        V.tensor_tensor(y[i][:].rearrange("p (h d) -> p h d", h=NH), b6[:, DI:2 * DI].rearrange("p (h d) -> p h d", h=NH),
                                        heads(dece[:, 1, c * NH:(c + 1) * NH], HD), ALU.mult).then_inc(p1["y0"], 1)
                        wait(dve, p1["st"], n)
                        st = state[:].rearrange("p (h d) -> p h d", h=NH)
                        V.tensor_tensor(st, st, heads(dece[0:DS, 2, c * NH:(c + 1) * NH], HD), ALU.mult).then_inc(p1["stmul"], 1)
                        wait(dve, p1["y0"], n + 1)
                        V.tensor_tensor(y[i][:], b6[:, 0:DI], y[i][:], ALU.add).then_inc(p1["y"], 1)
                        wait(dve, p1["stmul"], n + 1)
                        wait(dve, p1["st_ps"], n + 1)
                        V.tensor_tensor(state[:], state[:], b3[0:DS, 0:DI], ALU.add).then_inc(p1["st"], 1)
                    if step < C:
                        c, n, i = step, C * a + step, step % 2
                        wait(dve, p1["ee"], n + 1)
                        wait(dve, p1["gt_ps"], n + 1)
                        V.tensor_tensor(decay[i][:], decay[i][:], b2[:, 0:P].unsqueeze(1).broadcast_to([P, NH, P]), ALU.mult).then_inc(p1["m"], 1)
                    if step == C + 2:
                        make_lo(dve, "V", *upcoming, 0, 2)
                    if step >= 3:
                        c, n = step - 3, C * a + step - 3
                        wait(dve, p1["o_ps"], n + 1)
                        wait(dve, p1["rms"], n + 1)
                        wait(dve, p1["x1b"], a + 1)
                        V.scalar_tensor_tensor(out=x[:, t0 + c, :], in0=tr_ps[:, 0:D], scalar=rms[:, c:c + 1], in1=x[:, t0 + c, :],
                                               op0=ALU.mult, op1=ALU.add).then_inc(p1["x2"], 1)
                    if step == 1:
                        lo(12, 14)
                    if step == 3:
                        lo(14, G)

            make_lo(dve, "V", 1, 0, 0, G)
            make_lo(dve, "V", 1, 1, 0, 2)
            iter1(1, (1, 1), (1, 2))
            with dve.Fori(2, NB - 1) as b:
                iter1(b, (1, b), (1, b + 1))
            iter1(NB - 1, (1, NB - 1), (2, 0))
            iter1(NB, (2, 0), (2, 1))
            n = 3 * NB - 1
            dve.wait_ge(p1["x2"], C * NB)
            norm_stats(n, lambda c: x[:, NT - C + c, :])
            norm_apply(n, lambda c: x[:, NT - C + c, :], lambda c: fresh[:, c, :])
            next_halves(NB - 1)

            def iter2(b, here, upcoming):
                a = b - 1
                t0 = 4 * a

                def lo(q0, q1):
                    if here:
                        make_lo(dve, "V", 2, b, q0, q1)

                lo(2, 6)
                xb = x[:, ts(a, C), :]
                wait(dve, p2["mg_ps"], b)
                wait(dve, p2["xm"], b)
                V.tensor_tensor(xb, rows4(b3), xb, ALU.add).then_inc(p2["x3"], 1)
                wait(dve, p2["x3"], b)
                n = 3 * NB + a
                norm_stats(n, lambda c: x[:, t0 + c, :])
                lo(6, 8)
                norm_apply(n, lambda c: x[:, t0 + c, :], lambda c: xhat[:, c, :])
                wait(dve, p2["xt_sb"], b)
                wait(dve, p2["xt_hi"], b)
                V.tensor_tensor(xt16[:, 1], xhat_t[:], xt16[:, 0], ALU.subtract).then_inc(p2["xt_lo"], 1)
                lo(8, 10)
                wait(dve, p2["gl_ps"], b)
                wait(dve, p2["gt_ps"], a)
                V.tensor_tensor(lg[:, 0], b3[:, 0:C * E].rearrange("p (c e) -> p c e", c=C),
                                pc("br").unsqueeze(1).broadcast_to([P, C, E]), ALU.add).then_inc(p2["lg"], 1)
                wait(dve, p2["lg"], b)
                V.tensor_reduce(red[:, 0, :], lg[:, 0], AX_X, ALU.max).then_inc(p2["mx"], 1)
                wait(dve, p2["mx"], b)
                V.tensor_tensor(lg[:, 1], lg[:, 0], red[:, 0, :].unsqueeze(2).broadcast_to([P, C, E]), ALU.subtract).then_inc(p2["sub"], 1)
                wait(dve, p2["ex"], b)
                V.tensor_reduce(red[:, 1, :], lg[:, 2], AX_X, ALU.add).then_inc(p2["sum"], 1)
                wait(dve, p2["sum"], b)
                V.reciprocal(red[:, 2, :], red[:, 1, :]).then_inc(p2["rcp"], 1)
                wait(dve, p2["rcp"], b)
                wait(dve, p2["acc"], C * E * a)
                V.tensor_tensor(gate[:], lg[:, 2], red[:, 2, :].unsqueeze(2).broadcast_to([P, C, E]), ALU.mult).then_inc(p2["gate"], 1)
                lo(10, 12)
                wait(dve, p2["gate"], b)
                for e in range(E):
                    lo(min(12 + e, G), min(13 + e, G))
                    if upcoming and e == E - 1:
                        make_lo(dve, "V", *upcoming, 0, 2)
                    wait(dve, p2["wo_ps"], E * a + e + 1)
                    for c in range(C):
                        if e:
                            wait(dve, p2["acc"], C * (E * a + e - 1) + c + 1)
                        if e == 2:
                            wait(dve, p2["gb"], b)
                        V.scalar_tensor_tensor(out=x[:, t0 + c, :], in0=b7[:, c * D:(c + 1) * D], scalar=gate[:, c, e:e + 1],
                                               in1=x[:, t0 + c, :], op0=ALU.mult, op1=ALU.add).then_inc(p2["acc"], 1)
                    if e == 0:
                        wait(dve, p2["gt_ps"], b)
                        V.tensor_copy(gate_t[:], b3[0:E, :]).then_inc(p2["gt_sb"], 1)
                    if e == 1:
                        wait(dve, p2["gb_ps"], b)
                        wait(dve, p2["acc"], C * (E * a + 2))
                        V.tensor_tensor(xb, rows4(b3), xb, ALU.add).then_inc(p2["gb"], 1)


            iter2(1, True, (2, 2))
            with dve.Fori(2, NB - 1) as b:
                iter2(b, True, (2, b + 1))
            iter2(NB - 1, True, None)
            iter2(NB, False, None)

        @block.gpsimd
        def _(pool):
            Q = nc.gpsimd

            def norm_rstd(n):
                wait(pool, ln_aggr, 4 * n + 4)
                wait(pool, ln_rstd, n)
                hold(Q)
                Q.tensor_scalar(var[:], mv[:, :, 1], LN_EPS, None, ALU.add).then_inc(ln_var, 1)
                wait(pool, ln_var, n + 1)
                Q.tensor_tensor(rstd[:], var[:], neg_half[:, 0:C], ALU.pow).then_inc(ln_rstd, 1)

            pool.wait_ge(consts_set, 1)
            norm_rstd(0)
            def batch_norm():
                pool.wait_ge(par_loaded, 16)
                for k, (v, g, m, bb, be) in enumerate((("v1", "g1", "m1", "b1", "be1"), ("v2", "g2", "m2", "b2", "be2"))):
                    s = slice(k * E, (k + 1) * E)
                    base = 5 * k
                    Q.tensor_scalar(bn_t[:, 0, s], pc(v), BN_EPS, None, ALU.add).then_inc(prep_pool, 1)
                    pool.wait_ge(prep_pool, base + 1)
                    Q.tensor_tensor(bn_t[:, 1, s], bn_t[:, 0, s], neg_half[:, s], ALU.pow).then_inc(prep_pool, 1)
                    Q.tensor_tensor(bn_t[:, 2, s], pc(bb), pc(m), ALU.subtract).then_inc(prep_pool, 1)
                    pool.wait_ge(prep_pool, base + 3)
                    Q.tensor_tensor(bn_s[:, s], pc(g), bn_t[:, 1, s], ALU.mult).then_inc(prep_pool, 1)
                    pool.wait_ge(prep_pool, base + 4)
                    Q.tensor_tensor(bn_f[:, s], bn_t[:, 2, s], bn_s[:, s], ALU.mult).then_inc(prep_pool, 1)
                pool.wait_ge(prep_pool, 10)
                for k, be in enumerate(("be1", "be2")):
                    s = slice(k * E, (k + 1) * E)
                    Q.tensor_tensor(bn_f[:, s], bn_f[:, s], pc(be), ALU.add).then_inc(prep_pool, 1)

            def degrees(a):
                wait(pool, p0["deg"], a + 1)
                d = p0["dis"]
                hold(Q)
                Q.tensor_scalar(dg[:, 0, :], deg[:], 0.0, None, ALU.is_equal).then_inc(d, 1)
                wait(pool, d, 5 * a + 1)
                Q.tensor_tensor(dg[:, 1, :], deg[:], dg[:, 0, :], ALU.add).then_inc(d, 1)
                Q.tensor_scalar(dg[:, 3, :], dg[:, 0, :], -1.0, 1.0, ALU.mult, ALU.add).then_inc(d, 1)
                wait(pool, d, 5 * a + 3)
                Q.tensor_tensor(dg[:, 2, :], dg[:, 1, :], neg_half[:, 0:C], ALU.pow).then_inc(d, 1)
                wait(pool, d, 5 * a + 4)
                Q.tensor_tensor(dis[:, ts(a, C)], dg[:, 2, :], dg[:, 3, :], ALU.mult).then_inc(d, 1)

            def own_share(a):
                tb = ts(a, C)
                wait(pool, p0["s32"], 4 * a + 4)
                wait(pool, p0["sx"], 2 * a)
                hold(Q)
                Q.tensor_tensor(decay[1][:], fresh[:], dis[:, tb].unsqueeze(2).broadcast_to([P, C, D]), ALU.mult).then_inc(p0["sx"], 1)
                wait(pool, p0["sx"], 2 * a + 1)
                hold(Q)
                Q.tensor_tensor(x[:, tb, :], x[:, tb, :], decay[1][:], ALU.add).then_inc(p0["sx"], 1)

            def iter0(b, before, upcoming, norm):
                if before:
                    degrees(b - 1)
                make_lo(pool, "Q", 0, b, LEAD, 8)
                if norm:
                    norm_rstd(b + 1)
                make_lo(pool, "Q", 0, b, 8, G)
                if before:
                    own_share(b - 1)
                if upcoming:
                    make_lo(pool, "Q", *upcoming, 0, LEAD)

            make_lo(pool, "Q", 0, 0, 0, LEAD)
            iter0(0, False, (0, 1), True)
            batch_norm()
            iter0(1, True, (0, 2), True)
            with pool.Fori(2, NB - 1) as b:
                iter0(b, True, (0, b + 1), True)
            iter0(NB - 1, True, None, False)
            degrees(NB - 1)
            own_share(NB - 1)

            def iter1(b, here, upcoming):
                a = b - 1
                if not isinstance(b, int) or b > 1:
                    norm_rstd(NB + 2 * a - 1)
                norm_rstd(NB + 2 * a)
                make_lo(pool, "Q", *here, LEAD, 8)
                tb = ts(a, C)
                wait(pool, ln_norm, 4 * (NB + 2 * a + 1))
                hold(Q)
                Q.tensor_tensor(x[:, tb, :], x[:, tb, :], pc("b_lin").unsqueeze(1).broadcast_to([P, C, D]), ALU.add).then_inc(p1["x1b"], 1)
                make_lo(pool, "Q", *here, 8, 12)
                for step in range(C + 2):
                    if step < C:
                        c, n, i = step, C * a + step, step % 2
                        wait(pool, p1["xT"], n + 1)
                        wait(pool, p1["cols"], a + 1)
                        wait(pool, p1["y_ps"], n - 1)
                        h3 = lambda ap: ap.rearrange("p (h d) -> p h d", h=NH)
                        Q.tensor_tensor(h3(xdt[i][:]), h3(xt[i][:, 0:DI]), cols[:, 1, c, :].unsqueeze(2).broadcast_to([P, NH, HD]),
                                        ALU.mult).then_inc(p1["xdt"], 1)
                        wait(pool, p1["xdt"], n + 1)
                        wait(pool, p1["dece"], a + 1)
                        wait(pool, p1["st_ps"], n - 1)
                        Q.tensor_tensor(h3(xdd[i][:]), h3(xdt[i][:]), dece[:, 0, c * NH:(c + 1) * NH].unsqueeze(2).broadcast_to([P, NH, HD]),
                                        ALU.mult).then_inc(p1["xdd"], 1)
                    if 1 <= step <= C:
                        c, n, i = step - 1, C * a + step - 1, (step - 1) % 2
                        wait(pool, p1["y"], n + 1)
                        wait(pool, p1["zs"], 2 * a + 2)
                        wait(pool, p1["yT_ps"], n - 1)
                        wait(pool, p1["ssq"], n - 1)
                        Q.tensor_tensor(y2[i][:], y[i][:], zs[:, c, :], ALU.mult).then_inc(p1["y2"], 1)
                    if step >= 2:
                        c, n = step - 2, C * a + step - 2
                        wait(pool, p1["ssq"], n + 1)
                        wait(pool, p1["rms"], n)
                        hold(Q)
                        Q.tensor_scalar(msq[:, c:c + 1], ssq[:, c:c + 1], 1.0 / DI, RMS_EPS, ALU.mult, ALU.add).then_inc(p1["rv"], 1)
                        wait(pool, p1["rv"], n + 1)
                        wait(pool, p1["x2"], C * a)
                        Q.tensor_tensor(rms[:, c:c + 1], msq[:, c:c + 1], neg_half[:, 0:1], ALU.pow).then_inc(p1["rms"], 1)
                if upcoming:
                    make_lo(pool, "Q", *upcoming, 0, LEAD)

            make_lo(pool, "Q", 1, 0, 0, G)
            make_lo(pool, "Q", 1, 1, 0, LEAD)
            iter1(1, (1, 1), (1, 2))
            with pool.Fori(2, NB - 1) as b:
                iter1(b, (1, b), (1, b + 1))
            iter1(NB - 1, (1, NB - 1), (2, 0))
            iter1(NB, (2, 0), None)
            norm_rstd(3 * NB - 1)
            make_lo(pool, "Q", 2, 0, 12, G)
            make_lo(pool, "Q", 2, 1, 0, LEAD)

            def iter2(b, here, upcoming):
                a = b - 1

                def lo(q0, q1):
                    if here:
                        make_lo(pool, "Q", 2, b, q0, q1)

                tb = ts(a, C)
                hold(Q)
                Q.tensor_tensor(x[:, tb, :], x[:, tb, :], side[:, tb, :], ALU.add).then_inc(p2["xm"], 1)
                lo(LEAD, 8)
                norm_rstd(3 * NB + a)
                lo(8, G)
                if upcoming:
                    make_lo(pool, "Q", *upcoming, 0, LEAD)
                wait(pool, p2["acc"], C * E * (a + 1))
                pool.dma_start(out[a], x[:, tb, :]).then_inc(out_stored, 16)

            pool.wait_ge(p0["mg"], NB)
            pool.wait_ge(ln_norm, 4 * 3 * NB)
            iter2(1, True, (2, 2))
            with pool.Fori(2, NB - 1) as b:
                iter2(b, True, (2, b + 1))
            iter2(NB - 1, True, None)
            iter2(NB, False, None)
            pool.wait_ge(out_stored, 16 * NB)


def kernel(**inputs):
    import numpy as np
    import concourse.bacc as bacc
    from concourse.bass_utils import run_bass_kernel_spmd

    v = {k: np.asarray(a) for k, a in inputs.items()}
    adj = np.ascontiguousarray(v["adj"].reshape(NB, BT, G, GJ, P).transpose(0, 2, 4, 3, 1))

    par = np.zeros((P, PARAMS), np.float32)

    def put(name, a, rows=P):
        lo, hi = COL[name]
        par[0:rows, lo:hi] = a

    idx = np.arange(P)
    put("ident", np.eye(P))
    put("barred", np.where(idx[None, :] >= idx[:, None], 0.0, -1e30))
    put("last", np.broadcast_to((idx == P - 1)[:, None], (P, P)))
    put("ones", np.ones((P, P)))
    for part in range(3):
        par[32 * part:32 * part + NH, slice(*COL["pick"])] = np.eye(NH)
    put("g0_b", np.broadcast_to(v["L0_gnn_b"], (P, D)))
    put("bm", np.broadcast_to(v["L1_gnn_bm"], (P, D)))
    put("b_lin", np.broadcast_to(v["L0_ffn_b_lin"], (P, D)))
    put("br", np.broadcast_to(v["L1_ffn_br"], (P, E)))
    put("conv_w", v["L0_ffn_conv_w"].reshape(3, P, TAPS).transpose(1, 0, 2).reshape(P, 3 * TAPS))
    put("conv_b", v["L0_ffn_conv_b"].reshape(3, P).T)
    put("skip", np.repeat(v["L0_ffn_D"], HD).reshape(2, P).T)
    put("norm_w", v["L0_ffn_norm_w"].reshape(2, P).T)
    put("eps1", np.broadcast_to(v["L1_gnn_eps1"], (P, 1)))
    put("eps2", np.broadcast_to(v["L1_gnn_eps2"], (P, 1)))
    put("mlp1_b", v["L1_gnn_b1"].T)
    put("mlp2_b", v["L1_gnn_b2"].T)
    for name in ("g1", "be1", "m1", "v1", "b1", "g2", "be2", "m2", "v2", "b2"):
        put(name, v["L1_ffn_" + name].T)
    put("a_log", v["L0_ffn_A_log"][:, None], NH)
    put("dt_bias", v["L0_ffn_dt_bias"][:, None], NH)
    put("bo", v["L1_ffn_bo"], E)
    put("g0_w", v["L0_gnn_W"].T)
    put("w_in", v["L0_ffn_W_in"])
    put("w_out_t", v["L0_ffn_W_out"].T)
    put("w_lin", v["L0_ffn_W_lin"])
    put("mlp1_w", v["L1_gnn_W1"].transpose(2, 0, 1).reshape(D, 3 * D))
    put("mlp2_w", v["L1_gnn_W2"].transpose(2, 0, 1).reshape(D, 3 * D))
    put("wm", v["L1_gnn_Wm"].reshape(D, 2, D).transpose(2, 1, 0).reshape(D, 2 * D))
    put("wr", v["L1_ffn_Wr"])
    put("ew1", v["L1_ffn_W1"].transpose(1, 0, 2).reshape(D, E * D))
    put("ew2", v["L1_ffn_W2"].transpose(1, 0, 2).reshape(D, E * D))
    put("ewo", v["L1_ffn_Wo"].transpose(1, 0, 2).reshape(D, E * D))

    x = np.ascontiguousarray(v["x"].reshape(NT, P, D).transpose(1, 0, 2))
    x2 = np.ascontiguousarray(v["L1_gnn_x2"].reshape(G // 2, 2, GJ, P, D).transpose(1, 2, 3, 0, 4))
    arrays = {"x_dram": x, "x2_dram": x2,
              "adj_dram": adj, "par_dram": par}
    nc = bacc.Bacc("TRN2", target_bir_lowering=False, num_devices=1)
    args = [nc.dram_tensor(n, a.shape, mybir.dt.from_np(a.dtype), kind="ExternalInput").ap() for n, a in arrays.items()]
    res = nc.dram_tensor("out_dram", (NB, P, C, D), F32, kind="ExternalOutput").ap()
    build(nc, *args, res)
    r = run_bass_kernel_spmd(nc, [arrays], core_ids=[0])
    return np.ascontiguousarray(r.results[0]["out_dram"].transpose(0, 2, 1, 3).reshape(T, D))
```
